# Optimizing a Trainium2 kernel written in Bass

```python
import numpy as np
import jax
import jax.numpy as jnp

def _softmax(x, axis=-1):
    return jax.nn.softmax(x, axis=axis)

def _gelu(x):
    return jax.nn.gelu(x, approximate=True)

def _silu(x):
    return jax.nn.silu(x)

def _sigmoid(x):
    return jax.nn.sigmoid(x)

def _layernorm(x, axis=-1, eps=1e-05):
    m = jnp.mean(x, axis=axis, keepdims=True)
    v = jnp.var(x, axis=axis, keepdims=True)
    return (x - m) / jnp.sqrt(v + eps)

def _scatter_add(tgt, idx, src, axis=0):
    return tgt.at[idx].add(src)

def _segment_sum(src, seg, n):
    return jax.ops.segment_sum(src, seg, n)
kernel_name = 'mk_vit_tower_cls_d1_tok_img256_r4_8c94d3'

def setup_inputs(seed: int=0):
    np.random.seed(seed)
    _w = jnp.asarray

    def _rec_inputs():
        import jax
        import jax.numpy as jnp
        _rk = jax.random.key(seed)
        x = -0.000202321 + 1.00025 * jax.random.normal(jax.random.fold_in(_rk, 1), (8, 64, 56, 56), jnp.float32)
        cls_tok = 0.02 * jax.random.normal(jax.random.fold_in(_rk, 5), (1, 1, 64), jnp.float32)
        return (x, cls_tok)
    x, cls_tok = _rec_inputs()

    def _L0_tok_setup():
        import jax, jax.numpy as jnp
        import numpy as np
        B, C, H, W = (8, 64, 56, 56)
        K = 3

        def _unfold3x3(x):
            b, c, h, w = x.shape
            xp = jnp.pad(x, ((0, 0), (0, 0), (1, 1), (1, 1)))
            patches = jnp.stack([xp[:, :, i:i + h, j:j + w] for i in range(K) for j in range(K)], axis=2)
            return patches.reshape(b, c * K * K, h * w).transpose(0, 2, 1)
        key = jax.random.key(seed)
        ks = jax.random.split(key, 8)
        d = C * K * K
        s1 = 1.0 / np.sqrt(d)
        s2 = 1.0 / np.sqrt(C)
        return {'x': jax.random.normal(ks[0], (B, C, H, W), jnp.float32), 'W1': jax.random.uniform(ks[1], (d, C), jnp.float32, -s1, s1), 'b1': jax.random.uniform(ks[2], (C,), jnp.float32, -s1, s1), 'W2': jax.random.uniform(ks[3], (C, d), jnp.float32, -s2, s2), 'b2': jax.random.uniform(ks[4], (d,), jnp.float32, -s2, s2), 'W3': jax.random.uniform(ks[5], (d, C), jnp.float32, -s1, s1), 'b3': jax.random.uniform(ks[6], (C,), jnp.float32, -s1, s1)}
    _L0_tok_all = _L0_tok_setup()
    _L0_tok_in = {k: v for k, v in _L0_tok_all.items() if k in ('W1', 'b1', 'W2', 'b2', 'W3', 'b3')}
    del _L0_tok_all

    def _L0_attn_setup():
        import jax, jax.numpy as jnp
        import numpy as np
        D_MODEL = 64
        D_STATE = 16
        D_CONV = 4
        EXPAND = 2
        D_INNER = EXPAND * D_MODEL
        DT_RANK = (D_MODEL + 15) // 16
        B_SZ = 4
        SEQ = 1024

        def _mamba_params(key, prefix):
            ks = jax.random.split(key, 6)
            s = 0.02
            return {f'{prefix}_in_w': jax.random.normal(ks[0], (2 * D_INNER, D_MODEL), dtype=jnp.float32) * s, f'{prefix}_conv_w': jax.random.normal(ks[1], (D_INNER, D_CONV), dtype=jnp.float32) * s, f'{prefix}_conv_b': jnp.zeros((D_INNER,), dtype=jnp.float32), f'{prefix}_xproj_w': jax.random.normal(ks[2], (DT_RANK + 2 * D_STATE, D_INNER), dtype=jnp.float32) * s, f'{prefix}_dt_w': jax.random.normal(ks[3], (D_INNER, DT_RANK), dtype=jnp.float32) * s, f'{prefix}_dt_b': jax.random.normal(ks[4], (D_INNER,), dtype=jnp.float32) * s, f'{prefix}_A_log': jnp.log(jnp.tile(jnp.arange(1, D_STATE + 1, dtype=jnp.float32), (D_INNER, 1))), f'{prefix}_D': jnp.ones((D_INNER,), dtype=jnp.float32), f'{prefix}_out_w': jax.random.normal(ks[5], (D_MODEL, D_INNER), dtype=jnp.float32) * s}

        def _mamba(x, in_w, conv_w, conv_b, xproj_w, dt_w, dt_b, A_log, D_param, out_w):
            Bn, L, _ = x.shape
            xz = x @ in_w.T
            xin, z = jnp.split(xz, 2, axis=-1)
            lhs = xin.swapaxes(1, 2)
            rhs = conv_w[:, None, :]
            conv = jax.lax.conv_general_dilated(lhs, rhs, (1,), [(D_CONV - 1, 0)], dimension_numbers=('NCL', 'OIL', 'NCL'), feature_group_count=D_INNER)
            xc = jax.nn.silu(conv.swapaxes(1, 2) + conv_b)
            x_dbl = xc @ xproj_w.T
            dt_low = x_dbl[..., :DT_RANK]
            Bm = x_dbl[..., DT_RANK:DT_RANK + D_STATE]
            Cm = x_dbl[..., DT_RANK + D_STATE:]
            dt = jax.nn.softplus(dt_low @ dt_w.T + dt_b)
            A = -jnp.exp(A_log)

            def step(h, inps):
                dt_t, B_t, C_t, u_t = inps
                dA = jnp.exp(dt_t[:, :, None] * A)
                h = dA * h + dt_t[:, :, None] * B_t[:, None, :] * u_t[:, :, None]
                y = jnp.einsum('bdn,bn->bd', h, C_t)
                return (h, y)
            h0 = jnp.zeros((Bn, D_INNER, D_STATE), dtype=x.dtype)
            xs = (dt.swapaxes(0, 1), Bm.swapaxes(0, 1), Cm.swapaxes(0, 1), xc.swapaxes(0, 1))
            _, ys = jax.lax.scan(step, h0, xs)
            y = ys.swapaxes(0, 1) + D_param * xc
            y = y * jax.nn.silu(z)
            return y @ out_w.T
        key = jax.random.key(seed)
        k1, k2, k3 = jax.random.split(key, 3)
        inp = {'g_data': jax.random.normal(k1, (B_SZ, SEQ, D_MODEL), dtype=jnp.float32)}
        inp.update(_mamba_params(k2, 'f'))
        inp.update(_mamba_params(k3, 'b'))
        return inp
    _L0_attn_all = _L0_attn_setup()
    _L0_attn_in = {k: v for k, v in _L0_attn_all.items() if k in ('f_in_w', 'f_conv_w', 'f_conv_b', 'f_xproj_w', 'f_dt_w', 'f_dt_b', 'f_A_log', 'f_D', 'f_out_w', 'b_in_w', 'b_conv_w', 'b_conv_b', 'b_xproj_w', 'b_dt_w', 'b_dt_b', 'b_A_log', 'b_D', 'b_out_w')}
    del _L0_attn_all

    def _L0_ffn_setup():
        import jax, jax.numpy as jnp
        import numpy as np
        B, T, C = (64, 96, 64)
        NH, NKV = (4, 2)
        HD = C // NH
        NREP = NH // NKV
        NE, TOPK = (8, 2)
        HID = int(8 / 3 * C)
        EPS_RMS = 1e-06

        def _rope_tables(t_len):
            inv_freq = 1.0 / 10000.0 ** (np.arange(0, HD, 2, dtype=np.float32) / HD)
            t = np.arange(t_len, dtype=np.float32)
            freqs = np.outer(t, inv_freq)
            emb = np.concatenate([freqs, freqs], axis=-1)
            return (jnp.asarray(np.cos(emb)), jnp.asarray(np.sin(emb)))

        def _rotate_half(x):
            h = x.shape[-1] // 2
            return jnp.concatenate([-x[..., h:], x[..., :h]], axis=-1)

        def _rmsnorm(v, w):
            return v * jax.lax.rsqrt(jnp.mean(v * v, axis=-1, keepdims=True) + EPS_RMS) * w
        key = jax.random.key(seed)
        ks = jax.random.split(key, 10)
        s = lambda k, shape: jax.random.normal(k, shape, jnp.float32) * 0.02
        return {'x': jax.random.normal(ks[0], (B, T, C), jnp.float32), 'ln1_w': jnp.ones((C,), jnp.float32), 'ln2_w': jnp.ones((C,), jnp.float32), 'wq': s(ks[1], (NH * HD, C)), 'wk': s(ks[2], (NKV * HD, C)), 'wv': s(ks[3], (NKV * HD, C)), 'wo': s(ks[4], (C, C)), 'router_w': s(ks[5], (NE, C)), 'w1': s(ks[6], (NE, HID, C)), 'w2': s(ks[7], (NE, C, HID)), 'w3': s(ks[8], (NE, HID, C))}
    _L0_ffn_all = _L0_ffn_setup()
    _L0_ffn_in = {k: v for k, v in _L0_ffn_all.items() if k in ('ln1_w', 'ln2_w', 'wq', 'wk', 'wv', 'wo', 'router_w', 'w1', 'w2', 'w3')}
    del _L0_ffn_all
    return {'x': x, 'cls_tok': cls_tok, 'L0_tok_W1': _L0_tok_in['W1'], 'L0_tok_b1': _L0_tok_in['b1'], 'L0_tok_W2': _L0_tok_in['W2'], 'L0_tok_b2': _L0_tok_in['b2'], 'L0_tok_W3': _L0_tok_in['W3'], 'L0_tok_b3': _L0_tok_in['b3'], 'L0_attn_f_in_w': _L0_attn_in['f_in_w'], 'L0_attn_f_conv_w': _L0_attn_in['f_conv_w'], 'L0_attn_f_conv_b': _L0_attn_in['f_conv_b'], 'L0_attn_f_xproj_w': _L0_attn_in['f_xproj_w'], 'L0_attn_f_dt_w': _L0_attn_in['f_dt_w'], 'L0_attn_f_dt_b': _L0_attn_in['f_dt_b'], 'L0_attn_f_A_log': _L0_attn_in['f_A_log'], 'L0_attn_f_D': _L0_attn_in['f_D'], 'L0_attn_f_out_w': _L0_attn_in['f_out_w'], 'L0_attn_b_in_w': _L0_attn_in['b_in_w'], 'L0_attn_b_conv_w': _L0_attn_in['b_conv_w'], 'L0_attn_b_conv_b': _L0_attn_in['b_conv_b'], 'L0_attn_b_xproj_w': _L0_attn_in['b_xproj_w'], 'L0_attn_b_dt_w': _L0_attn_in['b_dt_w'], 'L0_attn_b_dt_b': _L0_attn_in['b_dt_b'], 'L0_attn_b_A_log': _L0_attn_in['b_A_log'], 'L0_attn_b_D': _L0_attn_in['b_D'], 'L0_attn_b_out_w': _L0_attn_in['b_out_w'], 'L0_ffn_ln1_w': _L0_ffn_in['ln1_w'], 'L0_ffn_ln2_w': _L0_ffn_in['ln2_w'], 'L0_ffn_wq': _L0_ffn_in['wq'], 'L0_ffn_wk': _L0_ffn_in['wk'], 'L0_ffn_wv': _L0_ffn_in['wv'], 'L0_ffn_wo': _L0_ffn_in['wo'], 'L0_ffn_router_w': _L0_ffn_in['router_w'], 'L0_ffn_w1': _L0_ffn_in['w1'], 'L0_ffn_w2': _L0_ffn_in['w2'], 'L0_ffn_w3': _L0_ffn_in['w3']}

def reference(x, cls_tok, L0_tok_W1, L0_tok_b1, L0_tok_W2, L0_tok_b2, L0_tok_W3, L0_tok_b3, L0_attn_f_in_w, L0_attn_f_conv_w, L0_attn_f_conv_b, L0_attn_f_xproj_w, L0_attn_f_dt_w, L0_attn_f_dt_b, L0_attn_f_A_log, L0_attn_f_D, L0_attn_f_out_w, L0_attn_b_in_w, L0_attn_b_conv_w, L0_attn_b_conv_b, L0_attn_b_xproj_w, L0_attn_b_dt_w, L0_attn_b_dt_b, L0_attn_b_A_log, L0_attn_b_D, L0_attn_b_out_w, L0_ffn_ln1_w, L0_ffn_ln2_w, L0_ffn_wq, L0_ffn_wk, L0_ffn_wv, L0_ffn_wo, L0_ffn_router_w, L0_ffn_w1, L0_ffn_w2, L0_ffn_w3):
    import jax
    import jax.numpy as jnp

    def _L0_tok_ref(x, W1, b1, W2, b2, W3, b3):
        import jax, jax.numpy as jnp
        import numpy as np
        B, C, H, W = (8, 64, 56, 56)
        K = 3

        def _unfold3x3(x):
            b, c, h, w = x.shape
            xp = jnp.pad(x, ((0, 0), (0, 0), (1, 1), (1, 1)))
            patches = jnp.stack([xp[:, :, i:i + h, j:j + w] for i in range(K) for j in range(K)], axis=2)
            return patches.reshape(b, c * K * K, h * w).transpose(0, 2, 1)
        t = _unfold3x3(x)
        h1 = jax.nn.relu(jnp.einsum('bld,dc->blc', t, W1) + b1)
        s = jax.nn.sigmoid(jnp.einsum('blc,cd->bld', h1, W2) + b2)
        out = jnp.einsum('bld,dc->blc', t * s, W3) + b3
        return out

    def _L0_attn_ref(g_data, f_in_w, f_conv_w, f_conv_b, f_xproj_w, f_dt_w, f_dt_b, f_A_log, f_D, f_out_w, b_in_w, b_conv_w, b_conv_b, b_xproj_w, b_dt_w, b_dt_b, b_A_log, b_D, b_out_w):
        import jax, jax.numpy as jnp
        import numpy as np
        D_MODEL = 64
        D_STATE = 16
        D_CONV = 4
        EXPAND = 2
        D_INNER = EXPAND * D_MODEL
        DT_RANK = (D_MODEL + 15) // 16
        B_SZ = 4
        SEQ = 1024

        def _mamba_params(key, prefix):
            ks = jax.random.split(key, 6)
            s = 0.02
            return {f'{prefix}_in_w': jax.random.normal(ks[0], (2 * D_INNER, D_MODEL), dtype=jnp.float32) * s, f'{prefix}_conv_w': jax.random.normal(ks[1], (D_INNER, D_CONV), dtype=jnp.float32) * s, f'{prefix}_conv_b': jnp.zeros((D_INNER,), dtype=jnp.float32), f'{prefix}_xproj_w': jax.random.normal(ks[2], (DT_RANK + 2 * D_STATE, D_INNER), dtype=jnp.float32) * s, f'{prefix}_dt_w': jax.random.normal(ks[3], (D_INNER, DT_RANK), dtype=jnp.float32) * s, f'{prefix}_dt_b': jax.random.normal(ks[4], (D_INNER,), dtype=jnp.float32) * s, f'{prefix}_A_log': jnp.log(jnp.tile(jnp.arange(1, D_STATE + 1, dtype=jnp.float32), (D_INNER, 1))), f'{prefix}_D': jnp.ones((D_INNER,), dtype=jnp.float32), f'{prefix}_out_w': jax.random.normal(ks[5], (D_MODEL, D_INNER), dtype=jnp.float32) * s}

        def _mamba(x, in_w, conv_w, conv_b, xproj_w, dt_w, dt_b, A_log, D_param, out_w):
            Bn, L, _ = x.shape
            xz = x @ in_w.T
            xin, z = jnp.split(xz, 2, axis=-1)
            lhs = xin.swapaxes(1, 2)
            rhs = conv_w[:, None, :]
            conv = jax.lax.conv_general_dilated(lhs, rhs, (1,), [(D_CONV - 1, 0)], dimension_numbers=('NCL', 'OIL', 'NCL'), feature_group_count=D_INNER)
            xc = jax.nn.silu(conv.swapaxes(1, 2) + conv_b)
            x_dbl = xc @ xproj_w.T
            dt_low = x_dbl[..., :DT_RANK]
            Bm = x_dbl[..., DT_RANK:DT_RANK + D_STATE]
            Cm = x_dbl[..., DT_RANK + D_STATE:]
            dt = jax.nn.softplus(dt_low @ dt_w.T + dt_b)
            A = -jnp.exp(A_log)

            def step(h, inps):
                dt_t, B_t, C_t, u_t = inps
                dA = jnp.exp(dt_t[:, :, None] * A)
                h = dA * h + dt_t[:, :, None] * B_t[:, None, :] * u_t[:, :, None]
                y = jnp.einsum('bdn,bn->bd', h, C_t)
                return (h, y)
            h0 = jnp.zeros((Bn, D_INNER, D_STATE), dtype=x.dtype)
            xs = (dt.swapaxes(0, 1), Bm.swapaxes(0, 1), Cm.swapaxes(0, 1), xc.swapaxes(0, 1))
            _, ys = jax.lax.scan(step, h0, xs)
            y = ys.swapaxes(0, 1) + D_param * xc
            y = y * jax.nn.silu(z)
            return y @ out_w.T
        fwd = _mamba(g_data, f_in_w, f_conv_w, f_conv_b, f_xproj_w, f_dt_w, f_dt_b, f_A_log, f_D, f_out_w)
        bwd = _mamba(jnp.flip(g_data, axis=-1), b_in_w, b_conv_w, b_conv_b, b_xproj_w, b_dt_w, b_dt_b, b_A_log, b_D, b_out_w)
        return fwd + jnp.flip(bwd, axis=-1) + g_data

    def _L0_ffn_ref(x, ln1_w, ln2_w, wq, wk, wv, wo, router_w, w1, w2, w3):
        import jax, jax.numpy as jnp
        import numpy as np
        B, T, C = (64, 96, 64)
        NH, NKV = (4, 2)
        HD = C // NH
        NREP = NH // NKV
        NE, TOPK = (8, 2)
        HID = int(8 / 3 * C)
        EPS_RMS = 1e-06

        def _rope_tables(t_len):
            inv_freq = 1.0 / 10000.0 ** (np.arange(0, HD, 2, dtype=np.float32) / HD)
            t = np.arange(t_len, dtype=np.float32)
            freqs = np.outer(t, inv_freq)
            emb = np.concatenate([freqs, freqs], axis=-1)
            return (jnp.asarray(np.cos(emb)), jnp.asarray(np.sin(emb)))

        def _rotate_half(x):
            h = x.shape[-1] // 2
            return jnp.concatenate([-x[..., h:], x[..., :h]], axis=-1)

        def _rmsnorm(v, w):
            return v * jax.lax.rsqrt(jnp.mean(v * v, axis=-1, keepdims=True) + EPS_RMS) * w
        Bx, Tx, Cx = x.shape
        h = _rmsnorm(x, ln1_w)
        q = (h @ wq.T).reshape(Bx, Tx, NH, HD).transpose(0, 2, 1, 3)
        k = (h @ wk.T).reshape(Bx, Tx, NKV, HD).transpose(0, 2, 1, 3)
        v = (h @ wv.T).reshape(Bx, Tx, NKV, HD).transpose(0, 2, 1, 3)
        cos, sin = _rope_tables(Tx)
        cos, sin = (cos[None, None], sin[None, None])
        q = q * cos + _rotate_half(q) * sin
        k = k * cos + _rotate_half(k) * sin
        k = jnp.repeat(k, NREP, axis=1)
        v = jnp.repeat(v, NREP, axis=1)
        scores = jnp.einsum('bhtd,bhsd->bhts', q, k) / jnp.sqrt(jnp.float32(HD))
        causal = jnp.tril(jnp.ones((Tx, Tx), dtype=bool))
        scores = jnp.where(causal[None, None], scores, jnp.float32(-1e+30))
        att = jax.nn.softmax(scores, axis=-1)
        y = jnp.einsum('bhts,bhsd->bhtd', att, v).transpose(0, 2, 1, 3).reshape(Bx, Tx, Cx)
        x = x + y @ wo.T
        flat = _rmsnorm(x, ln2_w).reshape(-1, Cx)
        probs = jax.nn.softmax(flat @ router_w.T, axis=-1)
        tp, ti = jax.lax.top_k(probs, TOPK)
        tp = tp / (jnp.sum(tp, axis=-1, keepdims=True) + 1e-09)
        weights = jnp.sum(tp[..., None] * jax.nn.one_hot(ti, NE, dtype=flat.dtype), axis=1)
        out = jnp.zeros_like(flat)
        for e in range(NE):
            hh = jax.nn.silu(flat @ w1[e].T) * (flat @ w3[e].T)
            out = out + weights[:, e:e + 1] * (hh @ w2[e].T)
        return x + out.reshape(Bx, Tx, Cx)
    h = _L0_tok_ref(x, L0_tok_W1, L0_tok_b1, L0_tok_W2, L0_tok_b2, L0_tok_W3, L0_tok_b3)
    h = jnp.concatenate([jnp.broadcast_to(cls_tok, (h.shape[0], 1, h.shape[2])), h], axis=1)
    h = h + _L0_attn_ref(_layernorm(h, axis=-1), L0_attn_f_in_w, L0_attn_f_conv_w, L0_attn_f_conv_b, L0_attn_f_xproj_w, L0_attn_f_dt_w, L0_attn_f_dt_b, L0_attn_f_A_log, L0_attn_f_D, L0_attn_f_out_w, L0_attn_b_in_w, L0_attn_b_conv_w, L0_attn_b_conv_b, L0_attn_b_xproj_w, L0_attn_b_dt_w, L0_attn_b_dt_b, L0_attn_b_A_log, L0_attn_b_D, L0_attn_b_out_w)
    h = h + _L0_ffn_ref(_layernorm(h, axis=-1), L0_ffn_ln1_w, L0_ffn_ln2_w, L0_ffn_wq, L0_ffn_wk, L0_ffn_wv, L0_ffn_wo, L0_ffn_router_w, L0_ffn_w1, L0_ffn_w2, L0_ffn_w3)
    return h

_drawn_inputs = setup_inputs


def setup_inputs(seed=0):
    import zlib

    import numpy as np

    out = dict(_drawn_inputs(seed))
    spreads = {'L0_attn_f_conv_b': (0.0, 0.8),
     'L0_attn_f_D': (1.0, 0.6),
     'L0_attn_b_conv_b': (0.0, 0.8),
     'L0_attn_b_D': (1.0, 0.6),
     'L0_ffn_ln1_w': (1.0, 0.6),
     'L0_ffn_ln2_w': (1.0, 0.6)}
    factors = {'cls_tok': 3.462,
     'L0_tok_b1': 8.0,
     'L0_attn_f_in_w': 8.0,
     'L0_attn_f_conv_w': 8.0,
     'L0_attn_f_xproj_w': 8.0,
     'L0_attn_f_dt_w': 8.0,
     'L0_attn_f_dt_b': 8.0,
     'L0_attn_f_A_log': 8.0,
     'L0_attn_f_out_w': 8.0,
     'L0_attn_b_in_w': 8.0,
     'L0_attn_b_conv_w': 8.0,
     'L0_attn_b_xproj_w': 8.0,
     'L0_attn_b_dt_w': 8.0,
     'L0_attn_b_dt_b': 8.0,
     'L0_attn_b_A_log': 8.0,
     'L0_attn_b_out_w': 8.0,
     'L0_ffn_wq': 8.0,
     'L0_ffn_wk': 8.0,
     'L0_ffn_wv': 8.0,
     'L0_ffn_wo': 8.0,
     'L0_ffn_router_w': 8.0,
     'L0_ffn_w1': 8.0,
     'L0_ffn_w2': 8.0,
     'L0_ffn_w3': 8.0}
    for name, (base, spread) in spreads.items():
        noise = np.random.default_rng([zlib.crc32(name.encode()), seed]).standard_normal(out[name].shape)
        drawn = base * np.exp(spread * noise) if base else spread * noise
        out[name] = jnp.asarray(drawn.astype(out[name].dtype))
    for name, factor in factors.items():
        out[name] = (out[name] * factor).astype(out[name].dtype)
    return out
```

```python
from contextlib import ExitStack

import concourse.bass as bass
from concourse import mybir

F32 = mybir.dt.float32
BF16 = mybir.dt.bfloat16
ALU = mybir.AluOpType
ACT = mybir.ActivationFunctionType
AX = mybir.AxisListType
B, C, HW = 8, 64, 56
L = HW * HW + 1
LT = 3200


def tok_phase(nc, d):
    WP = HW + 2
    AREA = WP * WP
    ROWS = 8
    CH = HW // ROWS
    N = ROWS * HW
    NSUB = 4
    SUB = N // NSUB
    PAIRS = [(0, 3, 0, 0, 0), (1, 4, 0, 0, 1), (2, 5, 0, 0, 2), (6, 7, 1, 2, 0), (8, None, 1, 2, 2)]
    NP = len(PAIRS)
    PER = 2 * CH
    h1 = d["h1"]
    x = d["x"]
    w1v = d["L0_tok_W1"].rearrange("(c k) o -> c k o", k=9)
    w3v = d["L0_tok_W3"].rearrange("(c k) o -> c k o", k=9)
    b2v = d["L0_tok_b2"].rearrange("(c k) -> c k", k=9)
    b1v = d["L0_tok_b1"].rearrange("(c a) -> c a", a=1)
    b3v = d["L0_tok_b3"].rearrange("(a c) -> a c", a=1)
    with ExitStack() as ctx:
        def sb(n, s, t=F32):
            return ctx.enter_context(nc.sbuf_tensor("tok_" + n, s, t))

        def sem(n):
            return ctx.enter_context(nc.semaphore("tok_" + n))

        img = [[sb(f"img{h}{k}", [128, AREA]) for k in range(2)] for h in range(2)]
        w1 = sb("w1", [128, NP, 128])
        w2raw = sb("w2raw", [C, 9 * C])
        w2 = sb("w2", [128, NP, 128])
        w3 = sb("w3", [128, NP, C])
        b1 = sb("b1", [128, 1])
        b2 = sb("b2", [128, NP])
        b3 = sb("b3", [128, C])
        zero = sb("zero", [64, C])
        hid = [sb(f"hid{i}", [128, N]) for i in range(2)]
        gate = [sb(f"gate{i}", [128, NP, N]) for i in range(2)]
        gated = [sb(f"gated{i}", [128, NP, N]) for i in range(2)]
        outs = [sb(f"outs{i}", [SUB, NSUB, C]) for i in range(2)]
        ps_hid = [ctx.enter_context(nc.psum_tensor(f"tok_ph{i}", [128, 512], F32)) for i in range(2)]
        ps_gate = [ctx.enter_context(nc.psum_tensor(f"tok_pg{i}", [128, 512], F32)) for i in range(4)]
        ps_out = [ctx.enter_context(nc.psum_tensor(f"tok_po{i}", [128, 512], F32)) for i in range(2)]

        cleared = sem("cleared")
        weights_in = sem("weights_in")
        w2_ready = sem("w2_ready")
        images_in = [sem(f"images_in{h}") for h in range(2)]
        conv_done = sem("conv_done")
        relu_done = sem("relu_done")
        w2_done = sem("w2_done")
        gate_done = sem("gate_done")
        gated_done = sem("gated_done")
        w3_done = sem("w3_done")
        out_ready = sem("out_ready")
        stored = [sem(f"stored{h}") for h in range(2)]
        edges = sem("edges")

        def img_view(half, k):
            return img[half][k][:].rearrange("p (r w) -> p r w", w=WP)

        def tap_view(half, p, ch):
            _, _, k, ki, kj = PAIRS[p]
            r = ch * ROWS + ki
            return img_view(half, k)[:, r:r + ROWS, kj:kj + HW]

        nw = 0
        with nc.Block() as block:
            @block.sync
            def _(sp):
                nonlocal nw
                sp.wait_ge(cleared, 1)
                for p, (lo, up, *_r) in enumerate(PAIRS):
                    for part, k in ((0, lo), (1, up)):
                        if k is None:
                            continue
                        rows = slice(64 * part, 64 * part + 64)
                        sp.dma_start(w1[rows, p, 0:C], w1v[:, k, :]).then_inc(weights_in, 16)
                        sp.dma_start(w1[rows, p, C:], w1v[:, k, :]).then_inc(weights_in, 16)
                        sp.dma_start(w3[rows, p, :], w3v[:, k, :]).then_inc(weights_in, 16)
                        with nc.allow_non_contiguous_dma(reason="64 biases"):
                            sp.dma_start(b2[rows, p:p + 1], b2v[:, k:k + 1]).then_inc(weights_in, 16)
                        nw += 4
                sp.dma_start(w2raw[:], d["L0_tok_W2"]).then_inc(weights_in, 16)
                sp.dma_start(b1[0:C], b1v).then_inc(weights_in, 16)
                sp.dma_start(b1[C:], b1v).then_inc(weights_in, 16)
                sp.dma_start(b3[:], b3v.to_broadcast([128, C])).then_inc(weights_in, 16)
                nw += 4
                sp.dma_start(h1[:, 0, :], d["cls_tok"].rearrange("a b c -> (a b) c").to_broadcast([B, C])).then_inc(edges, 16)
                for b in range(B):
                    sp.dma_start(h1[b, 1 + HW * HW:LT, :], zero[0:LT - 1 - HW * HW, :]).then_inc(edges, 16)
                with sp.Fori(0, B // 2) as i:
                    for k in range(PER):
                        g = i * PER + k
                        sp.wait_ge(out_ready, g + 1 + 2 * CH)
                        row = (i * 2 + k // CH) * LT + (1 + (k % CH) * N)
                        dst = h1.rearrange("b t c -> (b t) c")[bass.ds(row, N), :]
                        sp.dma_start(dst.rearrange("(s p) c -> p s c", p=SUB), outs[k % 2][:]).then_inc(stored[k % 2], 16)
                for buf in range(2):
                    sp.wait_ge(stored[buf], 16 + 16 * B * CH // 2)
                sp.wait_ge(edges, 16 * (B + 1))

            @block.tensor
            def _(pe):
                pe.wait_ge(weights_in, 16 * nw)
                pe.wait_ge(w2_ready, NP * 2 - 1)

                def conv(i, g, half, ch, k):
                    if ch == 0:
                        pe.wait_ge(images_in[half], (i + 1) * 64)
                    pe.wait_ge(relu_done, g + 1)
                    for p in range(NP):
                        mm = pe.matmul(ps_hid[k % 2][:, 0:N], w1[:, p, :], tap_view(half, p, ch),
                                       start=p == 0, stop=p == NP - 1)
                    mm.then_inc(conv_done, 1)

                def gates(g, k):
                    pe.wait_ge(relu_done, g + 1 + 2)
                    for p in range(NP):
                        pe.wait_ge(gate_done, g * NP + p + 1)
                        pe.matmul(ps_gate[(k * NP + p) % 4][:, 0:N], w2[:, p, :], hid[k % 2][:],
                                  start=True, stop=True).then_inc(w2_done, 1)

                def outputs(g, k):
                    pe.wait_ge(gated_done, g * NP + NP + 2 * NP)
                    pe.wait_ge(out_ready, g + 1 + 2 * CH - 2)
                    for s in range(NSUB):
                        for p in range(NP):
                            mm = pe.matmul(ps_out[k % 2][0:SUB, s * C:(s + 1) * C],
                                           gated[k % 2][:, p, s * SUB:(s + 1) * SUB], w3[:, p, :],
                                           start=p == 0, stop=p == NP - 1)
                    mm.then_inc(w3_done, 1)

                with pe.Fori(0, B // 2) as i:
                    for k in range(PER + 1):
                        if k < PER:
                            conv(i, i * PER + k, k // CH, k % CH, k)
                        if k > 0:
                            outputs(i * PER + (k - 1), k - 1)
                        if k < PER:
                            gates(i * PER + k, k)

            @block.scalar
            def _(act):
                act.wait_ge(weights_in, 16 * nw)
                with act.Fori(0, B // 2) as i:
                    for k in range(PER):
                        g = i * PER + k
                        act.wait_ge(conv_done, g + 1)
                        act.wait_ge(w2_done, g * NP + NP)
                        act.activation(hid[k % 2][:], ps_hid[k % 2][:, 0:N], ACT.Relu,
                                       bias=b1[:]).then_inc(relu_done, 1)
                        for p in range(NP):
                            act.wait_ge(w2_done, g * NP + p + 1 + 2 * NP)
                            if p == 0:
                                act.wait_ge(gated_done, g * NP + NP)
                            act.activation(gate[k % 2][:, p, :], ps_gate[(k * NP + p) % 4][:, 0:N], ACT.Sigmoid,
                                           bias=b2[:, p:p + 1]).then_inc(gate_done, 1)

            @block.vector
            def _(dve):
                dve.memset(w1[:], 0.0)
                dve.memset(w2[:], 0.0)
                dve.memset(w3[:], 0.0)
                dve.memset(b2[:], 0.0)
                dve.memset(zero[:], 0.0)
                dve.sem_inc(relu_done, 2)
                dve.sem_inc(w2_done, 2 * NP)
                dve.sem_inc(gate_done, 4)
                dve.sem_inc(gated_done, 2 * NP)
                dve.sem_inc(w3_done, 2)
                dve.sem_inc(stored[0], 16)
                dve.sem_inc(stored[1], 16)
                dve.drain().then_inc(cleared, 1)
                for half in range(2):
                    dve.memset(img[half][0][:], 0.0)
                    dve.memset(img[half][1][:], 0.0)
                    dve.drain().then_inc(out_ready, CH)
                dve.wait_ge(weights_in, 16 * nw)
                w2c = w2raw[:].rearrange("h (c k) -> h k c", k=9)
                for p, (lo, up, *_r) in enumerate(PAIRS):
                    dve.tensor_copy(w2[0:64, p, 0:64], w2c[:, lo, :]).then_inc(w2_ready, 1)
                    if up is not None:
                        dve.tensor_copy(w2[0:64, p, 64:128], w2c[:, up, :]).then_inc(w2_ready, 1)

                def evac(i, g, k):
                    dve.wait_ge(w3_done, g + 1 + 2)
                    dve.wait_ge(stored[k % 2], (i * CH + (k // 2 + 1)) * 16)
                    dve.tensor_tensor(outs[k % 2][:], ps_out[k % 2][0:SUB, 0:NSUB * C].rearrange("p (s c) -> p s c", c=C),
                                      b3[0:SUB].unsqueeze(1).to_broadcast([SUB, NSUB, C]), ALU.add).then_inc(out_ready, 1)

                with dve.Fori(0, B // 2) as i:
                    for k in range(PER + 1):
                        g = i * PER + k
                        if k < PER:
                            for p in range(NP):
                                dve.wait_ge(gate_done, g * NP + p + 1 + 4)
                                if p == 0:
                                    dve.wait_ge(w3_done, g + 1)
                                dve.tensor_tensor(gated[k % 2][:, p, :].rearrange("p (r w) -> p r w", w=HW),
                                                  gate[k % 2][:, p, :].rearrange("p (r w) -> p r w", w=HW),
                                                  tap_view(k // CH, p, k % CH), ALU.mult).then_inc(gated_done, 1)
                        if k > 0:
                            evac(i, i * PER + (k - 1), k - 1)

            @block.gpsimd
            def _(pool):
                with pool.Fori(0, B // 2) as i:
                    for half in range(2):
                        pool.wait_ge(out_ready, (i * 2 + half) * CH + CH)
                        src = x[bass.ds(i * 2 + half, 1)].rearrange("a c h w -> (a c) h w")
                        a, c = img_view(half, 0), img_view(half, 1)
                        pool.dma_start(a[0:64, 1:57, 1:57], src).then_inc(images_in[half], 16)
                        pool.dma_start(a[64:128, 0:56, 1:57], src).then_inc(images_in[half], 16)
                        pool.dma_start(c[0:64, 1:57, 1:57], src).then_inc(images_in[half], 16)
                        pool.dma_start(c[64:128, 1:57, 0:56], src).then_inc(images_in[half], 16)


def mamba_phase(nc, d):
    P = 128
    S = 16
    N = 800
    Q = LT // N
    U = 2 * Q
    J = 8
    NT = N // J
    H2 = N // 2
    LAG = 3
    EPS = 1e-5
    h1r = d["h1"].rearrange("b t c -> (b t) c")
    h2r = d["h2"].rearrange("b t c -> (b t) c")
    with ExitStack() as ctx:
        def sb(n, s, t=F32):
            return ctx.enter_context(nc.sbuf_tensor("mb_" + n, s, t))

        def sem(n):
            return ctx.enter_context(nc.semaphore("mb_" + n))

        def ps(n):
            return ctx.enter_context(nc.psum_tensor("mb_" + n, [P, 2, 512], F32))

        ident = sb("ident", [P, P])
        sel = sb("sel", [96, 2 * S, P], BF16)
        part23 = sb("part23", [96, 2])
        raw_in = [sb(f"raw_in{k}", [P, 2, C]) for k in range(2)]
        raw_conv = [sb(f"raw_conv{k}", [P, 4]) for k in range(2)]
        raw_bc = [sb(f"raw_bc{k}", [96, P]) for k in range(2)]
        raw_dtx = [sb(f"raw_dtx{k}", [4, P]) for k in range(2)]
        raw_dtw = [sb(f"raw_dtw{k}", [P, 4]) for k in range(2)]
        raw_out = [sb(f"raw_out{k}", [C, P]) for k in range(2)]
        taps = [sb(f"taps{k}", [P, 3, 2, C]) for k in range(2)]
        conv_b = [sb(f"conv_b{k}", [P, 1]) for k in range(2)]
        dt_b = [sb(f"dt_b{k}", [P, 1]) for k in range(2)]
        skip = [sb(f"skip{k}", [P, 1]) for k in range(2)]
        a_log = [sb(f"a_log{k}", [P, S]) for k in range(2)]
        a_exp = [sb(f"a_exp{k}", [P, S]) for k in range(2)]
        a_neg = [sb(f"a_neg{k}", [P, S]) for k in range(2)]
        w_in = [sb(f"w_in{k}", [P, 3, P]) for k in range(2)]
        w_bc = [sb(f"w_bc{k}", [P, 96]) for k in range(2)]
        w_dt4 = [sb(f"w_dt4{k}", [4, P]) for k in range(2)]
        w_dt = [sb(f"w_dt{k}", [P, P]) for k in range(2)]
        w_out = [sb(f"w_out{k}", [P, C]) for k in range(2)]

        xin = [sb(f"xin{k}", [NT, J, C]) for k in range(2)]
        cen = sb("cen", [NT, J, C])
        sq = sb("sq", [NT, J, C])
        st = sb("st", [NT, 6, J])
        half_neg = sb("half_neg", [NT, J])
        norm_consts = sb("norm_consts", [NT, 3, J])
        zero = sb("zero", [P, 1])
        gg = sb("gg", [NT, J, 2, C])
        hg = [sb(f"hg{k}", [NT, J, C]) for k in range(2)]
        res = [sb(f"res{k}", [NT, J, C]) for k in range(2)]
        G = sb("G", [P, N + 4])
        xc = [sb(f"xc{k}", [P, N]) for k in range(2)]
        sz = [sb(f"sz{k}", [P, N]) for k in range(2)]
        dt = [sb(f"dt{k}", [P, N]) for k in range(2)]
        du = [sb(f"du{k}", [P, N]) for k in range(2)]
        sp1 = sb("sp1", [P, N])
        sp2 = sb("sp2", [P, N])
        sp3 = sb("sp3", [P, N])
        relu = sb("relu", [P, N])
        part1 = sb("part1", [96, N], BF16)
        rest1 = sb("rest1", [96, N])
        part2 = sb("part2", [96, N], BF16)
        bc = [sb(f"bc{k}", [96, N], BF16) for k in range(2)]
        dA = [sb(f"dA{k}", [P, N]) for k in range(4)]
        dB = [sb(f"dB{k}", [P, N]) for k in range(2)]
        hs = [sb(f"hs{k}", [P, N]) for k in range(4)]
        cs = [sb(f"cs{k}", [P, N]) for k in range(4)]
        hc = [sb(f"hc{k}", [P, N]) for k in range(4)]
        carry = [sb(f"carry{k}", [P, S]) for k in range(2)]
        yd = sb("yd", [P, N])
        yz = [sb(f"yz{k}", [P, N]) for k in range(2)]
        PB, PC, PY, PP = ps("PB"), ps("PC"), ps("PY"), ps("PP")

        names = {}

        def S_(n):
            if n not in names:
                names[n] = sem(n)
            return names[n]

        w_loaded = S_("w_loaded")
        x_loaded = [S_("x_loaded0"), S_("x_loaded1")]
        res_stored = [S_("res_stored0"), S_("res_stored1")]
        su_dve, su_pe, su_act = S_("su_dve"), S_("su_pe"), S_("su_act")
        su_pool = S_("su_pool")
        ln_dve, ln_pool = S_("ln_dve"), S_("ln_pool")
        pp_w = S_("pp_w")
        g_ready = S_("g_ready")
        act_prep = S_("act_prep")
        dve_prep = S_("dve_prep")
        pool_prep = S_("pool_prep")
        o_w = S_("o_w")
        out_done = S_("out_done")
        b_w, c_w, y_w = S_("b_w"), S_("c_w"), S_("y_w")
        dA_r, cs_r = S_("dA_r"), S_("cs_r")
        dB_r, h_r = S_("dB_r"), S_("h_r")
        car_r, hc_r = S_("car_r"), S_("hc_r")
        yd_r, yz_r = S_("yd_r"), S_("yz_r")

        def halves(t):
            return t.rearrange("p (h n) -> p h n", h=2)

        def tasks(b, u):
            return b * (U * 4 + Q) + (4 * u + u // 2 + 1)

        wl = 0
        with nc.Block() as block:
            @block.sync
            def _(sp):
                nonlocal wl
                def load(dst, src):
                    nonlocal wl
                    sp.dma_start(dst, src).then_inc(w_loaded, 16)
                    wl += 16
                load(ident[:], d["ident"])
                load(sel[:], d["selectors"])
                load(part23[:], d["part_signs"])
                for k, z in enumerate("fb"):
                    w = lambda n: d[f"L0_attn_{z}_{n}"]
                    load(raw_in[k][:], w("in_w").rearrange("(x p) c -> p x c", x=2))
                    load(raw_conv[k][:], w("conv_w"))
                    for r in range(3):
                        load(raw_bc[k][32 * r:32 * r + 32, :], w("xproj_w")[4:36, :])
                    load(raw_dtx[k][:], w("xproj_w")[0:4, :])
                    load(raw_dtw[k][:], w("dt_w"))
                    load(raw_out[k][:], w("out_w"))
                    load(a_log[k][:], w("A_log"))
                    for t, n in ((conv_b, "conv_b"), (dt_b, "dt_b"), (skip, "D")):
                        load(t[k][:], w(n).rearrange("(p a) -> p a", a=1))

                def load_x(b, q):
                    c = b * Q + q
                    sp.wait_ge(ln_pool, c * 8 + 8)
                    sp.dma_start(xin[q % 2][:], h1r[bass.ds((b * Q + q) * N, N), :].rearrange("(p j) c -> p j c", j=J)
                                 ).then_inc(x_loaded[q % 2], 16)

                def store(b, q):
                    c = b * Q + q
                    sp.wait_ge(out_done, c + 1 + 2)
                    sp.dma_start(h2r[bass.ds((b * Q + q) * N, N), :].rearrange("(p j) c -> p j c", j=J), res[q % 2][:]
                                 ).then_inc(res_stored[q % 2], 16)

                def image(b, first, last):
                    for q in range(Q):
                        if q < Q - 1:
                            load_x(b, q + 1)
                        elif not last:
                            load_x(b + 1, 0)
                        if q > 0:
                            store(b, q - 1)
                        elif not first:
                            store(b - 1, Q - 1)

                load_x(0, 0)
                image(0, True, False)
                with sp.Fori(1, B - 1) as b:
                    image(b, False, False)
                image(B - 1, False, True)
                store(B - 1, Q - 1)
                for k in range(2):
                    sp.wait_ge(res_stored[k], 16 * (B * Q // 2 + 1))

            @block.tensor
            def _(pe):
                pe.wait_ge(w_loaded, wl)
                for k in range(2):
                    pe.wait_ge(su_dve, 6 if k == 0 else 17)
                    for r in range(3):
                        pe.transpose(PB[:, 0, r * P:(r + 1) * P], taps[k][:, r].rearrange("p a c -> p (a c)"), ident[:])
                    pe.transpose(PC[:, 0, 0:96], raw_bc[k][:], ident[0:96, 0:96])
                    pe.transpose(PC[:, 0, 96:96 + C], raw_out[k][:], ident[0:C, 0:C])
                    pe.transpose(PC[0:4, 1, 0:P], raw_dtw[k][:], ident[:]).then_inc(su_pe, 1)
                    pe.wait_ge(su_dve, 12 + 5 * k + 4)
                    pe.matmul(PP[:, 0, 0:P], raw_dtx[k][:], w_dt4[k][:], start=True, stop=True).then_inc(su_pe, 1)
                pe.wait_ge(su_dve, 22)

                def turn(b, q):
                    c = b * Q + q
                    pe.wait_ge(ln_pool, c * 8 + 7 + 16)
                    pe.wait_ge(out_done, c + 1)
                    pe.wait_ge(dve_prep, (b * U + 2 * q) * 3 + 3)
                    pe.wait_ge(act_prep, (b * U + 2 * q) * 6 + 4)
                    for j in range(J):
                        mm = pe.transpose(PP[:, j // 4, (j % 4) * NT:(j % 4 + 1) * NT],
                                          gg[:, j].rearrange("p a c -> p (a c)"), ident[0:NT, 0:NT])
                    mm.then_inc(pp_w, 1)

                def prep_z(b, u):
                    c, k = b * Q + u // 2, u % 2
                    pe.wait_ge(g_ready, c * 3 + 3 + 3)
                    if u % 2:
                        pe.wait_ge(dve_prep, (b * U + u) * 3 + 3)
                        pe.wait_ge(act_prep, (b * U + u) * 6 + 4)
                    for h in range(2):
                        mm = pe.matmul(PP[:, h, 0:H2], w_in[k][:, 2, :], G[:, 3 + h * H2:3 + (h + 1) * H2],
                                       start=True, stop=True)
                    mm.then_inc(pp_w, 1)

                def prep_k(b, u):
                    k = u % 2
                    pe.wait_ge(act_prep, (b * U + u) * 6 + 1 + 6)
                    for h in range(2):
                        for r in range(2):
                            at = 3 - 2 * r + h * H2
                            mm = pe.matmul(PP[:, h, 0:H2], w_in[k][:, r, :], G[:, at:at + H2], start=r == 0, stop=r == 1)
                    mm.then_inc(pp_w, 1)

                def prep_x(b, u):
                    k = u % 2
                    pe.wait_ge(act_prep, (b * U + u) * 6 + 2 + 6)
                    for h in range(2):
                        mm = pe.matmul(PP[0:96, h, 0:H2], w_bc[k][:], xc[k][:, h * H2:(h + 1) * H2], start=True, stop=True)
                    mm.then_inc(pp_w, 1)

                def prep_d(b, u):
                    k = u % 2
                    pe.wait_ge(dve_prep, (b * U + u) * 3 + 1 + 3)
                    pe.wait_ge(act_prep, (b * U + u) * 6 + 3 + 6)
                    for h in range(2):
                        mm = pe.matmul(PP[:, h, 0:H2], w_dt[k][:], xc[k][:, h * H2:(h + 1) * H2], start=True, stop=True)
                    mm.then_inc(pp_w, 1)

                def project(b, q, ahead=2):
                    c = b * Q + q
                    pe.wait_ge(yz_r, 2 * c + 2 + 2)
                    pe.wait_ge(dve_prep, (b * U + (2 * q + 2 + ahead)) * 3 + 3)
                    pe.wait_ge(act_prep, (b * U + (2 * q + 1 + ahead)) * 6 + 4 + 6)
                    for j in range(J):
                        for k in range(2):
                            mm = pe.matmul(PP[0:NT, 0, j * C:(j + 1) * C],
                                           yz[k][:].rearrange("p (t j) -> p j t", j=J)[:, j, :], w_out[k][:],
                                           start=k == 0, stop=k == 1)
                    mm.then_inc(o_w, 1)

                def row(b, u, n, which):
                    v, k = b * U * S + (u * S + n), u % 2
                    if which == 0:
                        pe.wait_ge(dB_r, v + 2 * S)
                        dst, out = PB, b_w
                    else:
                        pe.wait_ge(cs_r, v + 1)
                        dst, out = PC, c_w
                    for h in range(2):
                        mm = pe.matmul(dst[:, h, 0:H2], sel[:, which * S + n, :], bc[k][:, h * H2:(h + 1) * H2],
                                       start=True, stop=True)
                    mm.then_inc(out, 1)

                def add_state(b, u, n):
                    v = b * U * S + (u * S + n)
                    pe.wait_ge(hc_r, v + 1 + 4)
                    if n == 0:
                        pe.wait_ge(yd_r, b * U + (u + 2))
                    for h in range(2):
                        mm = pe.matmul(PY[:, h, 0:H2], ident[:], hc[n % 4][:, h * H2:(h + 1) * H2],
                                       start=n == 0, stop=n == S - 1)
                    mm.then_inc(y_w, 1)

                def unit(b, u, first, last):
                    for n in range(S):
                        if n == 0:
                            pe.wait_ge(dve_prep, (b * U + u) * 3 + 2 + 3)
                        row(b, u, n, 0)
                        row(b, u, n, 1)
                        if n >= LAG:
                            add_state(b, u, n - LAG)
                        elif u > 0:
                            add_state(b, u - 1, S + n - LAG)
                        elif not first:
                            add_state(b - 1, U - 1, S + n - LAG)
                        nb, nu = (b, u + 1) if u < U - 1 else (b + 1, 0)
                        if not (last and u == U - 1):
                            if n == 4 and nu % 2 == 0:
                                turn(nb, nu // 2)
                            if n == 6:
                                prep_z(nb, nu)
                            if n == 7:
                                prep_k(nb, nu)
                            if n == 9:
                                prep_x(nb, nu)
                            if n == 11:
                                prep_d(nb, nu)
                        if n == 14 and u % 2 == 0:
                            if u > 0:
                                project(b, u // 2 - 1)
                            elif not first:
                                project(b - 1, Q - 1)

                turn(0, 0)
                prep_z(0, 0)
                prep_k(0, 0)
                prep_x(0, 0)
                prep_d(0, 0)
                for u in range(U):
                    unit(0, u, True, False)
                with pe.Fori(1, B - 1) as b:
                    for u in range(U):
                        unit(b, u, False, False)
                for u in range(U):
                    unit(B - 1, u, False, True)
                for n in range(LAG):
                    add_state(B - 1, U - 1, S - LAG + n)
                project(B - 1, Q - 1, 0)

            @block.scalar
            def _(act):
                act.wait_ge(w_loaded, wl)
                for k in range(2):
                    act.activation(a_exp[k][:], a_log[k][:], ACT.Exp).then_inc(su_act, 1)
                act.wait_ge(su_dve, 24)

                def silus_z(b, u):
                    k, w = u % 2, b * U + u
                    act.wait_ge(pp_w, tasks(b, u) + 1)
                    act.wait_ge(yz_r, w + 1)
                    act.activation(halves(sz[k][:]), PP[:, :, 0:H2], ACT.Silu).then_inc(act_prep, 1)

                def silus_x(b, u):
                    k, w = u % 2, b * U + u
                    act.wait_ge(pp_w, tasks(b, u) + 2)
                    act.wait_ge(yd_r, w + 1)
                    act.activation(halves(xc[k][:]), PP[:, :, 0:H2], ACT.Silu, bias=conv_b[k][:]).then_inc(act_prep, 1)

                def first_part(b, u):
                    w = b * U + u
                    act.wait_ge(pp_w, tasks(b, u) + 3)
                    act.wait_ge(dve_prep, w * 3 + 1 + 1)
                    act.activation(halves(part1[:]), PP[0:96, :, 0:H2], ACT.Copy).then_inc(act_prep, 1)

                def softplus(b, u):
                    k, w = u % 2, b * U + u
                    act.wait_ge(pp_w, tasks(b, u) + 4)
                    act.wait_ge(act_prep, w * 6 + 5)
                    act.activation(halves(sp1[:]), PP[:, :, 0:H2], ACT.Abs, bias=dt_b[k][:]).then_inc(act_prep, 1)
                    act.wait_ge(act_prep, w * 6 + 4 + 6)
                    act.activation(sp2[:], sp1[:], ACT.Exp, scale=-1.0).then_inc(act_prep, 1)
                    act.wait_ge(act_prep, w * 6 + 5 + 6)
                    act.wait_ge(pool_prep, w * 3 + 2)
                    act.activation(sp3[:], sp2[:], ACT.Ln, bias=1.0).then_inc(act_prep, 1)

                def decay(b, u, n):
                    v, k = b * U * S + (u * S + n), u % 2
                    if n == 0:
                        act.wait_ge(pool_prep, (b * U + u) * 3 + 2 + 3)
                    act.wait_ge(h_r, v + 1)
                    act.activation(dA[n % 4][:], dt[k][:], ACT.Exp,
                                   scale=a_neg[k][:, n:n + 1]).then_inc(dA_r, 1)

                def copy_c(b, u, n):
                    v = b * U * S + (u * S + n)
                    act.wait_ge(c_w, v + 1 + 2 * S)
                    act.wait_ge(hc_r, v + 1)
                    act.activation(halves(cs[n % 4][:]), PC[:, :, 0:H2], ACT.Copy).then_inc(cs_r, 1)

                def unit(b, u, last):
                    nb, nu = (b, u + 1) if u < U - 1 else (b + 1, 0)
                    more = not (last and u == U - 1)
                    for n in range(S):
                        decay(b, u, n)
                        if more and n == 7:
                            silus_z(nb, nu)
                        copy_c(b, u, n)
                        if more and n == 7:
                            silus_x(nb, nu)
                        if more and n == 9:
                            first_part(nb, nu)
                        if more and n == 12:
                            softplus(nb, nu)

                silus_z(0, 0)
                silus_x(0, 0)
                first_part(0, 0)
                softplus(0, 0)
                for u in range(U):
                    unit(0, u, False)
                with act.Fori(1, B - 1) as b:
                    for u in range(U):
                        unit(b, u, False)
                for u in range(U):
                    unit(B - 1, u, True)

            @block.vector
            def _(dve):
                for s_, n_ in ((out_done, 2), (ln_pool, 16), (act_prep, 6), (dve_prep, 3), (pool_prep, 3), (yd_r, 2),
                               (yz_r, 2), (o_w, 1), (c_w, 2 * S), (dB_r, 2 * S), (dA_r, 2 * S), (cs_r, 1), (h_r, 4),
                               (hc_r, 4), (car_r, 2 * S), (y_w, 4), (res_stored[0], 16), (res_stored[1], 16)):
                    dve.sem_inc(s_, n_)
                dve.memset(G[:], 0.0).then_inc(g_ready, 3)
                dve.wait_ge(w_loaded, wl)
                for k in range(2):
                    for r in range(2):
                        for a in range(2):
                            i = 3 - (2 * r + a)
                            dve.tensor_scalar(taps[k][:, r, a, :], raw_in[k][:, 0, :], raw_conv[k][:, i:i + 1], None,
                                              ALU.mult).then_inc(su_dve, 1)
                    dve.tensor_copy(taps[k][:, 2, 0, :], raw_in[k][:, 1, :]).then_inc(su_dve, 1)
                    dve.memset(taps[k][:, 2, 1, :], 0.0).then_inc(su_dve, 1)
                for k in range(2):
                    dve.wait_ge(su_pe, 2 * k + 1)
                    dve.tensor_copy(w_in[k][:].rearrange("p r d -> p (r d)"), PB[:, 0, 0:3 * P]).then_inc(su_dve, 1)
                    dve.tensor_copy(w_bc[k][:], PC[:, 0, 0:96]).then_inc(su_dve, 1)
                    dve.tensor_copy(w_out[k][:], PC[:, 0, 96:96 + C]).then_inc(su_dve, 1)
                    dve.tensor_copy(w_dt4[k][:], PC[0:4, 1, 0:P]).then_inc(su_dve, 1)
                    dve.wait_ge(su_pe, 2 * k + 2)
                    dve.tensor_copy(w_dt[k][:], PP[:, 0, 0:P]).then_inc(su_dve, 1)
                dve.wait_ge(su_act, 2)
                for k in range(2):
                    dve.tensor_scalar(a_neg[k][:], a_exp[k][:], -1.0, None, ALU.mult).then_inc(su_dve, 1)

                def ln_sum(b, q):
                    c = b * Q + q
                    dve.wait_ge(x_loaded[q % 2], (b * (Q // 2) + (q // 2 + 1)) * 16)
                    dve.wait_ge(ln_pool, c * 8 + 16)
                    dve.tensor_reduce(st[:, 0, :], xin[q % 2][:], AX.X, ALU.add).then_inc(ln_dve, 1)

                def ln_var(b, q):
                    c = b * Q + q
                    dve.wait_ge(ln_pool, c * 8 + 3 + 16)
                    dve.tensor_reduce(st[:, 2, :], sq[:], AX.X, ALU.add).then_inc(ln_dve, 1)

                def take_g(b, q):
                    c = b * Q + q
                    dve.wait_ge(pp_w, tasks(b, 2 * q))
                    dve.wait_ge(g_ready, c * 3 + 3)
                    if q == 0:
                        dve.memset(G[:, 0:4], 0.0).then_inc(g_ready, 1)
                    else:
                        dve.tensor_copy(G[:, 0:4], G[:, N:N + 4]).then_inc(g_ready, 1)
                    dve.wait_ge(g_ready, c * 3 + 1 + 3)
                    for part in range(2):
                        rows = slice(64 * part, 64 * part + 64)
                        dst = G[rows, 3 + part:3 + part + N].rearrange("p (t h j) -> p h j t", h=2, j=J // 2)
                        src = PP[rows, :, 0:H2].rearrange("p h (j t) -> p h j t", t=NT)
                        dve.tensor_copy(dst, src).then_inc(g_ready, 1)

                def rest(b, u):
                    w = b * U + u
                    dve.wait_ge(act_prep, w * 6 + 3 + 6)
                    dve.wait_ge(dve_prep, w * 3 + 2)
                    dve.wait_ge(pool_prep, w * 3 + 1)
                    dve.scalar_tensor_tensor(halves(rest1[:]), halves(part1[:]), part23[:, 0:1], PP[0:96, :, 0:H2],
                                             ALU.mult, ALU.add).then_inc(dve_prep, 1)

                def parts(b, u):
                    k, w = u % 2, b * U + u
                    dve.wait_ge(pool_prep, w * 3 + 1 + 3)
                    dve.wait_ge(c_w, (w + 1) * S)
                    dve.scalar_tensor_tensor(bc[k][:], part2[:], part23[:, 1:2], rest1[:], ALU.mult,
                                             ALU.add).then_inc(dve_prep, 1)

                def relu_dt(b, u):
                    k, w = u % 2, b * U + u
                    dve.wait_ge(pp_w, tasks(b, u) + 4)
                    dve.wait_ge(pool_prep, w * 3 + 2)
                    dve.wait_ge(act_prep, w * 6 + 4 + 6)
                    dve.tensor_scalar(halves(relu[:]), PP[:, :, 0:H2], dt_b[k][:], 0.0, ALU.add,
                                      ALU.max).then_inc(dve_prep, 1)

                def input_term(b, u, n):
                    v, k = b * U * S + (u * S + n), u % 2
                    if n == 0:
                        dve.wait_ge(pool_prep, (b * U + u) * 3 + 3 + 3)
                    dve.wait_ge(b_w, v + 1)
                    dve.wait_ge(h_r, v + 3)
                    dve.tensor_tensor(halves(dB[n % 2][:]), halves(du[k][:]), PB[:, :, 0:H2], ALU.mult).then_inc(dB_r, 1)

                def scan(b, u, n):
                    v, k = b * U * S + (u * S + n), u % 2
                    dve.wait_ge(dA_r, v + 1 + 2 * S)
                    dve.wait_ge(dB_r, v + 1 + 2 * S)
                    dve.wait_ge(hc_r, v + 1)
                    dve.wait_ge(car_r, v + 2 * S - 3)
                    dve.tensor_tensor_scan(hs[n % 4][:], dA[n % 4][:], dB[n % 2][:],
                                           0.0 if u < 2 else carry[k][:, n:n + 1], ALU.mult, ALU.add).then_inc(h_r, 1)

                def add_skip(b, u):
                    k, w = u % 2, b * U + u
                    dve.wait_ge(y_w, (w + 1) * S + 4)
                    dve.wait_ge(yz_r, w + 2)
                    dve.scalar_tensor_tensor(halves(yd[:]), halves(xc[k][:]), skip[k][:], PY[:, :, 0:H2], ALU.mult,
                                             ALU.add).then_inc(yd_r, 1)

                def result(b, q):
                    c = b * Q + q
                    dve.wait_ge(o_w, c + 1 + 1)
                    dve.wait_ge(ln_pool, c * 8 + 8 + 16)
                    dve.wait_ge(res_stored[q % 2], (b * (Q // 2) + (q // 2 + 1)) * 16)
                    dve.tensor_tensor(res[q % 2][:], PP[0:NT, 0, :].rearrange("p (j c) -> p j c", c=C), hg[q % 2][:],
                                      ALU.add).then_inc(out_done, 1)

                def unit(b, u, first, last):
                    nb, nu = (b, u + 1) if u < U - 1 else (b + 1, 0)
                    more = not (last and u == U - 1)
                    nq = (b, u // 2 + 1) if u // 2 < Q - 1 else (b + 1, 0)
                    more_q = not (last and u // 2 == Q - 1)
                    for n in range(S):
                        if n == 3:
                            if u > 0:
                                add_skip(b, u - 1)
                            elif not first:
                                add_skip(b - 1, U - 1)
                        if n < S - 1:
                            input_term(b, u, n + 1)
                        elif more:
                            input_term(nb, nu, 0)
                        scan(b, u, n)
                        if u % 2 == 0 and more_q:
                            if n == 5:
                                ln_sum(*nq)
                            if n == 9:
                                ln_var(*nq)
                        if more:
                            if n == 4 and nu % 2 == 0:
                                take_g(nb, nu // 2)
                            if n == 9:
                                rest(nb, nu)
                            if n == 11:
                                parts(nb, nu)
                            if n == 12:
                                relu_dt(nb, nu)
                        if n == 14 and u % 2 == 0:
                            if u > 0:
                                result(b, u // 2 - 1)
                            elif not first:
                                result(b - 1, Q - 1)

                ln_sum(0, 0)
                ln_var(0, 0)
                take_g(0, 0)
                rest(0, 0)
                parts(0, 0)
                relu_dt(0, 0)
                input_term(0, 0, 0)
                for u in range(U):
                    unit(0, u, True, False)
                with dve.Fori(1, B - 1) as b:
                    for u in range(U):
                        unit(b, u, False, False)
                for u in range(U):
                    unit(B - 1, u, False, True)
                add_skip(B - 1, U - 1)
                result(B - 1, Q - 1)

            @block.gpsimd
            def _(pool):
                pool.memset(half_neg[:], -0.5)
                pool.memset(zero[:], 0.0)
                for i, value in enumerate((-1.0 / C, 1.0 / C, EPS)):
                    pool.memset(norm_consts[:, i, :], value)
                pool.drain().then_inc(su_pool, 1)
                pool.wait_ge(su_pool, 1)
                pool.wait_ge(w_loaded, wl)

                def normalise(b, q, step):
                    c = b * Q + q
                    n = c * 8 + 16
                    x, wide = xin[q % 2][:], [NT, J, C]
                    if step == 0:
                        pool.wait_ge(ln_dve, 2 * c + 1)
                        pool.wait_ge(ln_pool, n)
                        pool.tensor_tensor(st[:, 1, :], st[:, 0, :], norm_consts[:, 0, :], ALU.mult).then_inc(ln_pool, 1)
                        pool.wait_ge(ln_pool, n + 1)
                        pool.tensor_tensor(cen[:], x, st[:, 1, :].unsqueeze(2).to_broadcast(wide), ALU.add).then_inc(ln_pool, 1)
                        pool.wait_ge(ln_pool, n + 2)
                        pool.tensor_tensor(sq[:], cen[:], cen[:], ALU.mult).then_inc(ln_pool, 1)
                        return
                    pool.wait_ge(ln_dve, 2 * c + 2)
                    pool.tensor_tensor(st[:, 3, :], st[:, 2, :], norm_consts[:, 1, :], ALU.mult).then_inc(ln_pool, 1)
                    pool.wait_ge(ln_pool, n + 4)
                    pool.tensor_tensor(st[:, 5, :], st[:, 3, :], norm_consts[:, 2, :], ALU.add).then_inc(ln_pool, 1)
                    pool.wait_ge(ln_pool, n + 5)
                    pool.tensor_tensor(st[:, 4, :], st[:, 5, :], half_neg[:], ALU.pow).then_inc(ln_pool, 1)
                    pool.wait_ge(ln_pool, n + 6)
                    pool.wait_ge(g_ready, c * 3 + 3)
                    wide2 = [NT, J, 2, C]
                    pool.tensor_tensor(gg[:], cen[:].unsqueeze(2).to_broadcast(wide2),
                                       st[:, 4, :].unsqueeze(2).unsqueeze(3).to_broadcast(wide2), ALU.mult).then_inc(ln_pool, 1)

                def residual(b, q):
                    c = b * Q + q
                    pool.wait_ge(ln_pool, c * 8 + 7 + 16)
                    pool.wait_ge(out_done, c + 1)
                    pool.tensor_tensor(hg[q % 2][:], xin[q % 2][:], gg[:, :, 0, :], ALU.add).then_inc(ln_pool, 1)

                def second_part(b, u):
                    w = b * U + u
                    pool.wait_ge(dve_prep, w * 3 + 1 + 3)
                    pool.tensor_tensor(part2[:], rest1[:], zero[0:96, :].to_broadcast([96, N]), ALU.add).then_inc(pool_prep, 1)

                def steps(b, u):
                    k, w = u % 2, b * U + u
                    pool.wait_ge(act_prep, w * 6 + 6 + 6)
                    pool.wait_ge(dve_prep, w * 3 + 3 + 3)
                    pool.wait_ge(dA_r, (w + 1) * S)
                    pool.tensor_tensor(dt[k][:], relu[:], sp3[:], ALU.add).then_inc(pool_prep, 1)
                    pool.wait_ge(pool_prep, w * 3 + 2 + 3)
                    pool.wait_ge(dB_r, (w + 1) * S)
                    pool.tensor_tensor(du[k][:], dt[k][:], xc[k][:], ALU.mult).then_inc(pool_prep, 1)

                def gate(b, u):
                    k, w = u % 2, b * U + u
                    pool.wait_ge(yd_r, w + 1 + 2)
                    pool.wait_ge(o_w, b * Q + (u // 2 + 1))
                    pool.tensor_tensor(yz[k][:], yd[:], sz[k][:], ALU.mult).then_inc(yz_r, 1)

                def times_c(b, u, n):
                    v, k = b * U * S + (u * S + n), u % 2
                    pool.wait_ge(h_r, v + 1 + 4)
                    pool.tensor_tensor(carry[k][:, n:n + 1], hs[n % 4][:, N - 1:N], zero[:], ALU.add).then_inc(car_r, 1)
                    pool.wait_ge(cs_r, v + 1 + 1)
                    pool.wait_ge(y_w, v + 1)
                    pool.tensor_tensor(hc[n % 4][:], hs[n % 4][:], cs[n % 4][:], ALU.mult).then_inc(hc_r, 1)

                def unit(b, u, first, last):
                    nb, nu = (b, u + 1) if u < U - 1 else (b + 1, 0)
                    more = not (last and u == U - 1)
                    nq = (b, u // 2 + 1) if u // 2 < Q - 1 else (b + 1, 0)
                    more_q = not (last and u // 2 == Q - 1)
                    for n in range(S):
                        if n == 1 and u % 2 == 1 and more_q:
                            residual(*nq)
                        times_c(b, u, n)
                        if n == 3:
                            if u > 0:
                                gate(b, u - 1)
                            elif not first:
                                gate(b - 1, U - 1)
                        if u % 2 == 0 and more_q:
                            if n == 7:
                                normalise(*nq, 0)
                            if n == 11:
                                normalise(*nq, 1)
                        if more:
                            if n == 10:
                                second_part(nb, nu)
                            if n == 13:
                                steps(nb, nu)

                normalise(0, 0, 0)
                normalise(0, 0, 1)
                residual(0, 0)
                second_part(0, 0)
                steps(0, 0)
                for u in range(U):
                    unit(0, u, True, False)
                with pool.Fori(1, B - 1) as b:
                    for u in range(U):
                        unit(b, u, False, False)
                for u in range(U):
                    unit(B - 1, u, False, True)
                gate(B - 1, U - 1)


def attn_phase(nc, d):
    P = 128
    NB = LT // P
    HALF = (NB + 1) // 2
    D = 16
    NH, NKV = 4, 2
    QROWS = (NH + NKV) * D
    KR = 98
    QPART, KPART = (0, 0, 0, 1, 1, 2), (0, 1, 2, 0, 1, 0)
    NJ = 7
    SC = D ** -0.5
    LN_EPS, RMS_EPS = 1e-5, 1e-6
    W = [min(512, LT - 512 * j) for j in range(NJ)]

    def steps_of(j):
        out = []
        if j < NJ - 1:
            for k in range(4 * j + 4):
                for kv in range(NKV):
                    out.append((kv, [(k, max(0, (k - 4 * j)) * P)]))
        else:
            cuts = [NB * i // 8 for i in range(9)]
            for i in range(8):
                for kv in range(NKV):
                    out.append((kv, [(k, None) for k in range(cuts[i], cuts[i + 1])]))
        return out

    STEPS = [steps_of(j) for j in range(NJ)]
    NS = [len(s) for s in STEPS]
    SOFF = [sum(NS[:j]) for j in range(NJ)]
    NSI = sum(NS)
    TILES = [[(i, h, c, min(512, P * (i + 1) - 512 * c)) for i in range(4 * j, min(4 * j + 4, NB))
              for h in range(NH) for c in range(i // 4 + 1)] for j in range(NJ)]
    NT = [len(t) for t in TILES]
    TOFF = [sum(NT[:j]) for j in range(NJ)]
    NTI = sum(NT)
    assert NSI % 4 == 0 and NTI % 2 == 0

    def share(j, e):
        n, m = NT[(j + 1) % NJ], NS[j] - 2
        return range(n * e // m, n * (e + 1) // m) if e < m else range(0)

    LN0, TR0, V0 = 50, 82, 138
    NG = 7
    QK0 = [90, 96, 102, 108, 122, 128, 134]
    GROUPS = [(half, g * 512, min(512, (HALF if half == 0 else NB - HALF) * P - g * 512))
              for half in range(2) for g in range(4) if (HALF if half == 0 else NB - HALF) * P > g * 512]
    assert len(GROUPS) == NG
    NTR = (HALF + 3) // 4
    VCUT = 16

    def prep_tasks():
        return [(f"T{i}", 1) for i in range(NTR)] + [x for g in range(NG) for x in ((f"Q{g}", 1), (f"R{g}", 1))] + [("V0", 1), ("V1", 1)]

    def image_tasks(last):
        out = []
        for j in range(NJ):
            for e in range(NS[j]):
                s = SOFF[j] + e
                if j > 0 and e == 4:
                    out.append((f"DEN{j - 1}", 1))
                if j > 0 and e == 7:
                    out.append((f"PROJ{j - 1}", 1))
                if not last:
                    for i in range(NTR):
                        if s == TR0 + 2 * i:
                            out.append((f"T{i}", 1))
                    for g in range(NG):
                        if s == QK0[g]:
                            out.append((f"Q{g}", 1))
                        if s == QK0[g] + 1:
                            out.append((f"R{g}", 1))
                    for i in range(2):
                        if s == V0 + 2 * i:
                            out.append((f"V{i}", 1))
                if e == NS[j] - 1 and not (last and j == NJ - 1):
                    out.append((f"MT{(j + 1) % NJ}", 2))
        return out + [(f"DEN{NJ - 1}", 1), (f"PROJ{NJ - 1}", 1)]

    def index(tasks):
        at, w, r = {}, 0, 0
        for name, reads in tasks:
            at[name] = (w, r)
            w, r = w + 1, r + reads
        return at, w, r

    PRO, PRO_W, PRO_R = index(prep_tasks() + [("MT0", 2)])
    IMG, IMG_W, IMG_R = index(image_tasks(False))
    END, _, _ = index(image_tasks(True))

    class Task:
        def __init__(self, where, b, name):
            if where == "pro":
                (w, self.r), bw, self.b = PRO[name], 0, 0
            else:
                (w, self.r), bw, self.b = (END if where == "end" else IMG)[name], b * IMG_W + PRO_W, b * IMG_R + PRO_R
            self.made, self.j = bw + (w + 1), int(name[-1])

        def read(self, n=1):
            return self.b + (self.r + n)

    h2r = d["h2"].rearrange("b t c -> (b t) c")
    x2r = d["x2"].rearrange("b t c -> (b t) c")
    with ExitStack() as ctx:
        def sb(n, s, t=F32):
            return ctx.enter_context(nc.sbuf_tensor("at_" + n, s, t))

        def sem(n):
            return ctx.enter_context(nc.semaphore("at_" + n))

        ident = sb("ident", [P, P])
        identb = sb("identb", [P, P], BF16)
        mask_q = sb("mask_q", [P, P], BF16)
        mask_k = sb("mask_k", [P, P], BF16)
        den_sel = sb("den_sel", [P, P])
        cos = sb("cos", [QROWS, LT])
        sin = sb("sin", [QROWS, LT])
        raw = sb("raw", [QROWS, 3, 2, P])
        raw_o = sb("raw_o", [C, P])
        ln1 = sb("ln1", [P, 1])
        w_qk = sb("w_qk", [P, 2, 2, QROWS])
        w_v = sb("w_v", [P, 2, NKV * D])
        w_o = sb("w_o", [P, C])
        half_neg = sb("half_neg", [P, NB])
        norm_consts = sb("norm_consts", [P, 3, NB])
        X0 = sb("X0", [P, NB, C])
        cen = sb("cen", [P, NB, C])
        stt = sb("stt", [P, 8, NB])
        X = [sb(f"xn{k}", [P, NB, C]) for k in range(2)]
        R = sb("R", [P, HALF, 2, C])
        T = sb("T", [P, HALF, P])
        V = [sb(f"V{k}", [P, NB, NKV, 32]) for k in range(2)]
        t1 = sb("t1", [QROWS, 512])
        t2 = sb("t2", [QROWS, 512])
        qk = sb("qk", [QROWS, 512])
        qr = sb("qr", [QROWS, 512])
        parts = [sb(f"parts{k}", [QROWS, HALF * P], BF16) for k in range(3)]
        QS = [sb(f"QS{k}", [KR, NH, LT], BF16) for k in range(2)]
        KS = [sb(f"KS{k}", [KR, NKV, LT], BF16) for k in range(2)]
        pm = sb("pm", [P, 4, NH, NJ])
        negm = sb("negm", [P, 4, NH])
        m1 = sb("m1", [NH, 512], BF16)
        m2 = sb("m2", [NH, 512], BF16)
        E = [sb(f"E{k}", [P, 2, 512]) for k in range(4)]
        O = sb("O", [P, 512])
        rec = sb("rec", [P, 512])
        Y = sb("Y", [P, 512])
        x2 = [sb(f"x2{k}", [P, 4, C]) for k in range(2)]
        ST = [ctx.enter_context(nc.psum_tensor(f"at_ST{k}", [P, 2, 512], F32)) for k in range(2)]
        MX = [ctx.enter_context(nc.psum_tensor(f"at_MX{k}", [P, 512], F32)) for k in range(2)]
        PO = ctx.enter_context(nc.psum_tensor("at_PO", [P, 512], F32))
        MI = ctx.enter_context(nc.psum_tensor("at_MI", [P, 512], F32))

        loaded = sem("loaded")
        x_in = sem("x_in")
        stacked = [sem(f"stacked{k}") for k in range(2)]
        m_in = sem("m_in")
        x2_out = [sem(f"x2_out{k}") for k in range(2)]
        su_dve, su_pe = sem("su_dve"), sem("su_pe")
        su_pool = sem("su_pool")
        n_dve, n_pool, n_act = sem("n_dve"), sem("n_pool"), sem("n_act")
        mi_w, mi_r = sem("mi_w"), sem("mi_r")
        r_pool, r_act = sem("r_pool"), sem("r_act")
        st_w = sem("st_w")
        e_r = sem("e_r")
        pv_w = sem("pv_w")
        mx_w, mx_r = sem("mx_w"), sem("mx_r")
        fin = sem("fin")
        o_r = sem("o_r")
        y_r = sem("y_r")

        nl = 0

        with nc.Block() as block:
            @block.sync
            def _(sp):
                nonlocal nl

                def load(dst, src):
                    nonlocal nl
                    sp.dma_start(dst, src).then_inc(loaded, 16)
                    nl += 16
                load(ident[:], d["ident"])
                load(identb[:], d["ident_bf16"])
                load(mask_q[:], d["mask_queries"])
                load(mask_k[:], d["mask_keys"])
                load(den_sel[:], d["sum_selector"])
                load(cos[:], d["rope_cos"])
                load(sin[:], d["rope_sin"])
                sp.wait_ge(su_dve, 1)
                for half in range(2):
                    cols = slice(64 * half, 64 * half + 64)
                    load(raw[0:64, 0, half, cols], d["L0_ffn_wq"])
                    load(raw[64:96, 0, half, cols], d["L0_ffn_wk"])
                    load(raw[0:64, 1, half, cols], d["wq_rotated"])
                    load(raw[64:96, 1, half, cols], d["wk_rotated"])
                    load(raw[0:32, 2, half, cols], d["L0_ffn_wv"])
                    load(ln1[64 * half:64 * half + 64, :], d["L0_ffn_ln1_w"].rearrange("(c a) -> c a", a=1))
                for h in range(NH):
                    load(raw_o[:, 32 * h:32 * h + D], d["L0_ffn_wo"][:, D * h:D * h + D])

                def load_x(b):
                    sp.wait_ge(n_dve, b * 3 + 3)
                    sp.dma_start(X0[:], h2r[bass.ds(b * LT, LT), :].rearrange("(n p) c -> p n c", p=P)).then_inc(x_in, 16)

                def stack(gb, par, half):
                    ng = 4 if half == 0 else NG
                    sp.wait_ge(r_pool, gb * (3 * NG) + 3 * ng + 3)
                    n = (HALF if half == 0 else NB - HALF) * P
                    t0 = half * HALF * P
                    for a in range(6):
                        for h in range(NH):
                            sp.dma_start(QS[par][D * a:D * a + D, h, t0:t0 + n],
                                         parts[QPART[a]][D * h:D * h + D, 0:n]).then_inc(stacked[par], 16)
                        for kv in range(NKV):
                            r = (NH + kv) * D
                            sp.dma_start(KS[par][D * a:D * a + D, kv, t0:t0 + n],
                                         parts[KPART[a]][r:r + D, 0:n]).then_inc(stacked[par], 16)

                def maxima(task, par, j):
                    sp.wait_ge(mi_r, task.read(2))
                    sp.dma_start(QS[par][96:97, :, 512 * j:512 * j + W[j]], m1[:, 0:W[j]]).then_inc(m_in, 16)
                    sp.dma_start(QS[par][97:98, :, 512 * j:512 * j + W[j]], m2[:, 0:W[j]]).then_inc(m_in, 16)

                def store(where, b, par, j):
                    w = W[j]
                    sp.wait_ge(mi_r, Task(where, b, f"PROJ{j}").read())
                    sp.dma_start(x2r[bass.ds(b * LT + 512 * j, w), :].rearrange("(n p) c -> p n c", p=P),
                                 x2[(par * NJ + j) % 2][:, 0:w // P, :]).then_inc(x2_out[(par * NJ + j) % 2], 16)

                def image(b, par, where):
                    last = where == "end"
                    if not last:
                        load_x(b + 1)
                    for j in range(NJ):
                        for e in range(NS[j]):
                            s = SOFF[j] + e
                            if j > 0 and e == 10:
                                store(where, b, par, j - 1)
                            if not last:
                                if s == QK0[3] + 7:
                                    stack(b + 1, 1 - par, 0)
                                if s == QK0[6] + 7:
                                    stack(b + 1, 1 - par, 1)
                        if j < NJ - 1 or not last:
                            maxima(Task(where, b, f"MT{(j + 1) % NJ}"), par if j < NJ - 1 else 1 - par, (j + 1) % NJ)
                    store(where, b, par, NJ - 1)

                load_x(0)
                stack(0, 0, 0)
                stack(0, 0, 1)
                maxima(Task("pro", 0, "MT0"), 0, 0)
                with sp.Fori(0, B // 2 - 1) as i:
                    image(2 * i, 0, "img")
                    image(2 * i + 1, 1, "img")
                image(B - 2, 0, "img")
                image(B - 1, 1, "end")
                for k in range(2):
                    sp.wait_ge(x2_out[k], 16 + 16 * (B * NJ // 2))

            @block.tensor
            def _(pe):
                pe.wait_ge(loaded, nl)
                pe.wait_ge(su_dve, 2)
                for half in range(2):
                    pe.transpose(MI[:, 96 * half:96 * half + 96], raw[:, 0, half, :], ident[0:96, 0:96])
                    pe.transpose(MI[:, 192 + 96 * half:288 + 96 * half], raw[:, 1, half, :], ident[0:96, 0:96])
                    pe.transpose(MI[:, 384 + 32 * half:416 + 32 * half], raw[0:32, 2, half, :], ident[0:32, 0:32])
                pe.transpose(MI[:, 448:512], raw_o[:], ident[0:C, 0:C]).then_inc(su_pe, 1)
                pe.wait_ge(su_dve, 6)

                def open_task(t, where):
                    if where != "pro" or t.r > 0:
                        pe.wait_ge(mi_r, t.read(0))

                def turn(t, where, gb, i):
                    open_task(t, where)
                    if i == 0:
                        pe.wait_ge(n_pool, gb * 9 + 9 + 9)
                    ms = range(4 * i, min(4 * i + 4, HALF))
                    for m in ms:
                        mm = pe.transpose(MI[:, (m - 4 * i) * P:(m - 4 * i + 1) * P], R[:, m].rearrange("p a c -> p (a c)"),
                                          ident[:])
                    mm.then_inc(mi_w, 1)

                def project(t, where, g, rot):
                    half, c0, n = GROUPS[g]
                    open_task(t, where)
                    pe.matmul(MI[0:QROWS, 0:n], w_qk[:, rot, half, :], T[:].rearrange("p m t -> p (m t)")[:, c0:c0 + n],
                              start=True, stop=True).then_inc(mi_w, 1)

                def values(t, where, i):
                    open_task(t, where)
                    for n in range(VCUT * i, min(VCUT * i + VCUT, NB)):
                        half, m = n // HALF, n % HALF
                        o = (n - VCUT * i) * NKV * D
                        mm = pe.matmul(MI[:, o:o + NKV * D], T[:, m, :], w_v[:, half, :], start=True, stop=True)
                    mm.then_inc(mi_w, 1)

                def turn_max(t, where, gb, par, j):
                    open_task(t, where)
                    pe.wait_ge(fin, gb * NB + min(4 * j + 4, NB) + 3)
                    for i in range(W[j] // P):
                        mm = pe.transpose(MI[0:NH, i * P:(i + 1) * P], negm[:, i, :], ident[:])
                    mm.then_inc(mi_w, 1)

                def tile(gb, par, j, n):
                    i, h, c, w = TILES[j][n]
                    m = gb * NTI + (TOFF[j] + n)
                    pe.wait_ge(mx_r, m + 1)
                    diag = 512 * c + w == P * (i + 1)
                    k = (TOFF[j] + n) % 2
                    mm = pe.matmul(MX[k][:, 0:w], QS[par][0:96, h, i * P:i * P + P],
                                   KS[par][0:96, h // 2, 512 * c:512 * c + w], start=True, stop=not diag)
                    if diag:
                        mm = pe.matmul(MX[k][:, w - P:w], identb[:], mask_q[:], start=False, stop=True)
                    mm.then_inc(mx_w, 1)

                def transposed(b, par, j, e):
                    kv, blocks = STEPS[j][e]
                    g = b * NSI + (SOFF[j] + e)
                    if e == 0:
                        pe.wait_ge(m_in, (b * NJ + (j + 1)) * 32)
                    pe.wait_ge(e_r, g + 1)
                    k2 = (SOFF[j] + e) % 2
                    for hh in range(2):
                        h = 2 * kv + hh
                        for n, (k, off) in enumerate(blocks):
                            if off is None:
                                dst, a, w = ST[k2][:, hh, n * P:n * P + P], 512 * j, P
                                diag, dd = k == NB - 1, n * P
                            else:
                                dst, a, w = ST[k2][:, hh, off:512], 512 * j + off, 512 - off
                                diag, dd = k >= 4 * j, off
                            mm = pe.matmul(dst, KS[par][:, kv, k * P:k * P + P], QS[par][:, h, a:a + w],
                                           start=True, stop=not diag)
                            if diag:
                                mm = pe.matmul(ST[k2][:, hh, dd:dd + P], identb[:], mask_k[:], start=False, stop=True)
                    mm.then_inc(st_w, 1)

                def times_v(b, par, j, e):
                    s = b * NJ + j
                    pe.wait_ge(e_r, b * NSI + (SOFF[j] + e + 2 + 2))
                    if e == 0:
                        pe.wait_ge(o_r, s + 1)
                    blocks = STEPS[j][e][1]
                    for n, (k, off) in enumerate(blocks):
                        for h in range(NH):
                            kv, hh = h // 2, h % 2
                            src = E[(SOFF[j] + e + kv) % 4]
                            a, z = (n * P, n * P + P) if off is None else (off, 512)
                            oa, oz = (0, P) if off is None else (off, 512)
                            mm = pe.matmul(PO[32 * h:32 * h + 32, oa:oz], V[par][:, k, kv, :], src[:, hh, a:z],
                                           start=k == 0, stop=k == min(4 * j + 3, NB - 1), skip_group_check=True)
                    mm.then_inc(pv_w, 2)

                def sums(t, where, s):
                    open_task(t, where)
                    pe.wait_ge(o_r, s + 1 + 1)
                    j = t.j
                    pe.matmul(MI[:, 0:W[j]], den_sel[:], O[:, 0:W[j]], start=True, stop=True).then_inc(mi_w, 1)

                def out_proj(t, where, s):
                    open_task(t, where)
                    pe.wait_ge(y_r, s + 1 + 1)
                    for i in range(W[t.j] // P):
                        mm = pe.matmul(MI[:, i * C:(i + 1) * C], Y[:, i * P:(i + 1) * P], w_o[:], start=True, stop=True)
                    mm.then_inc(mi_w, 1)

                def image(b, par, where, count):
                    last = where == "end"
                    for j in range(NJ):
                        for e in range(NS[j]):
                            s = SOFF[j] + e
                            transposed(b, par, j, e)
                            if not (last and j == NJ - 1):
                                nb, np_, nj = (b, par, j + 1) if j < NJ - 1 else (b + 1, 1 - par, 0)
                                for n in share(j, e):
                                    if nj == 0 and n == 0:
                                        pe.wait_ge(stacked[np_], count)
                                    tile(nb, np_, nj, n)
                            if e % 2 == 1:
                                if e >= 3:
                                    times_v(b, par, j, e - 3)
                                elif j > 0:
                                    times_v(b, par, j - 1, NS[j - 1] - 2)
                            if j > 0 and e == 4:
                                sums(Task(where, b, f"DEN{j - 1}"), where, b * NJ + (j - 1))
                            if j > 0 and e == 7:
                                out_proj(Task(where, b, f"PROJ{j - 1}"), where, b * NJ + (j - 1))
                            if not last:
                                for i in range(NTR):
                                    if s == TR0 + 2 * i:
                                        turn(Task(where, b, f"T{i}"), where, b + 1, i)
                                for g in range(NG):
                                    if s == QK0[g]:
                                        project(Task(where, b, f"Q{g}"), where, g, 0)
                                    if s == QK0[g] + 1:
                                        project(Task(where, b, f"R{g}"), where, g, 1)
                                for i in range(2):
                                    if s == V0 + 2 * i:
                                        values(Task(where, b, f"V{i}"), where, i)
                            if e == NS[j] - 1 and not (last and j == NJ - 1):
                                nb, np_, nj = (b, par, j + 1) if j < NJ - 1 else (b + 1, 1 - par, 0)
                                turn_max(Task(where, b, f"MT{nj}"), where, nb, np_, nj)
                    times_v(b, par, NJ - 1, NS[NJ - 1] - 2)
                    sums(Task(where, b, f"DEN{NJ - 1}"), where, b * NJ + (NJ - 1))
                    out_proj(Task(where, b, f"PROJ{NJ - 1}"), where, b * NJ + (NJ - 1))

                for i in range(NTR):
                    turn(Task("pro", 0, f"T{i}"), "pro", 0, i)
                for g in range(NG):
                    project(Task("pro", 0, f"Q{g}"), "pro", g, 0)
                    project(Task("pro", 0, f"R{g}"), "pro", g, 1)
                for i in range(2):
                    values(Task("pro", 0, f"V{i}"), "pro", i)
                pe.wait_ge(stacked[0], 72 * 16)
                for n in range(NT[0]):
                    tile(0, 0, 0, n)
                turn_max(Task("pro", 0, "MT0"), "pro", 0, 0, 0)
                PER = 72 * 16
                with pe.Fori(0, B // 2 - 1) as i:
                    image(2 * i, 0, "img", (i + 1) * PER)
                    image(2 * i + 1, 1, "img", (i + 2) * PER)
                image(B - 2, 0, "img", (B // 2) * PER)
                image(B - 1, 1, "end", 0)

            @block.scalar
            def _(act):
                act.wait_ge(loaded, nl)

                def square(gb, par, n):
                    act.wait_ge(n_pool, gb * 9 + (2 if n == 0 else 5) + 9)
                    act.activation(X0[:], cen[:] if n == 0 else X[par][:], ACT.Square, scale=C ** -0.5).then_inc(n_act, 1)

                def part(gb, par, g, n, count, half_count):
                    half, c0, w = GROUPS[g]
                    a = gb * (3 * NG) + 3 * g + 3
                    if n == 0:
                        act.wait_ge(r_pool, a + 1)
                        if g == 0 and count is not None:
                            act.wait_ge(*count)
                        if g == 4:
                            act.wait_ge(stacked[par], half_count)
                        act.activation(parts[0][:, c0:c0 + w], qk[:, 0:w], ACT.Copy).then_inc(r_act, 1)
                    else:
                        act.wait_ge(r_pool, a + 2)
                        act.activation(parts[1][:, c0:c0 + w], qr[:, 0:w], ACT.Copy).then_inc(r_act, 1)

                def first_max(t, s):
                    act.wait_ge(mi_w, t.made)
                    act.wait_ge(m_in, s * 32 + 32)
                    act.activation(m1[:, 0:W[t.j]], MI[0:NH, 0:W[t.j]], ACT.Copy).then_inc(mi_r, 1)

                def exponential(b, j, e):
                    g = b * NSI + (SOFF[j] + e)
                    act.wait_ge(st_w, g + 1)
                    act.wait_ge(pv_w, g + 1)
                    blocks = STEPS[j][e][1]
                    a, z = (0, P * len(blocks)) if blocks[0][1] is None else (blocks[0][1], 512)
                    act.activation(E[(SOFF[j] + e) % 4][:, :, a:z], ST[(SOFF[j] + e) % 2][:, :, a:z], ACT.Exp,
                                   scale=SC).then_inc(e_r, 1)

                def take(b, j):
                    s = b * NJ + j
                    act.wait_ge(pv_w, b * NSI + (SOFF[j] + NS[j]) + 4)
                    act.wait_ge(y_r, s + 1)
                    act.activation(O[:, 0:W[j]], PO[:, 0:W[j]], ACT.Copy).then_inc(o_r, 1)

                def image(b, par, where, prev, half_count):
                    last = where == "end"
                    for j in range(NJ):
                        for e in range(NS[j]):
                            s = SOFF[j] + e
                            if e == NS[j] - 1 and not (last and j == NJ - 1):
                                nj = (j + 1) % NJ
                                first_max(Task(where, b, f"MT{nj}"), b * NJ + j)
                            exponential(b, j, e)
                            if j > 0 and e == 2:
                                take(b, j - 1)
                            if not last:
                                if s == LN0 + 8:
                                    square(b + 1, 1 - par, 0)
                                if s == LN0 + 20:
                                    square(b + 1, 1 - par, 1)
                                for g in range(NG):
                                    if s == QK0[g] + 3:
                                        part(b + 1, 1 - par, g, 0, prev, half_count)
                                    if s == QK0[g] + 5:
                                        part(b + 1, 1 - par, g, 1, prev, half_count)
                    take(b, NJ - 1)

                square(0, 0, 0)
                square(0, 0, 1)
                for g in range(NG):
                    part(0, 0, g, 0, None, 36 * 16)
                    part(0, 0, g, 1, None, 36 * 16)
                t = Task("pro", 0, "MT0")
                act.wait_ge(mi_w, t.made)
                act.activation(m1[:, 0:W[0]], MI[0:NH, 0:W[0]], ACT.Copy).then_inc(mi_r, 1)
                PER = 72 * 16
                with act.Fori(0, B // 2 - 1) as i:
                    image(2 * i, 0, "img", (stacked[0], (i + 1) * PER), i * PER + PER // 2)
                    image(2 * i + 1, 1, "img", (stacked[1], (i + 1) * PER), (i + 1) * PER + PER // 2)
                image(B - 2, 0, "img", (stacked[0], B // 2 * PER), (B // 2 - 1) * PER + PER // 2)
                image(B - 1, 1, "end", None, 0)

            @block.vector
            def _(dve):
                for s_, n_ in ((n_pool, 9), (n_dve, 3), (r_pool, 3), (e_r, 2), (pv_w, 4), (mx_r, 2), (fin, 3), (o_r, 1), (y_r, 1),
                               (x2_out[0], 16), (x2_out[1], 16)):
                    dve.sem_inc(s_, n_)
                dve.memset(raw[:], 0.0)
                dve.memset(raw_o[:], 0.0)
                dve.drain().then_inc(su_dve, 1)
                dve.memset(R[:], 0.0)
                for k in range(2):
                    dve.memset(V[k][:], 0.0)
                dve.drain().then_inc(su_dve, 1)
                dve.wait_ge(su_dve, 2)
                for k in range(2):
                    dve.memset(V[k][:, :, :, D:D + 1], 1.0)
                    dve.memset(KS[k][96:98], 1.0)
                dve.wait_ge(su_pe, 1)
                dve.wait_ge(loaded, nl)
                dve.tensor_scalar(w_qk[:].rearrange("p r h n -> p (r h n)"), MI[:, 0:384], ln1[:], None, ALU.mult).then_inc(su_dve, 1)
                dve.tensor_scalar(w_v[:].rearrange("p h n -> p (h n)"), MI[:, 384:448], ln1[:], None, ALU.mult).then_inc(su_dve, 1)
                dve.tensor_copy(w_o[:], MI[:, 448:512]).then_inc(su_dve, 1)
                dve.drain().then_inc(su_dve, 1)

                def moment(gb, n):
                    if n == 0:
                        dve.wait_ge(x_in, (gb + 1) * 16)
                        dve.wait_ge(n_pool, gb * 9 + 9)
                    else:
                        dve.wait_ge(n_act, gb * 2 + n)
                    dve.tensor_reduce(stt[:, n, :], X0[:], AX.X, ALU.add).then_inc(n_dve, 1)

                def take_t(t, i):
                    dve.wait_ge(mi_w, t.made)
                    a, z = 4 * i, min(4 * i + 4, HALF)
                    dve.tensor_copy(T[:, a:z, :], MI[:, 0:(z - a) * P].rearrange("p (m t) -> p m t", t=P)).then_inc(mi_r, 1)

                def rope(t, gb, g, rot):
                    half, c0, w = GROUPS[g]
                    t0 = half * HALF * P + c0
                    dve.wait_ge(mi_w, t.made)
                    dve.wait_ge(r_pool, gb * (3 * NG) + 3 * g + 1)
                    dve.tensor_tensor((t1, t2)[rot][:, 0:w], MI[0:QROWS, 0:w], (cos, sin)[rot][:, t0:t0 + w],
                                      ALU.mult).then_inc(mi_r, 1)

                def take_v(t, par, i):
                    dve.wait_ge(mi_w, t.made)
                    a, z = VCUT * i, min(VCUT * i + VCUT, NB)
                    dve.tensor_copy(V[par][:, a:z, :, 0:D],
                                    MI[:, 0:(z - a) * NKV * D].rearrange("p (n k e) -> p n k e", k=NKV, e=D)).then_inc(mi_r, 1)

                def tile(gb, j, n):
                    i, h, c, w = TILES[j][n]
                    m = gb * NTI + (TOFF[j] + n)
                    if h == 0 and c == 0:
                        if i == 0:
                            dve.wait_ge(fin, gb * NB + 3)
                        else:
                            dve.wait_ge(fin, gb * NB + (i + 1))
                    dve.wait_ge(mx_w, m + 1)
                    dve.tensor_reduce(pm[:, i % 4, h, c:c + 1], MX[(TOFF[j] + n) % 2][:, 0:w], AX.X, ALU.max).then_inc(mx_r, 1)
                    if h == NH - 1 and c == i // 4:
                        dve.wait_ge(mx_r, m + 1 + 2)
                        dve.tensor_reduce(negm[:, i % 4, :], pm[:, i % 4, :, 0:c + 1], AX.X, ALU.max,
                                          negate=True).then_inc(fin, 1)

                def second_max(t):
                    dve.wait_ge(mi_r, t.read(1))
                    dve.tensor_tensor(m2[:, 0:W[t.j]], MI[0:NH, 0:W[t.j]], m1[:, 0:W[t.j]], ALU.subtract).then_inc(mi_r, 1)

                def invert(t, s):
                    dve.wait_ge(mi_w, t.made)
                    dve.wait_ge(y_r, s + 1)
                    dve.reciprocal(rec[:, 0:W[t.j]], MI[:, 0:W[t.j]]).then_inc(mi_r, 1)

                def residual(t, b, par, j, count):
                    dve.wait_ge(mi_w, t.made)
                    k = (par * NJ + j) % 2
                    dve.wait_ge(x2_out[k], count)
                    w = W[j] // P
                    dve.tensor_tensor(x2[k][:, 0:w, :], MI[:, 0:w * C].rearrange("p (n c) -> p n c", c=C),
                                      X[par][:, 4 * j:4 * j + w, :], ALU.add).then_inc(mi_r, 1)

                def image(b, par, where, pair):
                    last = where == "end"

                    def stored(j):
                        return pair * (16 * NJ) + 16 * ((par * NJ + j) // 2 + 1)
                    for j in range(NJ):
                        for e in range(NS[j]):
                            s = SOFF[j] + e
                            nb, nj = (b, j + 1) if j < NJ - 1 else (b + 1, 0)
                            if not (last and j == NJ - 1):
                                for n in share(j, e):
                                    tile(nb, nj, n)
                            if not last:
                                for i in range(NTR):
                                    if s == TR0 + 2 * i + 1:
                                        take_t(Task(where, b, f"T{i}"), i)
                                for i in range(2):
                                    if s == V0 + 2 * i + 1:
                                        take_v(Task(where, b, f"V{i}"), 1 - par, i)
                            if j > 0 and e == 4:
                                invert(Task(where, b, f"DEN{j - 1}"), b * NJ + (j - 1))
                            if j > 0 and e == 7:
                                residual(Task(where, b, f"PROJ{j - 1}"), b, par, j - 1, stored(j - 1))
                            if not last:
                                for n, at in ((0, 0), (1, 10), (2, 22)):
                                    if s == LN0 + at:
                                        moment(b + 1, n)
                                for g in range(NG):
                                    if s == QK0[g]:
                                        rope(Task(where, b, f"Q{g}"), b + 1, g, 0)
                                    if s == QK0[g] + 1:
                                        rope(Task(where, b, f"R{g}"), b + 1, g, 1)
                            if e == NS[j] - 1 and not (last and j == NJ - 1):
                                second_max(Task(where, b, f"MT{nj}"))
                    invert(Task(where, b, f"DEN{NJ - 1}"), b * NJ + (NJ - 1))
                    residual(Task(where, b, f"PROJ{NJ - 1}"), b, par, NJ - 1, stored(NJ - 1))

                for n in range(3):
                    moment(0, n)
                for i in range(NTR):
                    take_t(Task("pro", 0, f"T{i}"), i)
                for g in range(NG):
                    rope(Task("pro", 0, f"Q{g}"), 0, g, 0)
                    rope(Task("pro", 0, f"R{g}"), 0, g, 1)
                for i in range(2):
                    take_v(Task("pro", 0, f"V{i}"), 0, i)
                for n in range(NT[0]):
                    tile(0, 0, n)
                second_max(Task("pro", 0, "MT0"))
                with dve.Fori(0, B // 2 - 1) as i:
                    image(2 * i, 0, "img", i)
                    image(2 * i + 1, 1, "img", i)
                image(B - 2, 0, "img", B // 2 - 1)
                image(B - 1, 1, "end", B // 2 - 1)

            @block.gpsimd
            def _(pool):
                pool.memset(half_neg[:], -0.5)
                for i, value in enumerate((-1.0 / C, LN_EPS, RMS_EPS)):
                    pool.memset(norm_consts[:, i, :], value)
                pool.drain().then_inc(su_pool, 1)
                pool.wait_ge(su_pool, 1)
                pool.wait_ge(su_dve, 2)

                def norms(gb, par, n):
                    c = gb * 9 + 9
                    wide = [P, NB, C]

                    def bc(k, a=0, z=NB):
                        return stt[:, k, a:z].unsqueeze(2).to_broadcast([P, z - a, C])
                    pool.wait_ge(n_dve, gb * 3 + n + 1 + 3)
                    if n == 0:
                        pool.wait_ge(n_pool, c)
                        pool.tensor_tensor(stt[:, 3, :], stt[:, 0, :], norm_consts[:, 0, :], ALU.mult).then_inc(n_pool, 1)
                        pool.wait_ge(n_pool, c + 1)
                        pool.tensor_tensor(cen[:], X0[:], bc(3), ALU.add).then_inc(n_pool, 1)
                    if n == 1:
                        pool.tensor_tensor(stt[:, 4, :], stt[:, 1, :], norm_consts[:, 1, :], ALU.add).then_inc(n_pool, 1)
                        pool.wait_ge(n_pool, c + 3)
                        pool.tensor_tensor(stt[:, 5, :], stt[:, 4, :], half_neg[:], ALU.pow).then_inc(n_pool, 1)
                        pool.wait_ge(n_pool, c + 4)
                        pool.tensor_tensor(X[par][:], cen[:], bc(5), ALU.mult).then_inc(n_pool, 1)
                    if n == 2:
                        pool.tensor_tensor(stt[:, 6, :], stt[:, 2, :], norm_consts[:, 2, :], ALU.add).then_inc(n_pool, 1)
                        pool.wait_ge(n_pool, c + 6)
                        pool.tensor_tensor(stt[:, 7, :], stt[:, 6, :], half_neg[:], ALU.pow).then_inc(n_pool, 1)
                        pool.wait_ge(n_pool, c + 7)
                        pool.tensor_tensor(R[:, :, 0, :], X[par][:, 0:HALF, :], bc(7, 0, HALF), ALU.mult).then_inc(n_pool, 1)
                        pool.tensor_tensor(R[:, 0:NB - HALF, 1, :], X[par][:, HALF:NB, :], bc(7, HALF, NB), ALU.mult).then_inc(n_pool, 1)

                def split(tr, gb, g, n):
                    half, c0, w = GROUPS[g]
                    a, r = gb * (3 * NG) + 3 * g + 3, gb * (2 * NG) + 2 * g
                    if n == 0:
                        pool.wait_ge(mi_r, tr.read())
                        pool.wait_ge(r_pool, a)
                        pool.tensor_tensor(qk[:, 0:w], t1[:, 0:w], t2[:, 0:w], ALU.add).then_inc(r_pool, 1)
                    if n == 1:
                        pool.wait_ge(r_act, r + 1)
                        pool.tensor_tensor(qr[:, 0:w], qk[:, 0:w], parts[0][:, c0:c0 + w], ALU.subtract).then_inc(r_pool, 1)
                    if n == 2:
                        pool.wait_ge(r_act, r + 2)
                        pool.tensor_tensor(parts[2][:, c0:c0 + w], qr[:, 0:w], parts[1][:, c0:c0 + w], ALU.subtract).then_inc(r_pool, 1)

                def divide(t, s):
                    pool.wait_ge(mi_r, t.read())
                    pool.tensor_tensor(Y[:, 0:W[t.j]], O[:, 0:W[t.j]], rec[:, 0:W[t.j]], ALU.mult).then_inc(y_r, 1)

                def image(b, par, where):
                    last = where == "end"
                    for j in range(NJ):
                        for e in range(NS[j]):
                            s = SOFF[j] + e
                            if j > 0 and e == 5:
                                divide(Task(where, b, f"DEN{j - 1}"), b * NJ + (j - 1))
                            if not last:
                                for n, at in ((0, 0), (1, 10), (2, 22)):
                                    if s == LN0 + at:
                                        norms(b + 1, 1 - par, n)
                                for g in range(NG):
                                    for n in range(3):
                                        if s == QK0[g] + 2 + 2 * n:
                                            split(Task(where, b, f"R{g}"), b + 1, g, n)
                    divide(Task(where, b, f"DEN{NJ - 1}"), b * NJ + (NJ - 1))

                for n in range(3):
                    norms(0, 0, n)
                for g in range(NG):
                    for n in range(3):
                        split(Task("pro", 0, f"R{g}"), 0, g, n)
                with pool.Fori(0, B // 2 - 1) as i:
                    image(2 * i, 0, "img")
                    image(2 * i + 1, 1, "img")
                image(B - 2, 0, "img")
                image(B - 1, 1, "end")


def moe_phase(nc, d):
    P, TB = 128, 4
    NE, HID = 8, 170
    REST = HID - P
    PER = P // REST
    NM = NE + -(-NE // PER)
    NTI = 6
    NW = 2 * NM * P + NE
    EPS = 1e-6
    NCH = 22

    x2r = d["x2"].rearrange("b t c -> (b t) c")
    h2r = d["h2"].rearrange("b t c -> (b t) c")
    outr = d["out"].rearrange("b t c -> (b t) c")
    with ExitStack() as ctx:
        def sb(n, s, t=F32):
            return ctx.enter_context(nc.sbuf_tensor("mo_" + n, s, t))

        def sem(n):
            return ctx.enter_context(nc.semaphore("mo_" + n))

        ident = sb("ident", [P, P])
        rank = sb("rank", [P, TB * NE])
        half_neg = sb("half_neg", [P, TB])
        eps = sb("eps", [P, TB])
        ln2 = sb("ln2", [P, 1])
        wf = sb("wf", [P, NW])
        w_part2 = sb("w_part2", [C, NW], BF16)
        w12 = sb("w12", [P, NW], BF16)
        w31 = sb("w31", [P, NW], BF16)
        w2_main = sb("w2_main", [P, NE, C])
        w2_rest = sb("w2_rest", [P, NM - NE, PER * C])
        x2 = [sb(f"x2{k}", [P, TB, C]) for k in range(2)]
        h2 = [sb(f"h2{k}", [P, TB, C]) for k in range(2)]
        squares = sb("squares", [P, TB, C])
        ssum = sb("ssum", [P, TB])
        mean = sb("mean", [P, TB])
        rstd = sb("rstd", [P, TB])
        fd = sb("fd", [P, TB, 2, C])
        left = sb("left", [P, 512])
        f1 = [sb(f"f1{k}", [P, 512], BF16) for k in range(2)]
        f2 = [sb(f"f2{k}", [P, 512], BF16) for k in range(2)]
        f13 = [sb(f"f13{k}", [P, 512], BF16) for k in range(2)]
        res = [sb(f"res{k}", [P, TB, C]) for k in range(2)]
        S = [sb(f"S{k}", [P, 512]) for k in range(2)]
        hh = [sb(f"hh{k}", [P, NM, 512]) for k in range(2)]
        weighted = sb("weighted", [P, NE, C])
        summed = sb("summed", [P, TB, C])
        y = [sb(f"y{k}", [P, TB, C]) for k in range(2)]
        top = sb("top", [P, TB])
        lg = sb("lg", [P, TB, NE])
        ex = sb("ex", [P, TB, NE])
        pr = sb("pr", [P, TB, NE])
        eq = sb("eq", [P, TB, NE])
        m1 = sb("m1", [P, TB, NE])
        m2 = sb("m2", [P, TB, NE])
        wt = sb("wt", [P, TB, NE])
        H1 = [ctx.enter_context(nc.psum_tensor(f"mo_H1{k}", [P, 512], F32)) for k in range(2)]
        H3 = [ctx.enter_context(nc.psum_tensor(f"mo_H3{k}", [P, 512], F32)) for k in range(2)]
        OUT = [ctx.enter_context(nc.psum_tensor(f"mo_OUT{k}", [P, 512], F32)) for k in range(2)]
        TP = ctx.enter_context(nc.psum_tensor("mo_TP", [P, 512], F32))
        LG = ctx.enter_context(nc.psum_tensor("mo_LG", [P, 512], F32))

        loaded = sem("loaded")
        x_in = [sem(f"x_in{k}") for k in range(2)]
        stored = [sem(f"stored{k}") for k in range(2)]
        su_dve, su_act = sem("su_dve"), sem("su_act")
        su_pool = sem("su_pool")
        f_act = sem("f_act")
        f_dve = sem("f_dve")
        f_pool = sem("f_pool")
        tp_w = sem("tp_w")
        lg_w = sem("lg_w")
        ex_w = sem("ex_w")
        r_dve = sem("r_dve")
        h1_w, h3_w = sem("h1_w"), sem("h3_w")
        s_w = sem("s_w")
        hh_w = sem("hh_w")
        o_w = sem("o_w")
        ow_r = sem("ow_r")
        sum_w = sem("sum_w")
        y_w = sem("y_w")
        TP_0, RD_0, FD_0, FP_0, S_0, HH_0, O_0, OW_0, SUM_0, Y_0 = 1, NCH, 2, 5, 2, 2, 8, 2, 1, 4
        nl = 10 * 16

        with nc.Block() as block:
            @block.sync
            def _(sp):
                sp.dma_start(ident[:], d["ident"]).then_inc(loaded, 16)
                sp.dma_start(rank[:], d["expert_rank"]).then_inc(loaded, 16)
                for a in (0, C):
                    sp.dma_start(wf[a:a + C, 0:2 * NM * P], d["w13_columns"]).then_inc(loaded, 16)
                    sp.dma_start(wf[a:a + C, 2 * NM * P:NW], d["router_columns"]).then_inc(loaded, 16)
                    sp.dma_start(ln2[a:a + C, :], d["L0_ffn_ln2_w"].rearrange("(c a) -> c a", a=1)).then_inc(loaded, 16)
                sp.dma_start(w2_main[:], d["w2_main"]).then_inc(loaded, 16)
                sp.dma_start(w2_rest[:], d["w2_rest"]).then_inc(loaded, 16)

                def load(g, k, rows):
                    for dst, src in ((x2, x2r), (h2, h2r)):
                        sp.dma_start(dst[k][:], src[rows, :].rearrange("(n p) c -> p n c", p=P)).then_inc(x_in[k], 16)

                def load_tail(k, b0):
                    for dst, src in ((x2, "x2"), (h2, "h2")):
                        sp.dma_start(dst[k][:], d[src][b0:b0 + TB, LT - P:LT, :].rearrange("b t c -> t b c")).then_inc(x_in[k], 16)

                def free(g):
                    sp.wait_ge(f_pool, 5 * g + FP_0 - 5)

                def store(g, k, rows):
                    sp.wait_ge(y_w, TB * g + TB + Y_0)
                    sp.dma_start(outr[rows, :].rearrange("(n p) c -> p n c", p=P), y[k][:]).then_inc(stored[k], 16)

                def store_tail(g, k, b0):
                    n = L - (LT - P)
                    sp.wait_ge(y_w, TB * g + TB + Y_0)
                    sp.dma_start(d["out"][b0:b0 + TB, LT - P:L, :].rearrange("b t c -> t b c"), y[k][0:n]).then_inc(stored[k], 16)

                def rows(b, j, stride):
                    return bass.ds(b * stride + j * 512, 512)

                load(0, 0, rows(0, 0, LT))
                load(1, 1, rows(0, 1, LT))

                def image(b, first, last):
                    for j in range(NTI):
                        g = NTI * b + j
                        free(g + 2)
                        if last and j >= NTI - 2:
                            load_tail(j % 2, TB * (j % 2))
                        else:
                            load(g + 2, j % 2, rows(b, j + 2, LT) if j < NTI - 2 else rows(b + 1, j + 2 - NTI, LT))
                        if not (first and j == 0):
                            store(g - 1, (j + 1) % 2, rows(b, j - 1, L) if j > 0 else rows(b - 1, NTI - 1, L))
                image(0, True, False)
                with sp.Fori(1, B - 1) as b:
                    image(b, False, False)
                image(B - 1, False, True)
                store(NTI * B - 1, 1, rows(B - 1, NTI - 1, L))
                store_tail(NTI * B, 0, 0)
                store_tail(NTI * B + 1, 1, TB)
                for k in range(2):
                    sp.wait_ge(stored[k], 16 + 16 * (NTI * B + 2) // 2)

            @block.tensor
            def _(pe):
                pe.wait_ge(loaded, nl)
                pe.wait_ge(su_dve, 4)

                def turn(g, k):
                    pe.wait_ge(f_pool, 5 * g + 3 + FP_0)
                    pe.wait_ge(f_dve, 2 * g + FD_0)
                    for n in range(TB):
                        mm = pe.transpose(TP[:, n * P:(n + 1) * P], fd[:, n].rearrange("p a c -> p (a c)"), ident[:])
                    mm.then_inc(tp_w, 1)

                def route(g, k):
                    pe.wait_ge(f_act, 4 * g + 4)
                    pe.wait_ge(f_pool, 5 * g + 4 + FP_0)
                    pe.wait_ge(r_dve, NCH * (g - 1) + 2 + RD_0)
                    for n in range(TB):
                        for a, (f, w) in enumerate(((f1, w12), (f2, w12), (f13, w31))):
                            mm = pe.matmul(LG[:, n * NE:(n + 1) * NE], f[k][:, n * P:(n + 1) * P], w[:, 2 * NM * P:NW],
                                           start=a == 0, stop=a == 2)
                    mm.then_inc(lg_w, 1)

                def hidden(g, k, m):
                    s = NM * g + m
                    i = (k + m) % 2
                    pe.wait_ge(s_w, s + 1 - 2 + S_0)
                    for a, (f, w) in enumerate(((f1, w12), (f2, w12), (f13, w31))):
                        mm = pe.matmul(H1[i][:], w[:, m * P:(m + 1) * P], f[k][:], start=a == 0, stop=a == 2)
                    mm.then_inc(h1_w, 1)
                    pe.wait_ge(hh_w, s + 1 - 2 + HH_0)
                    for a, (f, w) in enumerate(((f1, w12), (f2, w12), (f13, w31))):
                        mm = pe.matmul(H3[i][:], w[:, (NM + m) * P:(NM + m + 1) * P], f[k][:], start=a == 0, stop=a == 2)
                    mm.then_inc(h3_w, 1)

                def experts(g, k, n):
                    q = TB * g + n
                    if n == 0:
                        pe.wait_ge(hh_w, NM * g + NM + HH_0)
                    pe.wait_ge(ow_r, q + 1 - 2 + OW_0)
                    dst = OUT[n % 2]
                    for r in range(NM - NE):
                        w = min(PER, NE - PER * r) * C
                        pe.matmul(dst[:, PER * C * r:PER * C * r + w], hh[k][:, NE + r, n * P:(n + 1) * P], w2_rest[:, r, 0:w],
                                  start=r == 0, stop=False, skip_group_check=True)
                    for e in range(NE):
                        mm = pe.matmul(dst[:, C * e:C * e + C], hh[k][:, e, n * P:(n + 1) * P], w2_main[:, e, :],
                                       start=False, stop=True, skip_group_check=True)
                    mm.then_inc(o_w, 1)

                def period(g, k, first, last):
                    for m in range(NM):
                        hidden(g, k, m)
                        if not first and m in (2, 4, 6, 8):
                            experts(g - 1, 1 - k, (m - 2) // 2)
                        if not last and m == 3:
                            turn(g + 1, 1 - k)
                        if not last and m == 6:
                            route(g + 1, 1 - k)

                turn(0, 0)
                route(0, 0)
                for j in range(NTI):
                    period(j, j % 2, j == 0, False)
                with pe.Fori(1, B) as b:
                    for j in range(NTI):
                        period(NTI * b + j, j % 2, False, False)
                period(NTI * B, 0, False, False)
                period(NTI * B + 1, 1, False, True)
                for n in range(TB):
                    experts(NTI * B + 1, 1, n)

            @block.scalar
            def _(act):
                act.wait_ge(su_dve, 1)
                act.activation(w12[0:C], wf[0:C], ACT.Copy).then_inc(su_act, 1)
                act.activation(w31[C:P], wf[C:P], ACT.Copy).then_inc(su_act, 1)
                act.wait_ge(su_dve, 3)
                act.activation(w12[C:P], wf[C:P], ACT.Copy).then_inc(su_act, 1)
                act.activation(w_part2[:], wf[0:C], ACT.Copy).then_inc(su_act, 1)

                def square(g, k, pair):
                    act.wait_ge(x_in[k], 32 * pair + 32)
                    act.wait_ge(f_dve, 2 * g + 1 - 2 + FD_0)
                    act.activation(squares[:], x2[k][:], ACT.Square, scale=C ** -0.5).then_inc(f_act, 1)

                def first_part(g, k):
                    act.wait_ge(tp_w, g + 1 + TP_0)
                    act.activation(f1[k][:], TP[:], ACT.Copy).then_inc(f_act, 1)
                    act.wait_ge(f_act, 4 * g + 2)
                    act.activation(f13[k][0:C], f1[k][0:C], ACT.Copy).then_inc(f_act, 1)

                def second_part(g, k):
                    act.wait_ge(f_dve, 2 * g + 2 + FD_0)
                    act.activation(f2[k][:], left[:], ACT.Copy).then_inc(f_act, 1)

                def exponential(g):
                    act.wait_ge(r_dve, NCH * g + 2 + RD_0)
                    act.activation(ex[:], lg[:], ACT.Exp).then_inc(ex_w, 1)

                def silu(g, k, m):
                    s = NM * g + m
                    i = (k + m) % 2
                    act.wait_ge(h1_w, s + 1)
                    act.wait_ge(hh_w, s + 1 - 2 + HH_0)
                    act.activation(S[i][:], H1[i][:], ACT.Silu).then_inc(s_w, 1)

                def period(g, k, pair, last):
                    for m in range(NM):
                        silu(g, k, m)
                        if m == 1:
                            exponential(g)
                            if not last:
                                square(g + 1, 1 - k, pair)
                        if not last and m == 3:
                            first_part(g + 1, 1 - k)
                        if not last and m == 4:
                            second_part(g + 1, 1 - k)

                act.wait_ge(su_dve, 4)
                square(0, 0, 0)
                first_part(0, 0)
                second_part(0, 0)
                with act.Fori(0, B) as b:
                    for j in range(NTI):
                        period(NTI * b + j, j % 2, (NTI // 2) * b + (j + 1) // 2, False)
                period(NTI * B, 0, NTI * B // 2, False)
                period(NTI * B + 1, 1, None, True)

            @block.vector
            def _(dve):
                for s_, n_ in ((tp_w, TP_0), (r_dve, RD_0), (f_dve, FD_0), (f_pool, FP_0), (s_w, S_0), (hh_w, HH_0), (o_w, O_0),
                               (ow_r, OW_0), (sum_w, SUM_0), (y_w, Y_0), (stored[0], 16), (stored[1], 16)):
                    dve.sem_inc(s_, n_)
                dve.wait_ge(loaded, nl)
                dve.tensor_scalar(wf[:], wf[:], ln2[:], None, ALU.mult).then_inc(su_dve, 1)
                dve.wait_ge(su_dve, 1)
                dve.wait_ge(su_act, 2)
                dve.tensor_tensor(wf[0:C], wf[0:C], w12[0:C], ALU.subtract).then_inc(su_dve, 1)
                dve.tensor_tensor(wf[C:P], wf[C:P], w31[C:P], ALU.subtract).then_inc(su_dve, 1)
                dve.wait_ge(su_dve, 3)
                dve.wait_ge(su_act, 4)
                dve.tensor_tensor(w31[0:C], wf[0:C], w_part2[:], ALU.subtract).then_inc(su_dve, 1)

                def sum_squares(g):
                    dve.wait_ge(f_act, 4 * g + 1)
                    dve.wait_ge(f_pool, 5 * g + 1 - 5 + FP_0)
                    dve.tensor_reduce(ssum[:], squares[:], AX.X, ALU.add).then_inc(f_dve, 1)

                def leave(g, k):
                    dve.wait_ge(f_act, 4 * g + 2)
                    dve.wait_ge(f_pool, 5 * g + 4 - 5 + FP_0)
                    dve.tensor_tensor(left[:], TP[:], f1[k][:], ALU.subtract).then_inc(f_dve, 1)

                def routing(g, steps):
                    r = NCH * g + RD_0

                    def wide(a):
                        return a[:].unsqueeze(2).to_broadcast([P, TB, NE])
                    logits = LG[:, 0:TB * NE].rearrange("p (n e) -> p n e", e=NE)
                    rk = rank[:].rearrange("p (n e) -> p n e", e=NE)
                    for i in steps:
                        dve.wait_ge(r_dve, r + i)
                        if i == 0:
                            dve.wait_ge(lg_w, g + 1)
                            op = dve.tensor_reduce(top[:], logits, AX.X, ALU.max)
                        elif i == 1:
                            op = dve.tensor_tensor(lg[:], logits, wide(top), ALU.subtract)
                        elif i == 2:
                            dve.wait_ge(ex_w, g + 1)
                            op = dve.tensor_reduce(top[:], ex[:], AX.X, ALU.add)
                        elif i == 3:
                            op = dve.reciprocal(top[:], top[:])
                        elif i == 4:
                            op = dve.tensor_tensor(pr[:], ex[:], wide(top), ALU.mult)
                        elif i == 5:
                            op = dve.tensor_reduce(top[:], pr[:], AX.X, ALU.max)
                        elif i == 6:
                            op = dve.tensor_tensor(eq[:], pr[:], wide(top), ALU.is_equal)
                        elif i == 7:
                            op = dve.tensor_tensor(eq[:], eq[:], rk, ALU.mult)
                        elif i == 8:
                            op = dve.tensor_reduce(top[:], eq[:], AX.X, ALU.max)
                        elif i == 9:
                            op = dve.tensor_tensor(m1[:], eq[:], wide(top), ALU.is_equal)
                        elif i == 10:
                            op = dve.scalar_tensor_tensor(ex[:], m1[:], -2.0, pr[:], ALU.mult, ALU.add)
                        elif i == 11:
                            op = dve.tensor_reduce(top[:], ex[:], AX.X, ALU.max)
                        elif i == 12:
                            op = dve.tensor_tensor(eq[:], ex[:], wide(top), ALU.is_equal)
                        elif i == 13:
                            op = dve.tensor_tensor(eq[:], eq[:], rk, ALU.mult)
                        elif i == 14:
                            op = dve.tensor_reduce(top[:], eq[:], AX.X, ALU.max)
                        elif i == 15:
                            op = dve.tensor_tensor(m2[:], eq[:], wide(top), ALU.is_equal)
                        elif i == 16:
                            op = dve.tensor_tensor(m1[:], m1[:], m2[:], ALU.add)
                        elif i == 17:
                            op = dve.tensor_tensor(pr[:], pr[:], m1[:], ALU.mult)
                        elif i == 18:
                            op = dve.tensor_reduce(top[:], pr[:], AX.X, ALU.add)
                        elif i == 19:
                            op = dve.tensor_scalar(top[:], top[:], 1e-9, None, ALU.add)
                        elif i == 20:
                            op = dve.reciprocal(top[:], top[:])
                        elif i == 21:
                            dve.wait_ge(ow_r, TB * g + OW_0)
                            op = dve.tensor_tensor(wt[:], pr[:], wide(top), ALU.mult)
                        op.then_inc(r_dve, 1)

                def product(g, k, m):
                    s = NM * g + m
                    i = (k + m) % 2
                    if m == 0:
                        dve.wait_ge(o_w, TB * (g - 1) + O_0)
                    dve.wait_ge(s_w, s + 1 + S_0)
                    dve.wait_ge(h3_w, s + 1)
                    dve.tensor_tensor(hh[k][:, m, :], S[i][:], H3[i][:], ALU.mult).then_inc(hh_w, 1)

                def weigh(g, n):
                    q = TB * g + n
                    dve.wait_ge(o_w, q + 1 + O_0)
                    dve.wait_ge(sum_w, q + SUM_0)
                    if n == 0:
                        dve.wait_ge(r_dve, NCH * g + NCH + RD_0)
                    dve.tensor_tensor(weighted[:], OUT[n % 2][:].rearrange("p (e c) -> p e c", c=C),
                                      wt[:, n, :].unsqueeze(2).to_broadcast([P, NE, C]), ALU.mult).then_inc(ow_r, 1)

                def add_experts(g, n):
                    q = TB * g + n
                    dve.wait_ge(ow_r, q + 1 + OW_0)
                    dve.wait_ge(y_w, q + 1 - 4 + Y_0)
                    dve.tensor_reduce(summed[:, n, :], weighted[:].rearrange("p e c -> p c e"), AX.X, ALU.add).then_inc(sum_w, 1)

                def period(g, k, first, last):
                    for m in range(NM):
                        if m == 0:
                            routing(g, range(0, 2))
                        product(g, k, m)
                        if not first:
                            if m in (3, 5, 7, 9):
                                weigh(g - 1, (m - 3) // 2)
                            if m in (4, 6, 8, 10):
                                add_experts(g - 1, (m - 4) // 2)
                        if m >= 3:
                            routing(g, range(2 + (NCH - 2) * (m - 3) // 8, 2 + (NCH - 2) * (m - 2) // 8))
                        if not last and m == 2:
                            sum_squares(g + 1)
                        if not last and m == 4:
                            leave(g + 1, 1 - k)

                sum_squares(0)
                leave(0, 0)
                for j in range(NTI):
                    period(j, j % 2, j == 0, False)
                with dve.Fori(1, B) as b:
                    for j in range(NTI):
                        period(NTI * b + j, j % 2, False, False)
                period(NTI * B, 0, False, False)
                period(NTI * B + 1, 1, False, True)
                for n in range(TB):
                    weigh(NTI * B + 1, n)
                    add_experts(NTI * B + 1, n)

            @block.gpsimd
            def _(pool):
                pool.memset(half_neg[:], -0.5)
                pool.memset(eps[:], EPS)
                pool.drain().then_inc(su_pool, 1)
                pool.wait_ge(su_pool, 1)
                pool.wait_ge(f_pool, FP_0)

                def normed(g, k):
                    r = 5 * g + FP_0
                    pool.wait_ge(f_dve, 2 * g + 1 + FD_0)
                    pool.wait_ge(f_pool, r)
                    pool.tensor_tensor(mean[:], ssum[:], eps[:], ALU.add).then_inc(f_pool, 1)
                    pool.wait_ge(f_pool, r + 1)
                    pool.tensor_tensor(rstd[:], mean[:], half_neg[:], ALU.pow).then_inc(f_pool, 1)
                    pool.wait_ge(f_pool, r + 2)
                    pool.wait_ge(tp_w, g + TP_0)
                    pool.tensor_tensor(fd[:], x2[k][:].unsqueeze(2).to_broadcast([P, TB, 2, C]),
                                       rstd[:].unsqueeze(2).unsqueeze(3).to_broadcast([P, TB, 2, C]), ALU.mult).then_inc(f_pool, 1)

                def third_part(g, k):
                    pool.wait_ge(f_act, 4 * g + 4)
                    pool.tensor_tensor(f13[k][C:P], left[C:P], f2[k][C:P], ALU.subtract).then_inc(f_pool, 1)
                    pool.wait_ge(f_pool, 5 * g + 4 + FP_0)

                def residual(g, k):
                    pool.wait_ge(y_w, TB * (g - 1) + Y_0)
                    pool.tensor_tensor(res[k][:], x2[k][:], h2[k][:], ALU.add).then_inc(f_pool, 1)

                def output(g, k, n, pair):
                    q = TB * g + n
                    pool.wait_ge(sum_w, q + 1 + SUM_0)
                    if n == 0:
                        pool.wait_ge(stored[k], 16 * pair + 16)
                        pool.wait_ge(f_pool, 5 * g + 5 + FP_0)
                    pool.tensor_tensor(y[k][:, n, :], summed[:, n, :], res[k][:, n, :], ALU.add).then_inc(y_w, 1)

                def period(g, k, first, last, pair):
                    for m in range(NM):
                        if not last and m == 2:
                            normed(g + 1, 1 - k)
                        if not last and m == 5:
                            third_part(g + 1, 1 - k)
                        if not first and m in (5, 7, 9):
                            output(g - 1, 1 - k, (m - 5) // 2, pair)
                    if not first:
                        output(g - 1, 1 - k, TB - 1, pair)
                    if not last:
                        residual(g + 1, 1 - k)

                normed(0, 0)
                third_part(0, 0)
                residual(0, 0)
                for j in range(NTI):
                    period(j, j % 2, j == 0, False, (j - 1) // 2)
                with pool.Fori(1, B) as b:
                    for j in range(NTI):
                        period(NTI * b + j, j % 2, False, False, (NTI // 2) * b + (j - 1) // 2)
                period(NTI * B, 0, False, False, NTI * B // 2 - 1)
                period(NTI * B + 1, 1, False, True, NTI * B // 2)
                for n in range(TB):
                    output(NTI * B + 1, 1, n, NTI * B // 2)


def shape_constants():
    import numpy as np
    P, S, D, NE = 128, 16, 16, 8
    bf16 = mybir.dt.np(BF16)
    r = np.arange(P)
    selectors = np.zeros((6 * S, 2 * S, P), np.float32)
    for k in range(6 * S):
        selectors[k, k % (2 * S)] = 1
    part_signs = np.zeros((6 * S, 2), np.float32)
    part_signs[2 * S:, 0] = -1
    part_signs[4 * S:, 1] = -1
    sum_selector = np.zeros((P, P), np.float32)
    sum_selector[32 * (r // 32) + D, r] = 1
    inv_freq = 1.0 / 10000.0 ** (np.arange(0, D, 2, dtype=np.float32) / D)
    freqs = np.outer(np.arange(LT, dtype=np.float32), inv_freq)
    emb = np.concatenate([freqs, freqs], axis=-1).astype(np.float32)
    cos, sin = np.cos(emb).T, np.sin(emb).T.copy()
    sin[:D // 2] *= -1
    return {
        "ident": np.eye(P, dtype=np.float32), "ident_bf16": np.eye(P).astype(bf16), "selectors": selectors.astype(bf16),
        "part_signs": part_signs, "sum_selector": sum_selector,
        "mask_queries": np.where(r[None, :] > r[:, None], -1e30, 0).astype(bf16),
        "mask_keys": np.where(r[:, None] > r[None, :], -1e30, 0).astype(bf16),
        "rope_cos": np.tile(cos, (6, 1)), "rope_sin": np.tile(sin, (6, 1)),
        "expert_rank": np.tile(np.arange(NE, 0, -1, dtype=np.float32), (P, 4)),
    }


def laid_out(inputs):
    import numpy as np
    P = 128
    d = {n: np.asarray(a) for n, a in inputs.items()}
    d["L0_attn_b_in_w"] = d["L0_attn_b_in_w"][:, ::-1]
    d["L0_attn_b_out_w"] = d["L0_attn_b_out_w"][::-1]
    for n in ("wq", "wk"):
        w = d["L0_ffn_" + n]
        d[n + "_rotated"] = w.reshape(-1, 2, 8, C)[:, ::-1].reshape(w.shape)
    w1, w2, w3 = (d.pop("L0_ffn_" + n) for n in ("w1", "w2", "w3"))
    ne, hid = w1.shape[:2]
    per = P // (hid - P)
    groups = [range(a, min(a + per, ne)) for a in range(0, ne, per)]
    columns = np.zeros((C, 2, ne + len(groups), P), w1.dtype)
    rest = np.zeros((P, len(groups), per, C), w2.dtype)
    for k, w in enumerate((w1, w3)):
        columns[:, k, :ne] = w[:, :P].transpose(2, 0, 1)
        for r, group in enumerate(groups):
            for a, e in enumerate(group):
                rows = slice(a * (hid - P), (a + 1) * (hid - P))
                columns[:, k, ne + r, rows] = w[e, P:].T
                rest[rows, r, a] = w2[e, :, P:].T
    d["w13_columns"] = columns.reshape(C, -1)
    d["router_columns"] = d.pop("L0_ffn_router_w").T
    d["w2_main"] = w2[:, :, :P].transpose(2, 0, 1)
    d["w2_rest"] = rest.reshape(P, len(groups), per * C)
    return d


def kernel(**inputs):
    import numpy as _np
    import concourse.bacc as _bacc
    from concourse import mybir as _mybir
    from concourse.bass_utils import run_bass_kernel_spmd as _run

    nc = _bacc.Bacc("TRN2", target_bir_lowering=False, num_devices=1)
    arrays, d = {}, {}
    for name, a in {**laid_out(inputs), **shape_constants()}.items():
        a = _np.ascontiguousarray(a)
        arrays[f"in_{name}_dram"] = a
        d[name] = nc.dram_tensor(f"in_{name}_dram", a.shape, _mybir.dt.from_np(a.dtype), kind="ExternalInput").ap()
    for name in ("h1", "h2", "x2"):
        d[name] = nc.dram_tensor(f"scratch_{name}", (B, LT, C), F32, kind="Internal").ap()
    d["out"] = nc.dram_tensor("out_0_dram", (B, L, C), F32, kind="ExternalOutput").ap()
    tok_phase(nc, d)
    mamba_phase(nc, d)
    attn_phase(nc, d)
    moe_phase(nc, d)
    r = _run(nc, [arrays], core_ids=[0])
    return r.results[0]["out_0_dram"]
```

```python
from contextlib import ExitStack

import concourse.bass as bass
from concourse import mybir

F32 = mybir.dt.float32
BF16 = mybir.dt.bfloat16
ALU = mybir.AluOpType
ACT = mybir.ActivationFunctionType
AX = mybir.AxisListType
B, C, HW = 8, 64, 56
L = HW * HW + 1
LT = 3200


def tok_phase(nc, d):
    WP = HW + 2
    AREA = WP * WP
    ROWS = 8
    CH = HW // ROWS
    N = ROWS * HW
    NSUB = 4
    SUB = N // NSUB
    PAIRS = [(0, 3, 0, 0, 0), (1, 4, 0, 0, 1), (2, 5, 0, 0, 2), (6, 7, 1, 2, 0), (8, None, 1, 2, 2)]
    NP = len(PAIRS)
    PER = 2 * CH
    h1 = d["h1"]
    x = d["x"]
    b1v = d["L0_tok_b1"].rearrange("(c a) -> c a", a=1)
    b3v = d["L0_tok_b3"].rearrange("(a c) -> a c", a=1)
    with ExitStack() as ctx:
        def sb(n, s, t=F32):
            return ctx.enter_context(nc.sbuf_tensor("tok_" + n, s, t))

        def sem(n):
            return ctx.enter_context(nc.semaphore("tok_" + n))

        img = [[sb(f"img{h}{k}", [128, AREA]) for k in range(2)] for h in range(2)]
        w1 = sb("w1", [128, NP, 128])
        w2 = sb("w2", [128, NP, 128])
        w2_part2 = sb("w2_part2", [C, NP, 128], BF16)
        w2_12 = sb("w2_12", [128, NP, 128], BF16)
        w2_31 = sb("w2_31", [128, NP, 128], BF16)
        w3 = sb("w3", [128, NP, C])
        b1 = sb("b1", [128, 1])
        b2 = sb("b2", [128, NP])
        b3 = sb("b3", [128, C])
        zero = sb("zero", [64, C])
        hid = [sb(f"hid{i}", [128, N]) for i in range(2)]
        left = sb("left", [128, N])
        hid_1 = [sb(f"hid_1{i}", [128, N], BF16) for i in range(2)]
        hid_2 = [sb(f"hid_2{i}", [128, N], BF16) for i in range(2)]
        hid_13 = [sb(f"hid_13{i}", [128, N], BF16) for i in range(2)]
        gate = [sb(f"gate{i}", [128, NP, N]) for i in range(2)]
        gated = [sb(f"gated{i}", [128, NP, N]) for i in range(2)]
        outs = [sb(f"outs{i}", [SUB, NSUB, C]) for i in range(2)]
        ps_hid = [ctx.enter_context(nc.psum_tensor(f"tok_ph{i}", [128, 512], F32)) for i in range(2)]
        ps_gate = [ctx.enter_context(nc.psum_tensor(f"tok_pg{i}", [128, 512], F32)) for i in range(4)]
        ps_out = [ctx.enter_context(nc.psum_tensor(f"tok_po{i}", [128, 512], F32)) for i in range(2)]

        cleared = sem("cleared")
        weights_in = sem("weights_in")
        w2_ready = sem("w2_ready")
        images_in = [sem(f"images_in{h}") for h in range(2)]
        conv_done = sem("conv_done")
        hid_act = sem("hid_act")
        hid_dve = sem("hid_dve")
        w2_done = sem("w2_done")
        gate_done = sem("gate_done")
        gated_done = sem("gated_done")
        w3_done = sem("w3_done")
        out_ready = sem("out_ready")
        stored = [sem(f"stored{h}") for h in range(2)]
        edges = sem("edges")

        def img_view(half, k):
            return img[half][k][:].rearrange("p (r w) -> p r w", w=WP)

        def tap_view(half, p, ch):
            _, _, k, ki, kj = PAIRS[p]
            r = ch * ROWS + ki
            return img_view(half, k)[:, r:r + ROWS, kj:kj + HW]

        nw = 7
        with nc.Block() as block:
            @block.sync
            def _(sp):
                for dst, src in ((w1, "tok_w1_pairs"), (w2, "tok_w2_pairs"), (w3, "tok_w3_pairs"), (b2, "tok_b2_pairs")):
                    sp.dma_start(dst[:], d[src]).then_inc(weights_in, 16)
                sp.dma_start(b1[0:C], b1v).then_inc(weights_in, 16)
                sp.dma_start(b1[C:], b1v).then_inc(weights_in, 16)
                sp.dma_start(b3[:], b3v.to_broadcast([128, C])).then_inc(weights_in, 16)
                sp.wait_ge(cleared, 1)
                sp.dma_start(h1[:, 0, :], d["cls_tok"].rearrange("a b c -> (a b) c").to_broadcast([B, C])).then_inc(edges, 16)
                for b in range(B):
                    sp.dma_start(h1[b, 1 + HW * HW:LT, :], zero[0:LT - 1 - HW * HW, :]).then_inc(edges, 16)
                with sp.Fori(0, B // 2) as i:
                    for k in range(PER):
                        g = i * PER + k
                        sp.wait_ge(out_ready, g + 1 + 2 * CH)
                        row = (i * 2 + k // CH) * LT + (1 + (k % CH) * N)
                        dst = h1.rearrange("b t c -> (b t) c")[bass.ds(row, N), :]
                        sp.dma_start(dst.rearrange("(s p) c -> p s c", p=SUB), outs[k % 2][:]).then_inc(stored[k % 2], 16)
                for buf in range(2):
                    sp.wait_ge(stored[buf], 16 + 16 * B * CH // 2)
                sp.wait_ge(edges, 16 * (B + 1))

            @block.tensor
            def _(pe):
                pe.wait_ge(weights_in, 16 * nw)
                pe.wait_ge(w2_ready, 7)

                def conv(i, g, half, ch, k):
                    if ch == 0:
                        pe.wait_ge(images_in[half], (i + 1) * 64)
                    pe.wait_ge(hid_act, 4 * g + 2)
                    for p in range(NP):
                        mm = pe.matmul(ps_hid[k % 2][:, 0:N], w1[:, p, :], tap_view(half, p, ch),
                                       start=p == 0, stop=p == NP - 1)
                    mm.then_inc(conv_done, 1)

                def gates(g, k):
                    pe.wait_ge(hid_act, 4 * g + 4 + 8)
                    pe.wait_ge(hid_dve, 2 * g + 2 + 4)
                    for p in range(NP):
                        pe.wait_ge(gate_done, g * NP + p + 1)
                        for a, (w, h) in enumerate(((w2_12, hid_1), (w2_12, hid_2), (w2_31, hid_13))):
                            mm = pe.matmul(ps_gate[(k * NP + p) % 4][:, 0:N], w[:, p, :], h[k % 2][:],
                                           start=a == 0, stop=a == 2)
                        mm.then_inc(w2_done, 1)

                def outputs(g, k):
                    pe.wait_ge(gated_done, g * NP + NP + 2 * NP)
                    pe.wait_ge(out_ready, g + 1 + 2 * CH - 2)
                    for s in range(NSUB):
                        for p in range(NP):
                            mm = pe.matmul(ps_out[k % 2][0:SUB, s * C:(s + 1) * C],
                                           gated[k % 2][:, p, s * SUB:(s + 1) * SUB], w3[:, p, :],
                                           start=p == 0, stop=p == NP - 1)
                    mm.then_inc(w3_done, 1)

                with pe.Fori(0, B // 2) as i:
                    for k in range(PER + 1):
                        if k < PER:
                            conv(i, i * PER + k, k // CH, k % CH, k)
                        if k > 0:
                            outputs(i * PER + (k - 1), k - 1)
                        if k < PER:
                            gates(i * PER + k, k)

            @block.scalar
            def _(act):
                act.wait_ge(weights_in, 16 * nw)
                with act.Fori(0, B // 2) as i:
                    for k in range(PER):
                        g = i * PER + k
                        act.wait_ge(conv_done, g + 1)
                        act.wait_ge(w2_done, g * NP + NP)
                        act.wait_ge(hid_dve, 2 * g + 1)
                        for dst in (hid, hid_1):
                            act.activation(dst[k % 2][:], ps_hid[k % 2][:, 0:N], ACT.Relu, bias=b1[:]).then_inc(hid_act, 1)
                        act.wait_ge(hid_act, 4 * g + 2 + 8)
                        act.activation(hid_13[k % 2][0:C], hid_1[k % 2][0:C], ACT.Copy).then_inc(hid_act, 1)
                        act.wait_ge(hid_dve, 2 * g + 1 + 4)
                        act.activation(hid_2[k % 2][:], left[:], ACT.Copy).then_inc(hid_act, 1)
                        for p in range(NP):
                            act.wait_ge(w2_done, g * NP + p + 1 + 2 * NP)
                            if p == 0:
                                act.wait_ge(gated_done, g * NP + NP)
                            act.activation(gate[k % 2][:, p, :], ps_gate[(k * NP + p) % 4][:, 0:N], ACT.Sigmoid,
                                           bias=b2[:, p:p + 1]).then_inc(gate_done, 1)

            @block.vector
            def _(dve):
                dve.memset(zero[:], 0.0)
                dve.sem_inc(hid_act, 8)
                dve.sem_inc(hid_dve, 4)
                dve.sem_inc(w2_done, 2 * NP)
                dve.sem_inc(gate_done, 4)
                dve.sem_inc(gated_done, 2 * NP)
                dve.sem_inc(w3_done, 2)
                dve.sem_inc(stored[0], 16)
                dve.sem_inc(stored[1], 16)
                dve.drain().then_inc(cleared, 1)

                def clear(half):
                    dve.memset(img[half][0][:], 0.0)
                    dve.memset(img[half][1][:], 0.0)
                    dve.drain().then_inc(out_ready, CH)

                clear(0)
                dve.wait_ge(weights_in, 16 * nw)
                dve.tensor_copy(w2_12[0:C], w2[0:C]).then_inc(w2_ready, 1)
                dve.tensor_copy(w2_31[C:], w2[C:]).then_inc(w2_ready, 1)
                dve.wait_ge(w2_ready, 2)
                dve.tensor_tensor(w2[0:C], w2[0:C], w2_12[0:C], ALU.subtract).then_inc(w2_ready, 1)
                dve.tensor_tensor(w2[C:], w2[C:], w2_31[C:], ALU.subtract).then_inc(w2_ready, 1)
                dve.wait_ge(w2_ready, 4)
                dve.tensor_copy(w2_12[C:], w2[C:]).then_inc(w2_ready, 1)
                dve.tensor_copy(w2_part2[:], w2[0:C]).then_inc(w2_ready, 1)
                dve.wait_ge(w2_ready, 6)
                dve.tensor_tensor(w2_31[0:C], w2[0:C], w2_part2[:], ALU.subtract).then_inc(w2_ready, 1)
                clear(1)

                def parts(g, k):
                    dve.wait_ge(hid_act, 4 * g + 2 + 8)
                    dve.wait_ge(hid_dve, 2 * g + 4)
                    dve.tensor_tensor(left[:], hid[k % 2][:], hid_1[k % 2][:], ALU.subtract).then_inc(hid_dve, 1)
                    dve.wait_ge(hid_act, 4 * g + 4 + 8)
                    dve.tensor_tensor(hid_13[k % 2][C:], left[C:], hid_2[k % 2][C:], ALU.subtract).then_inc(hid_dve, 1)

                def evac(i, g, k):
                    dve.wait_ge(w3_done, g + 1 + 2)
                    dve.wait_ge(stored[k % 2], (i * CH + (k // 2 + 1)) * 16)
                    dve.tensor_tensor(outs[k % 2][:], ps_out[k % 2][0:SUB, 0:NSUB * C].rearrange("p (s c) -> p s c", c=C),
                                      b3[0:SUB].unsqueeze(1).to_broadcast([SUB, NSUB, C]), ALU.add).then_inc(out_ready, 1)

                with dve.Fori(0, B // 2) as i:
                    for k in range(PER + 1):
                        g = i * PER + k
                        if k < PER:
                            parts(g, k)
                            for p in range(NP):
                                dve.wait_ge(gate_done, g * NP + p + 1 + 4)
                                if p == 0:
                                    dve.wait_ge(w3_done, g + 1)
                                dve.tensor_tensor(gated[k % 2][:, p, :].rearrange("p (r w) -> p r w", w=HW),
                                                  gate[k % 2][:, p, :].rearrange("p (r w) -> p r w", w=HW),
                                                  tap_view(k // CH, p, k % CH), ALU.mult).then_inc(gated_done, 1)
                        if k > 0:
                            evac(i, i * PER + (k - 1), k - 1)

            @block.gpsimd
            def _(pool):
                with pool.Fori(0, B // 2) as i:
                    for half in range(2):
                        pool.wait_ge(out_ready, (i * 2 + half) * CH + CH)
                        src = x[bass.ds(i * 2 + half, 1)].rearrange("a c h w -> (a c) h w")
                        a, c = img_view(half, 0), img_view(half, 1)
                        pool.dma_start(a[0:64, 1:57, 1:57], src).then_inc(images_in[half], 16)
                        pool.dma_start(a[64:128, 0:56, 1:57], src).then_inc(images_in[half], 16)
                        pool.dma_start(c[0:64, 1:57, 1:57], src).then_inc(images_in[half], 16)
                        pool.dma_start(c[64:128, 1:57, 0:56], src).then_inc(images_in[half], 16)


def mamba_phase(nc, d):
    P = 128
    S = 16
    N = 800
    Q = LT // N
    U = 2 * Q
    J = 8
    NT = N // J
    H2 = N // 2
    KB = 8
    LAG = 5
    EPS = 1e-5
    h1r = d["h1"].rearrange("b t c -> (b t) c")
    h2r = d["h2"].rearrange("b t c -> (b t) c")
    with ExitStack() as ctx:
        def sb(n, s, t=F32):
            return ctx.enter_context(nc.sbuf_tensor("mb_" + n, s, t))

        def sem(n):
            return ctx.enter_context(nc.semaphore("mb_" + n))

        def ps(n):
            return ctx.enter_context(nc.psum_tensor("mb_" + n, [P, 2, 512], F32))

        ident = sb("ident", [P, P])
        sel = sb("sel", [96, 2 * S, P], BF16)
        part23 = sb("part23", [96, 2])
        raw_in = [sb(f"raw_in{k}", [P, 2, C]) for k in range(2)]
        raw_conv = [sb(f"raw_conv{k}", [P, 4]) for k in range(2)]
        raw_bc = [sb(f"raw_bc{k}", [96, P]) for k in range(2)]
        raw_dtx = [sb(f"raw_dtx{k}", [4, P]) for k in range(2)]
        raw_dtw = [sb(f"raw_dtw{k}", [P, 4]) for k in range(2)]
        raw_out = [sb(f"raw_out{k}", [C, P]) for k in range(2)]
        taps = [sb(f"taps{k}", [P, 3, 2, C]) for k in range(2)]
        conv_b = [sb(f"conv_b{k}", [P, 1]) for k in range(2)]
        dt_b = [sb(f"dt_b{k}", [P, 1]) for k in range(2)]
        skip = [sb(f"skip{k}", [P, 1]) for k in range(2)]
        a_log = [sb(f"a_log{k}", [P, S]) for k in range(2)]
        a_exp = [sb(f"a_exp{k}", [P, S]) for k in range(2)]
        a_neg = [sb(f"a_neg{k}", [P, S]) for k in range(2)]
        w_in = [sb(f"w_in{k}", [P, 3, P]) for k in range(2)]
        w_bc = [sb(f"w_bc{k}", [P, 96]) for k in range(2)]
        w_dt4 = [sb(f"w_dt4{k}", [4, P]) for k in range(2)]
        w_dt = [sb(f"w_dt{k}", [P, P]) for k in range(2)]
        w_out = [sb(f"w_out{k}", [P, C]) for k in range(2)]

        xin = [sb(f"xin{k}", [NT, J, C]) for k in range(2)]
        cen = sb("cen", [NT, J, C])
        sq = sb("sq", [NT, J, C])
        st = sb("st", [NT, 6, J])
        half_neg = sb("half_neg", [NT, J])
        norm_consts = sb("norm_consts", [NT, 3, J])
        zero = sb("zero", [P, 1])
        gg = sb("gg", [NT, J, 2, C])
        hg = [sb(f"hg{k}", [NT, J, C]) for k in range(2)]
        res = [sb(f"res{k}", [NT, J, C]) for k in range(2)]
        G = sb("G", [P, N + 4])
        xc = [sb(f"xc{k}", [P, N]) for k in range(2)]
        sz = [sb(f"sz{k}", [P, N]) for k in range(4)]
        dt = [sb(f"dt{k}", [P, N]) for k in range(2)]
        du = [sb(f"du{k}", [P, N]) for k in range(2)]
        sp1 = sb("sp1", [P, N])
        sp2 = sb("sp2", [P, N])
        sp3 = sb("sp3", [P, N])
        relu = sb("relu", [P, N])
        part1 = sb("part1", [96, N], BF16)
        rest1 = sb("rest1", [96, N])
        part2 = sb("part2", [96, N], BF16)
        bc = [sb(f"bc{k}", [96, N], BF16) for k in range(2)]
        dA = [sb(f"dA{k}", [P, N]) for k in range(4)]
        dB = [sb(f"dB{k}", [P, N]) for k in range(2)]
        hs = [sb(f"hs{k}", [P, N]) for k in range(KB)]
        cs = [sb(f"cs{k}", [P, N]) for k in range(KB)]
        hc = [sb(f"hc{k}", [P, N]) for k in range(KB)]
        carry = [sb(f"carry{k}", [P, S]) for k in range(2)]
        yd = sb("yd", [P, N])
        yz = [sb(f"yz{k}", [P, N]) for k in range(2)]
        PB, PC, PY, PP = ps("PB"), ps("PC"), ps("PY"), ps("PP")

        names = {}

        def S_(n):
            if n not in names:
                names[n] = sem(n)
            return names[n]

        w_loaded = S_("w_loaded")
        x_loaded = [S_("x_loaded0"), S_("x_loaded1")]
        res_stored = [S_("res_stored0"), S_("res_stored1")]
        su_dve, su_pe, su_act = S_("su_dve"), S_("su_pe"), S_("su_act")
        su_pool = S_("su_pool")
        ln_dve, ln_pool = S_("ln_dve"), S_("ln_pool")
        pp_w = S_("pp_w")
        g_ready = S_("g_ready")
        act_prep = S_("act_prep")
        part2_r = S_("part2_r")
        dve_prep = S_("dve_prep")
        pool_prep = S_("pool_prep")
        o_w = S_("o_w")
        out_done = S_("out_done")
        b_w, c_w, y_w = S_("b_w"), S_("c_w"), S_("y_w")
        dA_r, cs_r = S_("dA_r"), S_("cs_r")
        dB_r, h_r = S_("dB_r"), S_("h_r")
        car_r, hc_r = S_("car_r"), S_("hc_r")
        yd_r, yz_r = S_("yd_r"), S_("yz_r")

        def halves(t):
            return t.rearrange("p (h n) -> p h n", h=2)

        def tasks(b, u):
            return b * (U * 4 + Q) + (4 * u + u // 2 + 1)

        wl = 0
        with nc.Block() as block:
            @block.sync
            def _(sp):
                nonlocal wl
                def load(dst, src):
                    nonlocal wl
                    sp.dma_start(dst, src).then_inc(w_loaded, 16)
                    wl += 16
                load(ident[:], d["ident"])
                load(sel[:], d["selectors"])
                load(part23[:], d["part_signs"])
                for k, z in enumerate("fb"):
                    w = lambda n: d[f"L0_attn_{z}_{n}"]
                    load(raw_in[k][:], w("in_w").rearrange("(x p) c -> p x c", x=2))
                    load(raw_conv[k][:], w("conv_w"))
                    for r in range(3):
                        load(raw_bc[k][32 * r:32 * r + 32, :], w("xproj_w")[4:36, :])
                    load(raw_dtx[k][:], w("xproj_w")[0:4, :])
                    load(raw_dtw[k][:], w("dt_w"))
                    load(raw_out[k][:], w("out_w"))
                    load(a_log[k][:], w("A_log"))
                    for t, n in ((conv_b, "conv_b"), (dt_b, "dt_b"), (skip, "D")):
                        load(t[k][:], w(n).rearrange("(p a) -> p a", a=1))

                def load_x(b, q):
                    c = b * Q + q
                    sp.wait_ge(ln_pool, c * 8 + 8)
                    sp.dma_start(xin[q % 2][:], h1r[bass.ds((b * Q + q) * N, N), :].rearrange("(p j) c -> p j c", j=J)
                                 ).then_inc(x_loaded[q % 2], 16)

                def store(b, q):
                    c = b * Q + q
                    sp.wait_ge(out_done, c + 1 + 2)
                    sp.dma_start(h2r[bass.ds((b * Q + q) * N, N), :].rearrange("(p j) c -> p j c", j=J), res[q % 2][:]
                                 ).then_inc(res_stored[q % 2], 16)

                def image(b, first, last):
                    for q in range(Q):
                        if q < Q - 1:
                            load_x(b, q + 1)
                        elif not last:
                            load_x(b + 1, 0)
                        if q > 0:
                            store(b, q - 1)
                        elif not first:
                            store(b - 1, Q - 1)

                load_x(0, 0)
                image(0, True, False)
                with sp.Fori(1, B - 1) as b:
                    image(b, False, False)
                image(B - 1, False, True)
                store(B - 1, Q - 1)
                for k in range(2):
                    sp.wait_ge(res_stored[k], 16 * (B * Q // 2 + 1))

            @block.tensor
            def _(pe):
                pe.wait_ge(w_loaded, wl)
                for k in range(2):
                    pe.wait_ge(su_dve, 6 if k == 0 else 17)
                    for r in range(3):
                        pe.transpose(PB[:, 0, r * P:(r + 1) * P], taps[k][:, r].rearrange("p a c -> p (a c)"), ident[:])
                    pe.transpose(PC[:, 0, 0:96], raw_bc[k][:], ident[0:96, 0:96])
                    pe.transpose(PC[:, 0, 96:96 + C], raw_out[k][:], ident[0:C, 0:C])
                    pe.transpose(PC[0:4, 1, 0:P], raw_dtw[k][:], ident[:]).then_inc(su_pe, 1)
                    pe.wait_ge(su_dve, 12 + 5 * k + 4)
                    pe.matmul(PP[:, 0, 0:P], raw_dtx[k][:], w_dt4[k][:], start=True, stop=True).then_inc(su_pe, 1)
                pe.wait_ge(su_dve, 22)

                def turn(b, q):
                    c = b * Q + q
                    pe.wait_ge(ln_pool, c * 8 + 7 + 16)
                    pe.wait_ge(out_done, c + 1)
                    pe.wait_ge(dve_prep, (b * U + 2 * q) * 3 + 3)
                    pe.wait_ge(act_prep, (b * U + 2 * q) * 6 + 4)
                    for j in range(J):
                        mm = pe.transpose(PP[:, j // 4, (j % 4) * NT:(j % 4 + 1) * NT],
                                          gg[:, j].rearrange("p a c -> p (a c)"), ident[0:NT, 0:NT])
                    mm.then_inc(pp_w, 1)

                def prep_z(b, u):
                    c, k = b * Q + u // 2, u % 2
                    pe.wait_ge(g_ready, c * 3 + 3 + 3)
                    if u % 2:
                        pe.wait_ge(dve_prep, (b * U + u) * 3 + 3)
                        pe.wait_ge(act_prep, (b * U + u) * 6 + 4)
                    for h in range(2):
                        mm = pe.matmul(PP[:, h, 0:H2], w_in[k][:, 2, :], G[:, 3 + h * H2:3 + (h + 1) * H2],
                                       start=True, stop=True)
                    mm.then_inc(pp_w, 1)

                def prep_k(b, u):
                    k = u % 2
                    pe.wait_ge(act_prep, (b * U + u) * 6 + 1 + 6)
                    for h in range(2):
                        for r in range(2):
                            at = 3 - 2 * r + h * H2
                            mm = pe.matmul(PP[:, h, 0:H2], w_in[k][:, r, :], G[:, at:at + H2], start=r == 0, stop=r == 1)
                    mm.then_inc(pp_w, 1)

                def prep_x(b, u):
                    k = u % 2
                    pe.wait_ge(act_prep, (b * U + u) * 6 + 2 + 6)
                    for h in range(2):
                        mm = pe.matmul(PP[0:96, h, 0:H2], w_bc[k][:], xc[k][:, h * H2:(h + 1) * H2], start=True, stop=True)
                    mm.then_inc(pp_w, 1)

                def prep_d(b, u):
                    k = u % 2
                    pe.wait_ge(dve_prep, (b * U + u) * 3 + 1 + 3)
                    pe.wait_ge(act_prep, (b * U + u) * 6 + 3 + 6)
                    for h in range(2):
                        mm = pe.matmul(PP[:, h, 0:H2], w_dt[k][:], xc[k][:, h * H2:(h + 1) * H2], start=True, stop=True)
                    mm.then_inc(pp_w, 1)

                def project(b, q, ahead=2):
                    c = b * Q + q
                    pe.wait_ge(yz_r, 2 * c + 2 + 4)
                    pe.wait_ge(dve_prep, (b * U + (2 * q + 2 + ahead)) * 3 + 3)
                    pe.wait_ge(act_prep, (b * U + (2 * q + 1 + ahead)) * 6 + 4 + 6)
                    for j in range(J):
                        for k in range(2):
                            mm = pe.matmul(PP[0:NT, 0, j * C:(j + 1) * C],
                                           yz[k][:].rearrange("p (t j) -> p j t", j=J)[:, j, :], w_out[k][:],
                                           start=k == 0, stop=k == 1)
                    mm.then_inc(o_w, 1)

                def row(b, u, n, which):
                    v, k = b * U * S + (u * S + n), u % 2
                    if which == 0:
                        pe.wait_ge(dB_r, v + 2 * S)
                        dst, out = PB, b_w
                    else:
                        pe.wait_ge(cs_r, v + 1)
                        dst, out = PC, c_w
                    for h in range(2):
                        mm = pe.matmul(dst[:, h, 0:H2], sel[:, which * S + n, :], bc[k][:, h * H2:(h + 1) * H2],
                                       start=True, stop=True)
                    mm.then_inc(out, 1)

                def add_state(b, u, n):
                    v = b * U * S + (u * S + n)
                    pe.wait_ge(hc_r, v + 1 + KB)
                    if n == 0:
                        pe.wait_ge(yd_r, b * U + (u + 2))
                    for h in range(2):
                        mm = pe.matmul(PY[:, h, 0:H2], ident[:], hc[n % KB][:, h * H2:(h + 1) * H2],
                                       start=n == 0, stop=n == S - 1)
                    mm.then_inc(y_w, 1)

                def unit(b, u, first, last):
                    for n in range(S):
                        if n == 0:
                            pe.wait_ge(dve_prep, (b * U + u) * 3 + 2 + 3)
                        row(b, u, n, 0)
                        row(b, u, n, 1)
                        if n > LAG:
                            if n == LAG + 1:
                                add_state(b, u, 0)
                            add_state(b, u, n - LAG)
                        elif n < LAG and u > 0:
                            add_state(b, u - 1, S + n - LAG)
                        elif n < LAG and not first:
                            add_state(b - 1, U - 1, S + n - LAG)
                        nb, nu = (b, u + 1) if u < U - 1 else (b + 1, 0)
                        if not (last and u == U - 1):
                            if n == 2 and nu % 2 == 0:
                                turn(nb, nu // 2)
                            if n == 4:
                                prep_z(nb, nu)
                            if n == 5:
                                prep_k(nb, nu)
                            if n == 6:
                                prep_x(nb, nu)
                            if n == 8:
                                prep_d(nb, nu)
                        if n == 14 and u % 2 == 0:
                            if u > 0:
                                project(b, u // 2 - 1)
                            elif not first:
                                project(b - 1, Q - 1)

                turn(0, 0)
                prep_z(0, 0)
                prep_k(0, 0)
                prep_x(0, 0)
                prep_d(0, 0)
                for u in range(U):
                    unit(0, u, True, False)
                with pe.Fori(1, B - 1) as b:
                    for u in range(U):
                        unit(b, u, False, False)
                for u in range(U):
                    unit(B - 1, u, False, True)
                for n in range(LAG):
                    add_state(B - 1, U - 1, S - LAG + n)
                project(B - 1, Q - 1, 0)

            @block.scalar
            def _(act):
                act.wait_ge(w_loaded, wl)
                for k in range(2):
                    act.activation(a_exp[k][:], a_log[k][:], ACT.Exp).then_inc(su_act, 1)
                act.wait_ge(su_dve, 24)

                def silus_z(b, u):
                    k, w = u % 2, b * U + u
                    act.wait_ge(pp_w, tasks(b, u) + 1)
                    act.wait_ge(yz_r, w + 1)
                    act.activation(halves(sz[u % 4][:]), PP[:, :, 0:H2], ACT.Silu).then_inc(act_prep, 1)

                def silus_x(b, u):
                    k, w = u % 2, b * U + u
                    act.wait_ge(pp_w, tasks(b, u) + 2)
                    act.wait_ge(yd_r, w + 1)
                    act.activation(halves(xc[k][:]), PP[:, :, 0:H2], ACT.Silu, bias=conv_b[k][:]).then_inc(act_prep, 1)

                def first_part(b, u):
                    w = b * U + u
                    act.wait_ge(pp_w, tasks(b, u) + 3)
                    act.wait_ge(dve_prep, w * 3 + 1 + 1)
                    act.activation(halves(part1[:]), PP[0:96, :, 0:H2], ACT.Copy).then_inc(act_prep, 1)

                def second_part(b, u):
                    w = b * U + u
                    act.wait_ge(dve_prep, w * 3 + 1 + 3)
                    act.activation(part2[:], rest1[:], ACT.Copy).then_inc(part2_r, 1)

                def softplus(b, u, step):
                    k, w = u % 2, b * U + u
                    if step == 0:
                        act.wait_ge(pp_w, tasks(b, u) + 4)
                        act.wait_ge(act_prep, w * 6 + 5)
                        act.activation(halves(sp1[:]), PP[:, :, 0:H2], ACT.Abs, bias=dt_b[k][:]).then_inc(act_prep, 1)
                    if step == 1:
                        act.wait_ge(act_prep, w * 6 + 4 + 6)
                        act.activation(sp2[:], sp1[:], ACT.Exp, scale=-1.0).then_inc(act_prep, 1)
                    if step == 2:
                        act.wait_ge(act_prep, w * 6 + 5 + 6)
                        act.wait_ge(pool_prep, w * 2 + 1)
                        act.activation(sp3[:], sp2[:], ACT.Ln, bias=1.0).then_inc(act_prep, 1)

                def decay(b, u, n):
                    v, k = b * U * S + (u * S + n), u % 2
                    if n == 0:
                        act.wait_ge(pool_prep, (b * U + u) * 2 + 1 + 2)
                    act.wait_ge(h_r, v + 1 - 4 + KB)
                    act.activation(dA[n % 4][:], dt[k][:], ACT.Exp,
                                   scale=a_neg[k][:, n:n + 1]).then_inc(dA_r, 1)

                def copy_c(b, u, n):
                    v = b * U * S + (u * S + n)
                    act.wait_ge(c_w, v + 1 + 2 * S)
                    act.wait_ge(hc_r, v + 1)
                    act.activation(halves(cs[n % KB][:]), PC[:, :, 0:H2], ACT.Copy).then_inc(cs_r, 1)

                def unit(b, u, last):
                    nb, nu = (b, u + 1) if u < U - 1 else (b + 1, 0)
                    more = not (last and u == U - 1)
                    for n in range(S):
                        decay(b, u, n)
                        if more and n == 5:
                            silus_z(nb, nu)
                        copy_c(b, u, n)
                        if more and n == 5:
                            silus_x(nb, nu)
                        if more and n == 6:
                            first_part(nb, nu)
                        if more and n == 7:
                            second_part(nb, nu)
                        for i in range(3):
                            if more and n == 9 + i:
                                softplus(nb, nu, i)

                silus_z(0, 0)
                silus_x(0, 0)
                first_part(0, 0)
                second_part(0, 0)
                for i in range(3):
                    softplus(0, 0, i)
                for u in range(U):
                    unit(0, u, False)
                with act.Fori(1, B - 1) as b:
                    for u in range(U):
                        unit(b, u, False)
                for u in range(U):
                    unit(B - 1, u, True)

            @block.vector
            def _(dve):
                for s_, n_ in ((out_done, 2), (ln_pool, 16), (act_prep, 6), (dve_prep, 3), (pool_prep, 2), (part2_r, 1), (yd_r, 2),
                               (yz_r, 4), (o_w, 1), (c_w, 2 * S), (dB_r, 2 * S), (dA_r, 2 * S), (cs_r, 1), (h_r, KB),
                               (hc_r, KB), (car_r, 2 * S), (y_w, KB), (res_stored[0], 16), (res_stored[1], 16)):
                    dve.sem_inc(s_, n_)
                dve.memset(G[:], 0.0).then_inc(g_ready, 3)
                dve.wait_ge(w_loaded, wl)
                for k in range(2):
                    for r in range(2):
                        for a in range(2):
                            i = 3 - (2 * r + a)
                            dve.tensor_scalar(taps[k][:, r, a, :], raw_in[k][:, 0, :], raw_conv[k][:, i:i + 1], None,
                                              ALU.mult).then_inc(su_dve, 1)
                    dve.tensor_copy(taps[k][:, 2, 0, :], raw_in[k][:, 1, :]).then_inc(su_dve, 1)
                    dve.memset(taps[k][:, 2, 1, :], 0.0).then_inc(su_dve, 1)
                for k in range(2):
                    dve.wait_ge(su_pe, 2 * k + 1)
                    dve.tensor_copy(w_in[k][:].rearrange("p r d -> p (r d)"), PB[:, 0, 0:3 * P]).then_inc(su_dve, 1)
                    dve.tensor_copy(w_bc[k][:], PC[:, 0, 0:96]).then_inc(su_dve, 1)
                    dve.tensor_copy(w_out[k][:], PC[:, 0, 96:96 + C]).then_inc(su_dve, 1)
                    dve.tensor_copy(w_dt4[k][:], PC[0:4, 1, 0:P]).then_inc(su_dve, 1)
                    dve.wait_ge(su_pe, 2 * k + 2)
                    dve.tensor_copy(w_dt[k][:], PP[:, 0, 0:P]).then_inc(su_dve, 1)
                dve.wait_ge(su_act, 2)
                for k in range(2):
                    dve.tensor_scalar(a_neg[k][:], a_exp[k][:], -1.0, None, ALU.mult).then_inc(su_dve, 1)

                def ln_sum(b, q):
                    c = b * Q + q
                    dve.wait_ge(x_loaded[q % 2], (b * (Q // 2) + (q // 2 + 1)) * 16)
                    dve.wait_ge(ln_pool, c * 8 + 16)
                    dve.tensor_reduce(st[:, 0, :], xin[q % 2][:], AX.X, ALU.add).then_inc(ln_dve, 1)

                def ln_var(b, q):
                    c = b * Q + q
                    dve.wait_ge(ln_pool, c * 8 + 3 + 16)
                    dve.tensor_reduce(st[:, 2, :], sq[:], AX.X, ALU.add).then_inc(ln_dve, 1)

                def take_g(b, q):
                    c = b * Q + q
                    dve.wait_ge(pp_w, tasks(b, 2 * q))
                    dve.wait_ge(g_ready, c * 3 + 3)
                    if q == 0:
                        dve.memset(G[:, 0:4], 0.0).then_inc(g_ready, 1)
                    else:
                        dve.tensor_copy(G[:, 0:4], G[:, N:N + 4]).then_inc(g_ready, 1)
                    dve.wait_ge(g_ready, c * 3 + 1 + 3)
                    for part in range(2):
                        rows = slice(64 * part, 64 * part + 64)
                        dst = G[rows, 3 + part:3 + part + N].rearrange("p (t h j) -> p h j t", h=2, j=J // 2)
                        src = PP[rows, :, 0:H2].rearrange("p h (j t) -> p h j t", t=NT)
                        dve.tensor_copy(dst, src).then_inc(g_ready, 1)

                def rest(b, u):
                    w = b * U + u
                    dve.wait_ge(act_prep, w * 6 + 3 + 6)
                    dve.wait_ge(dve_prep, w * 3 + 2)
                    dve.wait_ge(part2_r, w + 1)
                    dve.scalar_tensor_tensor(halves(rest1[:]), halves(part1[:]), part23[:, 0:1], PP[0:96, :, 0:H2],
                                             ALU.mult, ALU.add).then_inc(dve_prep, 1)

                def parts(b, u):
                    k, w = u % 2, b * U + u
                    dve.wait_ge(part2_r, w + 1 + 1)
                    dve.wait_ge(c_w, (w + 1) * S)
                    dve.scalar_tensor_tensor(bc[k][:], part2[:], part23[:, 1:2], rest1[:], ALU.mult,
                                             ALU.add).then_inc(dve_prep, 1)

                def relu_dt(b, u):
                    k, w = u % 2, b * U + u
                    dve.wait_ge(pp_w, tasks(b, u) + 4)
                    dve.wait_ge(pool_prep, w * 2 + 1)
                    dve.wait_ge(act_prep, w * 6 + 4 + 6)
                    dve.tensor_scalar(halves(relu[:]), PP[:, :, 0:H2], dt_b[k][:], 0.0, ALU.add,
                                      ALU.max).then_inc(dve_prep, 1)

                def input_term(b, u, n):
                    v, k = b * U * S + (u * S + n), u % 2
                    if n == 0:
                        dve.wait_ge(pool_prep, (b * U + u) * 2 + 2 + 2)
                    dve.wait_ge(b_w, v + 1)
                    dve.wait_ge(h_r, v + 1 - 2 + KB)
                    dve.tensor_tensor(halves(dB[n % 2][:]), halves(du[k][:]), PB[:, :, 0:H2], ALU.mult).then_inc(dB_r, 1)

                def scan(b, u, n):
                    v, k = b * U * S + (u * S + n), u % 2
                    dve.wait_ge(dA_r, v + 1 + 2 * S)
                    dve.wait_ge(dB_r, v + 1 + 2 * S)
                    dve.wait_ge(hc_r, v + 1)
                    dve.wait_ge(car_r, v + 2 * S + 1 - KB)
                    dve.tensor_tensor_scan(hs[n % KB][:], dA[n % 4][:], dB[n % 2][:],
                                           0.0 if u < 2 else carry[k][:, n:n + 1], ALU.mult, ALU.add).then_inc(h_r, 1)

                def add_skip(b, u):
                    k, w = u % 2, b * U + u
                    dve.wait_ge(y_w, (w + 1) * S + KB)
                    dve.wait_ge(yz_r, w + 4)
                    dve.scalar_tensor_tensor(halves(yd[:]), halves(xc[k][:]), skip[k][:], PY[:, :, 0:H2], ALU.mult,
                                             ALU.add).then_inc(yd_r, 1)

                def result(b, q):
                    c = b * Q + q
                    dve.wait_ge(o_w, c + 1 + 1)
                    dve.wait_ge(ln_pool, c * 8 + 8 + 16)
                    dve.wait_ge(res_stored[q % 2], (b * (Q // 2) + (q // 2 + 1)) * 16)
                    dve.tensor_tensor(res[q % 2][:], PP[0:NT, 0, :].rearrange("p (j c) -> p j c", c=C), hg[q % 2][:],
                                      ALU.add).then_inc(out_done, 1)

                def unit(b, u, first, last):
                    nb, nu = (b, u + 1) if u < U - 1 else (b + 1, 0)
                    more = not (last and u == U - 1)
                    nq = (b, u // 2 + 1) if u // 2 < Q - 1 else (b + 1, 0)
                    more_q = not (last and u // 2 == Q - 1)
                    for n in range(S):
                        if n == LAG:
                            if u > 0:
                                add_skip(b, u - 1)
                            elif not first:
                                add_skip(b - 1, U - 1)
                        if n < S - 1:
                            input_term(b, u, n + 1)
                        elif more:
                            input_term(nb, nu, 0)
                        scan(b, u, n)
                        if u % 2 == 0 and more_q:
                            if n == 5:
                                ln_sum(*nq)
                            if n == 9:
                                ln_var(*nq)
                        if more:
                            if n == 2 and nu % 2 == 0:
                                take_g(nb, nu // 2)
                            if n == 6:
                                rest(nb, nu)
                            if n == 8:
                                parts(nb, nu)
                            if n == 9:
                                relu_dt(nb, nu)
                        if n == 14 and u % 2 == 0:
                            if u > 0:
                                result(b, u // 2 - 1)
                            elif not first:
                                result(b - 1, Q - 1)

                ln_sum(0, 0)
                ln_var(0, 0)
                take_g(0, 0)
                rest(0, 0)
                parts(0, 0)
                relu_dt(0, 0)
                input_term(0, 0, 0)
                for u in range(U):
                    unit(0, u, True, False)
                with dve.Fori(1, B - 1) as b:
                    for u in range(U):
                        unit(b, u, False, False)
                for u in range(U):
                    unit(B - 1, u, False, True)
                add_skip(B - 1, U - 1)
                result(B - 1, Q - 1)

            @block.gpsimd
            def _(pool):
                pool.memset(half_neg[:], -0.5)
                pool.memset(zero[:], 0.0)
                for i, value in enumerate((-1.0 / C, 1.0 / C, EPS)):
                    pool.memset(norm_consts[:, i, :], value)
                pool.drain().then_inc(su_pool, 1)
                pool.wait_ge(su_pool, 1)
                pool.wait_ge(w_loaded, wl)

                def normalise(b, q, step):
                    c = b * Q + q
                    n = c * 8 + 16
                    x, wide = xin[q % 2][:], [NT, J, C]
                    if step == 0:
                        pool.wait_ge(ln_dve, 2 * c + 1)
                        pool.wait_ge(ln_pool, n)
                        pool.tensor_tensor(st[:, 1, :], st[:, 0, :], norm_consts[:, 0, :], ALU.mult).then_inc(ln_pool, 1)
                        pool.wait_ge(ln_pool, n + 1)
                        pool.tensor_tensor(cen[:], x, st[:, 1, :].unsqueeze(2).to_broadcast(wide), ALU.add).then_inc(ln_pool, 1)
                        pool.wait_ge(ln_pool, n + 2)
                        pool.tensor_tensor(sq[:], cen[:], cen[:], ALU.mult).then_inc(ln_pool, 1)
                        return
                    pool.wait_ge(ln_dve, 2 * c + 2)
                    pool.tensor_tensor(st[:, 3, :], st[:, 2, :], norm_consts[:, 1, :], ALU.mult).then_inc(ln_pool, 1)
                    pool.wait_ge(ln_pool, n + 4)
                    pool.tensor_tensor(st[:, 5, :], st[:, 3, :], norm_consts[:, 2, :], ALU.add).then_inc(ln_pool, 1)
                    pool.wait_ge(ln_pool, n + 5)
                    pool.tensor_tensor(st[:, 4, :], st[:, 5, :], half_neg[:], ALU.pow).then_inc(ln_pool, 1)
                    pool.wait_ge(ln_pool, n + 6)
                    pool.wait_ge(g_ready, c * 3 + 3)
                    wide2 = [NT, J, 2, C]
                    pool.tensor_tensor(gg[:], cen[:].unsqueeze(2).to_broadcast(wide2),
                                       st[:, 4, :].unsqueeze(2).unsqueeze(3).to_broadcast(wide2), ALU.mult).then_inc(ln_pool, 1)

                def residual(b, q):
                    c = b * Q + q
                    pool.wait_ge(ln_pool, c * 8 + 7 + 16)
                    pool.wait_ge(out_done, c + 1)
                    pool.tensor_tensor(hg[q % 2][:], xin[q % 2][:], gg[:, :, 0, :], ALU.add).then_inc(ln_pool, 1)

                def step_size(b, u):
                    k, w = u % 2, b * U + u
                    pool.wait_ge(act_prep, w * 6 + 6 + 6)
                    pool.wait_ge(dve_prep, w * 3 + 3 + 3)
                    pool.wait_ge(dA_r, (w + 1) * S)
                    pool.tensor_tensor(dt[k][:], relu[:], sp3[:], ALU.add).then_inc(pool_prep, 1)

                def step_input(b, u):
                    k, w = u % 2, b * U + u
                    pool.wait_ge(pool_prep, w * 2 + 1 + 2)
                    pool.wait_ge(dB_r, (w + 1) * S)
                    pool.tensor_tensor(du[k][:], dt[k][:], xc[k][:], ALU.mult).then_inc(pool_prep, 1)

                def gate(b, u):
                    k, w = u % 2, b * U + u
                    pool.wait_ge(yd_r, w + 1 + 2)
                    pool.wait_ge(o_w, b * Q + (u // 2 + 1))
                    pool.tensor_tensor(yz[k][:], yd[:], sz[u % 4][:], ALU.mult).then_inc(yz_r, 1)

                def times_c(b, u, n):
                    v, k = b * U * S + (u * S + n), u % 2
                    pool.wait_ge(h_r, v + 1 + KB)
                    pool.tensor_tensor(carry[k][:, n:n + 1], hs[n % KB][:, N - 1:N], zero[:], ALU.add).then_inc(car_r, 1)
                    pool.wait_ge(cs_r, v + 1 + 1)
                    pool.wait_ge(y_w, v + 1)
                    pool.tensor_tensor(hc[n % KB][:], hs[n % KB][:], cs[n % KB][:], ALU.mult).then_inc(hc_r, 1)

                def unit(b, u, first, last):
                    nb, nu = (b, u + 1) if u < U - 1 else (b + 1, 0)
                    more = not (last and u == U - 1)
                    nq = (b, u // 2 + 1) if u // 2 < Q - 1 else (b + 1, 0)
                    more_q = not (last and u // 2 == Q - 1)
                    for n in range(S):
                        if n == 1 and u % 2 == 1 and more_q:
                            residual(*nq)
                        times_c(b, u, n)
                        if n == LAG + 1:
                            if u > 0:
                                gate(b, u - 1)
                            elif not first:
                                gate(b - 1, U - 1)
                        if u % 2 == 0 and more_q:
                            if n == 7:
                                normalise(*nq, 0)
                            if n == 11:
                                normalise(*nq, 1)
                        if more:
                            if n == 10:
                                step_size(nb, nu)
                            if n == 11:
                                step_input(nb, nu)

                normalise(0, 0, 0)
                normalise(0, 0, 1)
                residual(0, 0)
                step_size(0, 0)
                step_input(0, 0)
                for u in range(U):
                    unit(0, u, True, False)
                with pool.Fori(1, B - 1) as b:
                    for u in range(U):
                        unit(b, u, False, False)
                for u in range(U):
                    unit(B - 1, u, False, True)
                gate(B - 1, U - 1)


def attn_phase(nc, d):
    P = 128
    NB = LT // P
    HALF = (NB + 1) // 2
    D = 16
    NH, NKV = 4, 2
    QROWS = (NH + NKV) * D
    KR = 98
    QPART, KPART = (0, 0, 0, 1, 1, 2), (0, 1, 2, 0, 1, 0)
    NJ = 7
    SC = D ** -0.5
    LN_EPS, RMS_EPS = 1e-5, 1e-6
    W = [min(512, LT - 512 * j) for j in range(NJ)]

    def steps_of(j):
        out = []
        if j < NJ - 1:
            for k in range(4 * j + 4):
                for kv in range(NKV):
                    out.append((kv, [(k, max(0, (k - 4 * j)) * P)]))
        else:
            cuts = [NB * i // 8 for i in range(9)]
            for i in range(8):
                for kv in range(NKV):
                    out.append((kv, [(k, None) for k in range(cuts[i], cuts[i + 1])]))
        return out

    STEPS = [steps_of(j) for j in range(NJ)]
    NS = [len(s) for s in STEPS]
    SOFF = [sum(NS[:j]) for j in range(NJ)]
    NSI = sum(NS)
    TILES = [[(i, h, c, min(512, P * (i + 1) - 512 * c)) for i in range(4 * j, min(4 * j + 4, NB))
              for h in range(NH) for c in range(i // 4 + 1)] for j in range(NJ)]
    NT = [len(t) for t in TILES]
    TOFF = [sum(NT[:j]) for j in range(NJ)]
    NTI = sum(NT)
    assert NSI % 4 == 0 and NTI % 2 == 0

    MTS = [n - 6 for n in NS]

    LEAD = 96
    EVEN = SOFF[NJ - 2] - 6

    def tiles_before(s):
        full = TOFF[NJ - 1]
        return LEAD + s * (full - LEAD) // EVEN if s < EVEN else full + (s - EVEN) * (NTI + LEAD - full) // (NSI - EVEN)

    def share(s, last):
        out = []
        for n in range(tiles_before(s), tiles_before(s + 1)):
            ahead, n = n // NTI, n % NTI
            j = max(q for q in range(NJ) if TOFF[q] <= n)
            if not (last and ahead):
                out.append((ahead, j, n - TOFF[j]))
        return out

    assert tiles_before(NSI) == NTI + LEAD
    assert all(tiles_before(SOFF[j] + MTS[j] + 1) >= TOFF[j + 1] + NT[j + 1] for j in range(NJ - 1))
    assert LEAD >= NT[0]
    LEAD_TILES = [(j, n) for j in range(NJ) for n in range(NT[j]) if TOFF[j] + n < LEAD]

    LN0, TR0, V0 = 2, 34, 92
    PROJ_AT = 9
    NG = 7
    QK0 = [42, 49, 57, 63, 74, 80, 89]
    GROUPS = [(half, g * 512, min(512, (HALF if half == 0 else NB - HALF) * P - g * 512))
              for half in range(2) for g in range(4) if (HALF if half == 0 else NB - HALF) * P > g * 512]
    assert len(GROUPS) == NG
    NTR = (HALF + 3) // 4
    VCUT = 16

    def prep_tasks():
        return [(f"T{i}", 1) for i in range(NTR)] + [x for g in range(NG) for x in ((f"Q{g}", 1), (f"R{g}", 1))] + [("V0", 1), ("V1", 1)]

    def image_tasks(last):
        out = []
        for j in range(NJ):
            for e in range(NS[j]):
                s = SOFF[j] + e
                if j > 0 and e == 4:
                    out.append((f"DEN{j - 1}", W[j - 1] // P))
                if j > 0 and e == PROJ_AT:
                    out.append((f"PROJ{j - 1}", 1))
                if not last:
                    for i in range(NTR):
                        if s == TR0 + 2 * i:
                            out.append((f"T{i}", 1))
                    for g in range(NG):
                        if s == QK0[g]:
                            out.append((f"Q{g}", 1))
                        if s == QK0[g] + 1:
                            out.append((f"R{g}", 1))
                    for i in range(2):
                        if s == V0 + 2 * i:
                            out.append((f"V{i}", 1))
                if e == MTS[j] and not (last and j == NJ - 1):
                    out.append((f"MT{(j + 1) % NJ}", 2))
        return out + [(f"DEN{NJ - 1}", W[NJ - 1] // P), (f"PROJ{NJ - 1}", 1)]

    def index(tasks):
        at, w, r = {}, 0, 0
        for name, reads in tasks:
            at[name] = (w, r)
            w, r = w + 1, r + reads
        return at, w, r

    PRO, PRO_W, PRO_R = index(prep_tasks() + [("MT0", 2)])
    IMG, IMG_W, IMG_R = index(image_tasks(False))
    END, _, _ = index(image_tasks(True))

    class Task:
        def __init__(self, where, b, name):
            if where == "pro":
                (w, self.r), bw, self.b = PRO[name], 0, 0
            else:
                (w, self.r), bw, self.b = (END if where == "end" else IMG)[name], b * IMG_W + PRO_W, b * IMG_R + PRO_R
            self.made, self.j = bw + (w + 1), int(name[-1])

        def read(self, n=1):
            return self.b + (self.r + n)

    h2r = d["h2"].rearrange("b t c -> (b t) c")
    x2r = d["x2"].rearrange("b t c -> (b t) c")
    with ExitStack() as ctx:
        def sb(n, s, t=F32):
            return ctx.enter_context(nc.sbuf_tensor("at_" + n, s, t))

        def sem(n):
            return ctx.enter_context(nc.semaphore("at_" + n))

        ident = sb("ident", [P, P])
        identb = sb("identb", [P, P], BF16)
        mask_q = sb("mask_q", [P, P], BF16)
        mask_k = sb("mask_k", [P, P], BF16)
        den_sel = sb("den_sel", [P, P])
        cos = sb("cos", [QROWS, LT])
        sin = sb("sin", [QROWS, LT])
        raw = sb("raw", [QROWS, 3, 2, P])
        raw_o = sb("raw_o", [C, P])
        ln1 = sb("ln1", [P, 1])
        w_qk = sb("w_qk", [P, 2, 2, QROWS])
        w_v = sb("w_v", [P, 2, NKV * D])
        w_o = sb("w_o", [P, C])
        half_neg = sb("half_neg", [P, NB])
        norm_consts = sb("norm_consts", [P, 3, NB])
        X0 = sb("X0", [P, NB, C])
        cen_pairs = sb("cen_pairs", [P, 2 * HALF, C])
        cen = cen_pairs[:, 0:NB, :]
        R = cen_pairs[:].rearrange("p (m a) c -> p m a c", a=2)
        stt = sb("stt", [P, 8, NB])
        X = [sb(f"xn{k}", [P, NB, C]) for k in range(2)]
        T = sb("T", [P, HALF, P])
        V = [sb(f"V{k}", [P, NB, NKV, 32]) for k in range(2)]
        t1 = sb("t1", [QROWS, 512])
        t2 = sb("t2", [QROWS, 512])
        qk = sb("qk", [QROWS, 512])
        qr = sb("qr", [QROWS, 512])
        parts = [[sb(f"parts{half}{k}", [QROWS, HALF * P], BF16) for k in range(3)] for half in range(2)]
        QS = [sb(f"QS{k}", [KR, NH, LT], BF16) for k in range(2)]
        KS = [sb(f"KS{k}", [KR, NKV, LT], BF16) for k in range(2)]
        pm = sb("pm", [P, 4, NH, NJ])
        negm = [sb(f"negm{k}", [P, NB, NH]) for k in range(2)]
        m1 = sb("m1", [NH, 512], BF16)
        m2 = sb("m2", [NH, 512], BF16)
        E = [sb(f"E{k}", [P, 2, 512]) for k in range(4)]
        O = sb("O", [P, 512])
        rec = sb("rec", [P, 512])
        Y = sb("Y", [P, 512])
        x2 = [sb(f"x2{k}", [P, 4, C]) for k in range(2)]
        ST = [ctx.enter_context(nc.psum_tensor(f"at_ST{k}", [P, 2, 512], F32)) for k in range(2)]
        MX = [ctx.enter_context(nc.psum_tensor(f"at_MX{k}", [P, 512], F32)) for k in range(2)]
        PO = ctx.enter_context(nc.psum_tensor("at_PO", [P, 512], F32))
        MI = ctx.enter_context(nc.psum_tensor("at_MI", [P, 512], F32))

        loaded = sem("loaded")
        x_in = sem("x_in")
        stacked = [sem(f"stacked{k}") for k in range(2)]
        m_in = sem("m_in")
        x2_out = [sem(f"x2_out{k}") for k in range(2)]
        su_dve, su_pe = sem("su_dve"), sem("su_pe")
        su_pool = sem("su_pool")
        n_dve, n_pool, n_act = sem("n_dve"), sem("n_pool"), sem("n_act")
        mi_w, mi_r = sem("mi_w"), sem("mi_r")
        r_pool, r_act = sem("r_pool"), sem("r_act")
        st_w = sem("st_w")
        e_r = sem("e_r")
        pv_w = sem("pv_w")
        mx_w, mx_r = sem("mx_w"), sem("mx_r")
        fin = sem("fin")
        o_r = sem("o_r")
        y_r = sem("y_r")

        nl = 0

        with nc.Block() as block:
            @block.sync
            def _(sp):
                nonlocal nl

                def load(dst, src):
                    nonlocal nl
                    sp.dma_start(dst, src).then_inc(loaded, 16)
                    nl += 16
                load(ident[:], d["ident"])
                load(identb[:], d["ident_bf16"])
                load(mask_q[:], d["mask_queries"])
                load(mask_k[:], d["mask_keys"])
                load(den_sel[:], d["sum_selector"])
                load(cos[:], d["rope_cos"])
                load(sin[:], d["rope_sin"])
                sp.wait_ge(su_dve, 1)
                for half in range(2):
                    cols = slice(64 * half, 64 * half + 64)
                    load(raw[0:64, 0, half, cols], d["L0_ffn_wq"])
                    load(raw[64:96, 0, half, cols], d["L0_ffn_wk"])
                    load(raw[0:64, 1, half, cols], d["wq_rotated"])
                    load(raw[64:96, 1, half, cols], d["wk_rotated"])
                    load(raw[0:32, 2, half, cols], d["L0_ffn_wv"])
                    load(ln1[64 * half:64 * half + 64, :], d["L0_ffn_ln1_w"].rearrange("(c a) -> c a", a=1))
                for h in range(NH):
                    load(raw_o[:, 32 * h:32 * h + D], d["L0_ffn_wo"][:, D * h:D * h + D])

                def load_x(b):
                    sp.wait_ge(n_dve, b * 3 + 3)
                    sp.dma_start(X0[:], h2r[bass.ds(b * LT, LT), :].rearrange("(n p) c -> p n c", p=P)).then_inc(x_in, 16)

                def stack(gb, par, half):
                    ng = 4 if half == 0 else NG
                    sp.wait_ge(r_pool, gb * (3 * NG) + 3 * ng + 3)
                    n = (HALF if half == 0 else NB - HALF) * P
                    t0 = half * HALF * P
                    for a in range(6):
                        for h in range(NH):
                            sp.dma_start(QS[par][D * a:D * a + D, h, t0:t0 + n],
                                         parts[half][QPART[a]][D * h:D * h + D, 0:n]).then_inc(stacked[par], 16)
                        for kv in range(NKV):
                            r = (NH + kv) * D
                            sp.dma_start(KS[par][D * a:D * a + D, kv, t0:t0 + n],
                                         parts[half][KPART[a]][r:r + D, 0:n]).then_inc(stacked[par], 16)

                def maxima(task, par, j):
                    sp.wait_ge(mi_r, task.read(2))
                    sp.dma_start(QS[par][96:97, :, 512 * j:512 * j + W[j]], m1[:, 0:W[j]]).then_inc(m_in, 16)
                    sp.dma_start(QS[par][97:98, :, 512 * j:512 * j + W[j]], m2[:, 0:W[j]]).then_inc(m_in, 16)

                def store(where, b, par, j):
                    w = W[j]
                    sp.wait_ge(mi_r, Task(where, b, f"PROJ{j}").read())
                    sp.dma_start(x2r[bass.ds(b * LT + 512 * j, w), :].rearrange("(n p) c -> p n c", p=P),
                                 x2[(par * NJ + j) % 2][:, 0:w // P, :]).then_inc(x2_out[(par * NJ + j) % 2], 16)

                def image(b, par, where):
                    last = where == "end"
                    if not last:
                        load_x(b + 1)
                    for j in range(NJ):
                        for e in range(NS[j]):
                            s = SOFF[j] + e
                            if j > 0 and e == PROJ_AT + 3:
                                store(where, b, par, j - 1)
                            if not last:
                                if s == QK0[3] + 7:
                                    stack(b + 1, 1 - par, 0)
                                if s == QK0[6] + 7:
                                    stack(b + 1, 1 - par, 1)
                            if e == MTS[j] + 1 and (j < NJ - 1 or not last):
                                maxima(Task(where, b, f"MT{(j + 1) % NJ}"), par if j < NJ - 1 else 1 - par, (j + 1) % NJ)
                    store(where, b, par, NJ - 1)

                load_x(0)
                stack(0, 0, 0)
                stack(0, 0, 1)
                maxima(Task("pro", 0, "MT0"), 0, 0)
                with sp.Fori(0, B // 2 - 1) as i:
                    image(2 * i, 0, "img")
                    image(2 * i + 1, 1, "img")
                image(B - 2, 0, "img")
                image(B - 1, 1, "end")
                for k in range(2):
                    sp.wait_ge(x2_out[k], 16 + 16 * (B * NJ // 2))

            @block.tensor
            def _(pe):
                pe.wait_ge(loaded, nl)
                pe.wait_ge(su_dve, 2)
                for half in range(2):
                    pe.transpose(MI[:, 96 * half:96 * half + 96], raw[:, 0, half, :], ident[0:96, 0:96])
                    pe.transpose(MI[:, 192 + 96 * half:288 + 96 * half], raw[:, 1, half, :], ident[0:96, 0:96])
                    pe.transpose(MI[:, 384 + 32 * half:416 + 32 * half], raw[0:32, 2, half, :], ident[0:32, 0:32])
                pe.transpose(MI[:, 448:512], raw_o[:], ident[0:C, 0:C]).then_inc(su_pe, 1)
                pe.wait_ge(su_dve, 6)

                def open_task(t, where):
                    if where != "pro" or t.r > 0:
                        pe.wait_ge(mi_r, t.read(0))

                def turn(t, where, gb, i):
                    open_task(t, where)
                    if i == 0:
                        pe.wait_ge(n_pool, gb * 9 + 9 + 9)
                    ms = range(4 * i, min(4 * i + 4, HALF))
                    for m in ms:
                        mm = pe.transpose(MI[:, (m - 4 * i) * P:(m - 4 * i + 1) * P], R[:, m].rearrange("p a c -> p (a c)"),
                                          ident[:])
                    mm.then_inc(mi_w, 1)

                def project(t, where, g, rot):
                    half, c0, n = GROUPS[g]
                    open_task(t, where)
                    pe.matmul(MI[0:QROWS, 0:n], w_qk[:, rot, half, :], T[:].rearrange("p m t -> p (m t)")[:, c0:c0 + n],
                              start=True, stop=True).then_inc(mi_w, 1)

                def values(t, where, i):
                    open_task(t, where)
                    for n in range(VCUT * i, min(VCUT * i + VCUT, NB)):
                        half, m = n // HALF, n % HALF
                        o = (n - VCUT * i) * NKV * D
                        mm = pe.matmul(MI[:, o:o + NKV * D], T[:, m, :], w_v[:, half, :], start=True, stop=True)
                    mm.then_inc(mi_w, 1)

                def turn_max(t, where, gb, par, j):
                    open_task(t, where)
                    pe.wait_ge(fin, gb * NB + min(4 * j + 4, NB) + 3)
                    for i in range(W[j] // P):
                        mm = pe.transpose(MI[0:NH, i * P:(i + 1) * P], negm[par][:, 4 * j + i, :], ident[:])
                    mm.then_inc(mi_w, 1)

                def tile(gb, par, j, n):
                    i, h, c, w = TILES[j][n]
                    m = gb * NTI + (TOFF[j] + n)
                    pe.wait_ge(mx_r, m + 1)
                    diag = 512 * c + w == P * (i + 1)
                    k = (TOFF[j] + n) % 2
                    mm = pe.matmul(MX[k][:, 0:w], QS[par][0:96, h, i * P:i * P + P],
                                   KS[par][0:96, h // 2, 512 * c:512 * c + w], start=True, stop=not diag)
                    if diag:
                        mm = pe.matmul(MX[k][:, w - P:w], identb[:], mask_q[:], start=False, stop=True)
                    mm.then_inc(mx_w, 1)

                def transposed(b, par, j, e, hh):
                    kv, blocks = STEPS[j][e]
                    g = b * NSI + (SOFF[j] + e)
                    if e == 0 and hh == 0:
                        pe.wait_ge(m_in, (b * NJ + (j + 1)) * 32)
                    if hh == 0:
                        pe.wait_ge(e_r, g + 1)
                    k2 = (SOFF[j] + e) % 2
                    h = 2 * kv + hh
                    for n, (k, off) in enumerate(blocks):
                        if off is None:
                            dst, a, w = ST[k2][:, hh, n * P:n * P + P], 512 * j, P
                            diag, dd = k == NB - 1, n * P
                        else:
                            dst, a, w = ST[k2][:, hh, off:512], 512 * j + off, 512 - off
                            diag, dd = k >= 4 * j, off
                        mm = pe.matmul(dst, KS[par][:, kv, k * P:k * P + P], QS[par][:, h, a:a + w],
                                       start=True, stop=not diag)
                        if diag:
                            mm = pe.matmul(ST[k2][:, hh, dd:dd + P], identb[:], mask_k[:], start=False, stop=True)
                    if hh == 1:
                        mm.then_inc(st_w, 1)

                def times_v(b, par, j, e):
                    s = b * NJ + j
                    pe.wait_ge(e_r, b * NSI + (SOFF[j] + e + 2 + 2))
                    if e == 0:
                        pe.wait_ge(o_r, s + 1)
                    blocks = STEPS[j][e][1]
                    for n, (k, off) in enumerate(blocks):
                        for h in range(NH):
                            kv, hh = h // 2, h % 2
                            src = E[(SOFF[j] + e + kv) % 4]
                            a, z = (n * P, n * P + P) if off is None else (off, 512)
                            oa, oz = (0, P) if off is None else (off, 512)
                            mm = pe.matmul(PO[32 * h:32 * h + 32, oa:oz], V[par][:, k, kv, :], src[:, hh, a:z],
                                           start=k == 0, stop=k == min(4 * j + 3, NB - 1), skip_group_check=True)
                    mm.then_inc(pv_w, 2)

                def sums(t, where, s):
                    open_task(t, where)
                    pe.wait_ge(o_r, s + 1 + 1)
                    j = t.j
                    pe.matmul(MI[:, 0:W[j]], den_sel[:], O[:, 0:W[j]], start=True, stop=True).then_inc(mi_w, 1)

                def out_proj(t, where, s):
                    open_task(t, where)
                    pe.wait_ge(y_r, s + 1 + 1)
                    for i in range(W[t.j] // P):
                        mm = pe.matmul(MI[:, i * C:(i + 1) * C], Y[:, i * P:(i + 1) * P], w_o[:], start=True, stop=True)
                    mm.then_inc(mi_w, 1)

                def image(b, par, where, count):
                    last = where == "end"
                    for j in range(NJ):
                        for e in range(NS[j]):
                            s = SOFF[j] + e
                            tiles = share(s, last)

                            def next_tile():
                                if tiles:
                                    ahead, tj, n = tiles.pop(0)
                                    if ahead and tj == 0 and n == 0:
                                        pe.wait_ge(stacked[1 - par], count)
                                    tile(b + ahead, (par + ahead) % 2, tj, n)
                            if e % 2 == 0:
                                next_tile()
                            transposed(b, par, j, e, 0)
                            if e % 2 == 1:
                                next_tile()
                            transposed(b, par, j, e, 1)
                            next_tile()
                            if e % 2 == 1:
                                if e >= 3:
                                    times_v(b, par, j, e - 3)
                                elif j > 0:
                                    times_v(b, par, j - 1, NS[j - 1] - 2)
                            while tiles:
                                next_tile()
                            if j > 0 and e == 4:
                                sums(Task(where, b, f"DEN{j - 1}"), where, b * NJ + (j - 1))
                            if j > 0 and e == PROJ_AT:
                                out_proj(Task(where, b, f"PROJ{j - 1}"), where, b * NJ + (j - 1))
                            if not last:
                                for i in range(NTR):
                                    if s == TR0 + 2 * i:
                                        turn(Task(where, b, f"T{i}"), where, b + 1, i)
                                for g in range(NG):
                                    if s == QK0[g]:
                                        project(Task(where, b, f"Q{g}"), where, g, 0)
                                    if s == QK0[g] + 1:
                                        project(Task(where, b, f"R{g}"), where, g, 1)
                                for i in range(2):
                                    if s == V0 + 2 * i:
                                        values(Task(where, b, f"V{i}"), where, i)
                            if e == MTS[j] and not (last and j == NJ - 1):
                                nb, np_, nj = (b, par, j + 1) if j < NJ - 1 else (b + 1, 1 - par, 0)
                                turn_max(Task(where, b, f"MT{nj}"), where, nb, np_, nj)
                    times_v(b, par, NJ - 1, NS[NJ - 1] - 2)
                    sums(Task(where, b, f"DEN{NJ - 1}"), where, b * NJ + (NJ - 1))
                    out_proj(Task(where, b, f"PROJ{NJ - 1}"), where, b * NJ + (NJ - 1))

                for i in range(NTR):
                    turn(Task("pro", 0, f"T{i}"), "pro", 0, i)
                for g in range(NG):
                    project(Task("pro", 0, f"Q{g}"), "pro", g, 0)
                    project(Task("pro", 0, f"R{g}"), "pro", g, 1)
                for i in range(2):
                    values(Task("pro", 0, f"V{i}"), "pro", i)
                pe.wait_ge(stacked[0], 72 * 16)
                for j, n in LEAD_TILES:
                    tile(0, 0, j, n)
                turn_max(Task("pro", 0, "MT0"), "pro", 0, 0, 0)
                pe.wait_ge(su_dve, 7)
                PER = 72 * 16
                with pe.Fori(0, B // 2 - 1) as i:
                    image(2 * i, 0, "img", (i + 1) * PER)
                    image(2 * i + 1, 1, "img", (i + 2) * PER)
                image(B - 2, 0, "img", (B // 2) * PER)
                image(B - 1, 1, "end", 0)

            @block.scalar
            def _(act):
                act.wait_ge(loaded, nl)

                def square(gb, par, n):
                    act.wait_ge(n_pool, gb * 9 + (2 if n == 0 else 5) + 9)
                    act.activation(X0[:], cen if n == 0 else X[par][:], ACT.Square, scale=C ** -0.5).then_inc(n_act, 1)

                def part(gb, par, g, n, count):
                    half, c0, w = GROUPS[g]
                    a = gb * (3 * NG) + 3 * g + 3
                    if n == 0:
                        act.wait_ge(r_pool, a + 1)
                        if g == 0 and count is not None:
                            act.wait_ge(*count)
                        act.activation(parts[half][0][:, c0:c0 + w], qk[:, 0:w], ACT.Copy).then_inc(r_act, 1)
                    else:
                        act.wait_ge(r_pool, a + 2)
                        act.activation(parts[half][1][:, c0:c0 + w], qr[:, 0:w], ACT.Copy).then_inc(r_act, 1)

                def first_max(t, s):
                    act.wait_ge(mi_w, t.made)
                    act.wait_ge(m_in, s * 32 + 32)
                    act.activation(m1[:, 0:W[t.j]], MI[0:NH, 0:W[t.j]], ACT.Copy).then_inc(mi_r, 1)

                def exponential(b, j, e):
                    g = b * NSI + (SOFF[j] + e)
                    act.wait_ge(st_w, g + 1)
                    act.wait_ge(pv_w, g + 1)
                    blocks = STEPS[j][e][1]
                    a, z = (0, P * len(blocks)) if blocks[0][1] is None else (blocks[0][1], 512)
                    act.activation(E[(SOFF[j] + e) % 4][:, :, a:z], ST[(SOFF[j] + e) % 2][:, :, a:z], ACT.Exp,
                                   scale=SC).then_inc(e_r, 1)

                def take(b, j):
                    s = b * NJ + j
                    act.wait_ge(pv_w, b * NSI + (SOFF[j] + NS[j]) + 4)
                    act.wait_ge(y_r, s + 1)
                    act.activation(O[:, 0:W[j]], PO[:, 0:W[j]], ACT.Copy).then_inc(o_r, 1)

                def image(b, par, where, prev):
                    last = where == "end"
                    for j in range(NJ):
                        for e in range(NS[j]):
                            s = SOFF[j] + e
                            exponential(b, j, e)
                            if e == MTS[j] + 1 and not (last and j == NJ - 1):
                                nj = (j + 1) % NJ
                                first_max(Task(where, b, f"MT{nj}"), b * NJ + j)
                            if j > 0 and e == 2:
                                take(b, j - 1)
                            if not last:
                                if s == LN0 + 8:
                                    square(b + 1, 1 - par, 0)
                                if s == LN0 + 20:
                                    square(b + 1, 1 - par, 1)
                                for g in range(NG):
                                    if s == QK0[g] + 3:
                                        part(b + 1, 1 - par, g, 0, prev)
                                    if s == QK0[g] + 5:
                                        part(b + 1, 1 - par, g, 1, prev)
                    take(b, NJ - 1)

                square(0, 0, 0)
                square(0, 0, 1)
                for g in range(NG):
                    part(0, 0, g, 0, None)
                    part(0, 0, g, 1, None)
                t = Task("pro", 0, "MT0")
                act.wait_ge(mi_w, t.made)
                act.activation(m1[:, 0:W[0]], MI[0:NH, 0:W[0]], ACT.Copy).then_inc(mi_r, 1)
                PER = 72 * 16
                with act.Fori(0, B // 2 - 1) as i:
                    image(2 * i, 0, "img", (stacked[0], (i + 1) * PER))
                    image(2 * i + 1, 1, "img", (stacked[1], (i + 1) * PER))
                image(B - 2, 0, "img", (stacked[0], B // 2 * PER))
                image(B - 1, 1, "end", None)

            @block.vector
            def _(dve):
                for s_, n_ in ((n_pool, 9), (n_dve, 3), (r_pool, 3), (e_r, 2), (pv_w, 4), (mx_r, 2), (fin, 3), (o_r, 1), (y_r, 1),
                               (x2_out[0], 16), (x2_out[1], 16)):
                    dve.sem_inc(s_, n_)
                dve.memset(raw[:], 0.0)
                dve.memset(raw_o[:], 0.0)
                dve.drain().then_inc(su_dve, 1)
                dve.memset(cen_pairs[:], 0.0)
                for k in range(2):
                    dve.memset(V[k][:], 0.0)
                dve.drain().then_inc(su_dve, 1)
                dve.wait_ge(su_dve, 2)
                for k in range(2):
                    dve.memset(V[k][:, :, :, D:D + 1], 1.0)
                dve.wait_ge(su_pe, 1)
                dve.wait_ge(loaded, nl)
                dve.tensor_scalar(w_qk[:].rearrange("p r h n -> p (r h n)"), MI[:, 0:384], ln1[:], None, ALU.mult).then_inc(su_dve, 1)
                dve.tensor_scalar(w_v[:].rearrange("p h n -> p (h n)"), MI[:, 384:448], ln1[:], None, ALU.mult).then_inc(su_dve, 1)
                dve.tensor_copy(w_o[:], MI[:, 448:512]).then_inc(su_dve, 1)
                dve.drain().then_inc(su_dve, 1)

                def moment(gb, n):
                    if n == 0:
                        dve.wait_ge(x_in, (gb + 1) * 16)
                        dve.wait_ge(n_pool, gb * 9 + 9)
                    else:
                        dve.wait_ge(n_act, gb * 2 + n)
                    dve.tensor_reduce(stt[:, n, :], X0[:], AX.X, ALU.add).then_inc(n_dve, 1)

                def take_t(t, i):
                    dve.wait_ge(mi_w, t.made)
                    a, z = 4 * i, min(4 * i + 4, HALF)
                    dve.tensor_copy(T[:, a:z, :], MI[:, 0:(z - a) * P].rearrange("p (m t) -> p m t", t=P)).then_inc(mi_r, 1)

                def rope(t, gb, g, rot):
                    half, c0, w = GROUPS[g]
                    t0 = half * HALF * P + c0
                    dve.wait_ge(mi_w, t.made)
                    dve.wait_ge(r_pool, gb * (3 * NG) + 3 * g + 1)
                    dve.tensor_tensor((t1, t2)[rot][:, 0:w], MI[0:QROWS, 0:w], (cos, sin)[rot][:, t0:t0 + w],
                                      ALU.mult).then_inc(mi_r, 1)

                def take_v(t, par, i):
                    dve.wait_ge(mi_w, t.made)
                    a, z = VCUT * i, min(VCUT * i + VCUT, NB)
                    dve.tensor_copy(V[par][:, a:z, :, 0:D],
                                    MI[:, 0:(z - a) * NKV * D].rearrange("p (n k e) -> p n k e", k=NKV, e=D)).then_inc(mi_r, 1)

                def tile(gb, par, j, n):
                    i, h, c, w = TILES[j][n]
                    m = gb * NTI + (TOFF[j] + n)
                    if h == 0 and c == 0:
                        if i == 0:
                            dve.wait_ge(fin, gb * NB + 3)
                        else:
                            dve.wait_ge(fin, gb * NB + (i + 1))
                    dve.wait_ge(mx_w, m + 1)
                    dve.tensor_reduce(pm[:, i % 4, h, c:c + 1], MX[(TOFF[j] + n) % 2][:, 0:w], AX.X, ALU.max).then_inc(mx_r, 1)
                    if h == NH - 1 and c == i // 4:
                        dve.wait_ge(mx_r, m + 1 + 2)
                        dve.tensor_reduce(negm[par][:, i, :], pm[:, i % 4, :, 0:c + 1], AX.X, ALU.max,
                                          negate=True).then_inc(fin, 1)

                def second_max(t):
                    dve.wait_ge(mi_r, t.read(1))
                    dve.tensor_tensor(m2[:, 0:W[t.j]], MI[0:NH, 0:W[t.j]], m1[:, 0:W[t.j]], ALU.subtract).then_inc(mi_r, 1)

                def invert(t, s, i):
                    dve.wait_ge(mi_w, t.made)
                    dve.wait_ge(y_r, s + 1)
                    dve.reciprocal(rec[:, i * P:(i + 1) * P], MI[:, i * P:(i + 1) * P]).then_inc(mi_r, 1)

                def residual(t, b, par, j, count):
                    dve.wait_ge(mi_w, t.made)
                    k = (par * NJ + j) % 2
                    dve.wait_ge(x2_out[k], count)
                    w = W[j] // P
                    dve.tensor_tensor(x2[k][:, 0:w, :], MI[:, 0:w * C].rearrange("p (n c) -> p n c", c=C),
                                      X[par][:, 4 * j:4 * j + w, :], ALU.add).then_inc(mi_r, 1)

                def image(b, par, where, pair):
                    last = where == "end"

                    def stored(j):
                        return pair * (16 * NJ) + 16 * ((par * NJ + j) // 2 + 1)
                    for j in range(NJ):
                        for e in range(NS[j]):
                            s = SOFF[j] + e
                            for ahead, tj, n in share(s, last):
                                tile(b + ahead, (par + ahead) % 2, tj, n)
                            if not last:
                                for i in range(NTR):
                                    if s == TR0 + 2 * i + 1:
                                        take_t(Task(where, b, f"T{i}"), i)
                                for i in range(2):
                                    if s == V0 + 2 * i + 1:
                                        take_v(Task(where, b, f"V{i}"), 1 - par, i)
                            if e == MTS[j] + 1 and not (last and j == NJ - 1):
                                second_max(Task(where, b, f"MT{(j + 1) % NJ}"))
                            if j > 0 and 4 <= e < 4 + W[j - 1] // P:
                                invert(Task(where, b, f"DEN{j - 1}"), b * NJ + (j - 1), e - 4)
                            if j > 0 and e == PROJ_AT:
                                residual(Task(where, b, f"PROJ{j - 1}"), b, par, j - 1, stored(j - 1))
                            if not last:
                                for n, at in ((0, 0), (1, 10), (2, 22)):
                                    if s == LN0 + at:
                                        moment(b + 1, n)
                                for g in range(NG):
                                    if s == QK0[g]:
                                        rope(Task(where, b, f"Q{g}"), b + 1, g, 0)
                                    if s == QK0[g] + 1:
                                        rope(Task(where, b, f"R{g}"), b + 1, g, 1)
                    invert(Task(where, b, f"DEN{NJ - 1}"), b * NJ + (NJ - 1), 0)
                    residual(Task(where, b, f"PROJ{NJ - 1}"), b, par, NJ - 1, stored(NJ - 1))

                for n in range(3):
                    moment(0, n)
                for i in range(NTR):
                    take_t(Task("pro", 0, f"T{i}"), i)
                for g in range(NG):
                    rope(Task("pro", 0, f"Q{g}"), 0, g, 0)
                    rope(Task("pro", 0, f"R{g}"), 0, g, 1)
                for i in range(2):
                    take_v(Task("pro", 0, f"V{i}"), 0, i)
                for k in range(2):
                    dve.memset(KS[k][96:98], 1.0)
                dve.drain().then_inc(su_dve, 1)
                for j, n in LEAD_TILES:
                    tile(0, 0, j, n)
                second_max(Task("pro", 0, "MT0"))
                with dve.Fori(0, B // 2 - 1) as i:
                    image(2 * i, 0, "img", i)
                    image(2 * i + 1, 1, "img", i)
                image(B - 2, 0, "img", B // 2 - 1)
                image(B - 1, 1, "end", B // 2 - 1)

            @block.gpsimd
            def _(pool):
                pool.memset(half_neg[:], -0.5)
                for i, value in enumerate((-1.0 / C, LN_EPS, RMS_EPS)):
                    pool.memset(norm_consts[:, i, :], value)
                pool.drain().then_inc(su_pool, 1)
                pool.wait_ge(su_pool, 1)
                pool.wait_ge(su_dve, 2)

                def norms(gb, par, n):
                    c = gb * 9 + 9
                    wide = [P, NB, C]

                    def bc(k, a=0, z=NB):
                        return stt[:, k, a:z].unsqueeze(2).to_broadcast([P, z - a, C])
                    pool.wait_ge(n_dve, gb * 3 + n + 1 + 3)
                    if n == 0:
                        pool.wait_ge(n_pool, c)
                        pool.tensor_tensor(stt[:, 3, :], stt[:, 0, :], norm_consts[:, 0, :], ALU.mult).then_inc(n_pool, 1)
                        pool.wait_ge(n_pool, c + 1)
                        pool.tensor_tensor(cen, X0[:], bc(3), ALU.add).then_inc(n_pool, 1)
                    if n == 1:
                        pool.tensor_tensor(stt[:, 4, :], stt[:, 1, :], norm_consts[:, 1, :], ALU.add).then_inc(n_pool, 1)
                        pool.wait_ge(n_pool, c + 3)
                        pool.tensor_tensor(stt[:, 5, :], stt[:, 4, :], half_neg[:], ALU.pow).then_inc(n_pool, 1)
                        pool.wait_ge(n_pool, c + 4)
                        pool.tensor_tensor(X[par][:], cen, bc(5), ALU.mult).then_inc(n_pool, 1)
                    if n == 2:
                        pool.tensor_tensor(stt[:, 6, :], stt[:, 2, :], norm_consts[:, 2, :], ALU.add).then_inc(n_pool, 1)
                        pool.wait_ge(n_pool, c + 6)
                        pool.tensor_tensor(stt[:, 7, :], stt[:, 6, :], half_neg[:], ALU.pow).then_inc(n_pool, 1)
                        pool.wait_ge(n_pool, c + 7)
                        pool.tensor_tensor(R[:, :, 0, :], X[par][:, 0:HALF, :], bc(7, 0, HALF), ALU.mult).then_inc(n_pool, 1)
                        pool.tensor_tensor(R[:, 0:NB - HALF, 1, :], X[par][:, HALF:NB, :], bc(7, HALF, NB), ALU.mult).then_inc(n_pool, 1)

                def split(tr, gb, g, n):
                    half, c0, w = GROUPS[g]
                    a, r = gb * (3 * NG) + 3 * g + 3, gb * (2 * NG) + 2 * g
                    if n == 0:
                        pool.wait_ge(mi_r, tr.read())
                        pool.wait_ge(r_pool, a)
                        pool.tensor_tensor(qk[:, 0:w], t1[:, 0:w], t2[:, 0:w], ALU.add).then_inc(r_pool, 1)
                    if n == 1:
                        pool.wait_ge(r_act, r + 1)
                        pool.tensor_tensor(qr[:, 0:w], qk[:, 0:w], parts[half][0][:, c0:c0 + w], ALU.subtract).then_inc(r_pool, 1)
                    if n == 2:
                        pool.wait_ge(r_act, r + 2)
                        pool.tensor_tensor(parts[half][2][:, c0:c0 + w], qr[:, 0:w], parts[half][1][:, c0:c0 + w], ALU.subtract).then_inc(r_pool, 1)

                def divide(t, s):
                    pool.wait_ge(mi_r, t.read(W[t.j] // P))
                    pool.tensor_tensor(Y[:, 0:W[t.j]], O[:, 0:W[t.j]], rec[:, 0:W[t.j]], ALU.mult).then_inc(y_r, 1)

                def image(b, par, where):
                    last = where == "end"
                    for j in range(NJ):
                        for e in range(NS[j]):
                            s = SOFF[j] + e
                            if j > 0 and e == PROJ_AT - 1:
                                divide(Task(where, b, f"DEN{j - 1}"), b * NJ + (j - 1))
                            if not last:
                                for n, at in ((0, 0), (1, 10), (2, 22)):
                                    if s == LN0 + at:
                                        norms(b + 1, 1 - par, n)
                                for g in range(NG):
                                    for n in range(3):
                                        if s == QK0[g] + 2 + 2 * n:
                                            split(Task(where, b, f"R{g}"), b + 1, g, n)
                    divide(Task(where, b, f"DEN{NJ - 1}"), b * NJ + (NJ - 1))

                for n in range(3):
                    norms(0, 0, n)
                for g in range(NG):
                    for n in range(3):
                        split(Task("pro", 0, f"R{g}"), 0, g, n)
                with pool.Fori(0, B // 2 - 1) as i:
                    image(2 * i, 0, "img")
                    image(2 * i + 1, 1, "img")
                image(B - 2, 0, "img")
                image(B - 1, 1, "end")


def moe_phase(nc, d):
    P, TB = 128, 4
    NE, HID = 8, 170
    REST = HID - P
    PER = P // REST
    NM = NE + -(-NE // PER)
    NTI = 6
    NW = 2 * NM * P + NE
    EPS = 1e-6
    THIRD = 8
    NCH = 22

    x2r = d["x2"].rearrange("b t c -> (b t) c")
    h2r = d["h2"].rearrange("b t c -> (b t) c")
    outr = d["out"].rearrange("b t c -> (b t) c")
    with ExitStack() as ctx:
        def sb(n, s, t=F32):
            return ctx.enter_context(nc.sbuf_tensor("mo_" + n, s, t))

        def sem(n):
            return ctx.enter_context(nc.semaphore("mo_" + n))

        ident = sb("ident", [P, P])
        rank = sb("rank", [P, TB * NE])
        half_neg = sb("half_neg", [P, TB])
        eps = sb("eps", [P, TB])
        ln2 = sb("ln2", [P, 1])
        wf = sb("wf", [P, NW])
        w_part2 = sb("w_part2", [C, NW], BF16)
        w12 = sb("w12", [P, NW], BF16)
        w31 = sb("w31", [P, NW], BF16)
        w2_main = sb("w2_main", [P, NE, C])
        w2_rest = sb("w2_rest", [P, NM - NE, PER * C])
        x2 = [sb(f"x2{k}", [P, TB, C]) for k in range(2)]
        h2 = [sb(f"h2{k}", [P, TB, C]) for k in range(2)]
        squares = sb("squares", [P, TB, C])
        ssum = sb("ssum", [P, TB])
        mean = sb("mean", [P, TB])
        rstd = sb("rstd", [P, TB])
        fd = sb("fd", [P, TB, 2, C])
        left = sb("left", [P, 512])
        f1 = [sb(f"f1{k}", [P, 512], BF16) for k in range(2)]
        f2 = [sb(f"f2{k}", [P, 512], BF16) for k in range(2)]
        f13 = [sb(f"f13{k}", [P, 512], BF16) for k in range(2)]
        res = [sb(f"res{k}", [P, TB, C]) for k in range(2)]
        S = [sb(f"S{k}", [P, 512]) for k in range(2)]
        hh = [sb(f"hh{k}", [P, NM, 512]) for k in range(2)]
        weighted = sb("weighted", [P, NE, C])
        summed = sb("summed", [P, TB, C])
        y = [sb(f"y{k}", [P, TB, C]) for k in range(2)]
        top = sb("top", [P, TB])
        lg = sb("lg", [P, TB, NE])
        ex = sb("ex", [P, TB, NE])
        pr = sb("pr", [P, TB, NE])
        eq = sb("eq", [P, TB, NE])
        m1 = sb("m1", [P, TB, NE])
        m2 = sb("m2", [P, TB, NE])
        wt = sb("wt", [P, TB, NE])
        H1 = [ctx.enter_context(nc.psum_tensor(f"mo_H1{k}", [P, 512], F32)) for k in range(2)]
        H3 = [ctx.enter_context(nc.psum_tensor(f"mo_H3{k}", [P, 512], F32)) for k in range(2)]
        OUT = [ctx.enter_context(nc.psum_tensor(f"mo_OUT{k}", [P, 512], F32)) for k in range(2)]
        TP = ctx.enter_context(nc.psum_tensor("mo_TP", [P, 512], F32))
        LG = ctx.enter_context(nc.psum_tensor("mo_LG", [P, 512], F32))

        loaded = sem("loaded")
        x_in = [sem(f"x_in{k}") for k in range(2)]
        stored = [sem(f"stored{k}") for k in range(2)]
        su_dve, su_act = sem("su_dve"), sem("su_act")
        su_pool = sem("su_pool")
        f_act = sem("f_act")
        f_dve = sem("f_dve")
        f_pool = sem("f_pool")
        tp_w = sem("tp_w")
        lg_w = sem("lg_w")
        ex_w = sem("ex_w")
        r_dve = sem("r_dve")
        h1_w, h3_w = sem("h1_w"), sem("h3_w")
        s_w = sem("s_w")
        hh_w = sem("hh_w")
        o_w = sem("o_w")
        ow_r = sem("ow_r")
        sum_w = sem("sum_w")
        y_w = sem("y_w")
        TP_0, RD_0, FD_0, FP_0, S_0, HH_0, O_0, OW_0, SUM_0, Y_0 = 1, NCH, 2, 5, 2, 2, 8, 2, 1, 4
        nl = 10 * 16

        with nc.Block() as block:
            @block.sync
            def _(sp):
                def load(g, k, rows):
                    for dst, src in ((x2, x2r), (h2, h2r)):
                        sp.dma_start(dst[k][:], src[rows, :].rearrange("(n p) c -> p n c", p=P)).then_inc(x_in[k], 16)

                def load_tail(k, b0):
                    for dst, src in ((x2, "x2"), (h2, "h2")):
                        sp.dma_start(dst[k][:], d[src][b0:b0 + TB, LT - P:LT, :].rearrange("b t c -> t b c")).then_inc(x_in[k], 16)

                def free(g):
                    sp.wait_ge(f_pool, 5 * g + FP_0 - 5)

                def store(g, k, rows):
                    sp.wait_ge(y_w, TB * g + TB + Y_0)
                    sp.dma_start(outr[rows, :].rearrange("(n p) c -> p n c", p=P), y[k][:]).then_inc(stored[k], 16)

                def store_tail(g, k, b0):
                    n = L - (LT - P)
                    sp.wait_ge(y_w, TB * g + TB + Y_0)
                    sp.dma_start(d["out"][b0:b0 + TB, LT - P:L, :].rearrange("b t c -> t b c"), y[k][0:n]).then_inc(stored[k], 16)

                def rows(b, j, stride):
                    return bass.ds(b * stride + j * 512, 512)

                load(0, 0, rows(0, 0, LT))
                sp.dma_start(ident[:], d["ident"]).then_inc(loaded, 16)
                sp.dma_start(rank[:], d["expert_rank"]).then_inc(loaded, 16)
                for a in (0, C):
                    sp.dma_start(wf[a:a + C, 0:2 * NM * P], d["w13_columns"]).then_inc(loaded, 16)
                    sp.dma_start(wf[a:a + C, 2 * NM * P:NW], d["router_columns"]).then_inc(loaded, 16)
                    sp.dma_start(ln2[a:a + C, :], d["L0_ffn_ln2_w"].rearrange("(c a) -> c a", a=1)).then_inc(loaded, 16)
                sp.dma_start(w2_main[:], d["w2_main"]).then_inc(loaded, 16)
                sp.dma_start(w2_rest[:], d["w2_rest"]).then_inc(loaded, 16)
                load(1, 1, rows(0, 1, LT))

                def image(b, first, last):
                    for j in range(NTI):
                        g = NTI * b + j
                        free(g + 2)
                        if last and j >= NTI - 2:
                            load_tail(j % 2, TB * (j % 2))
                        else:
                            load(g + 2, j % 2, rows(b, j + 2, LT) if j < NTI - 2 else rows(b + 1, j + 2 - NTI, LT))
                        if not (first and j == 0):
                            store(g - 1, (j + 1) % 2, rows(b, j - 1, L) if j > 0 else rows(b - 1, NTI - 1, L))
                image(0, True, False)
                with sp.Fori(1, B - 1) as b:
                    image(b, False, False)
                image(B - 1, False, True)
                store(NTI * B - 1, 1, rows(B - 1, NTI - 1, L))
                store_tail(NTI * B, 0, 0)
                store_tail(NTI * B + 1, 1, TB)
                for k in range(2):
                    sp.wait_ge(stored[k], 16 + 16 * (NTI * B + 2) // 2)

            @block.tensor
            def _(pe):
                pe.wait_ge(loaded, nl)

                def turn(g, k):
                    pe.wait_ge(f_pool, 5 * g + 3 + FP_0)
                    pe.wait_ge(f_dve, 2 * g + FD_0)
                    for n in range(TB):
                        mm = pe.transpose(TP[:, n * P:(n + 1) * P], fd[:, n].rearrange("p a c -> p (a c)"), ident[:])
                    mm.then_inc(tp_w, 1)

                def route(g, k):
                    pe.wait_ge(f_act, 4 * g + 4)
                    pe.wait_ge(f_pool, 5 * g + 4 + FP_0)
                    pe.wait_ge(r_dve, NCH * (g - 1) + 2 + RD_0)
                    for n in range(TB):
                        for a, (f, w) in enumerate(((f1, w12), (f2, w12), (f13, w31))):
                            mm = pe.matmul(LG[:, n * NE:(n + 1) * NE], f[k][:, n * P:(n + 1) * P], w[:, 2 * NM * P:NW],
                                           start=a == 0, stop=a == 2)
                    mm.then_inc(lg_w, 1)

                def hidden(g, k, m):
                    s = NM * g + m
                    i = (k + m) % 2
                    pe.wait_ge(s_w, s + 1 - 2 + S_0)
                    for a, (f, w) in enumerate(((f1, w12), (f2, w12), (f13, w31))):
                        mm = pe.matmul(H1[i][:], w[:, m * P:(m + 1) * P], f[k][:], start=a == 0, stop=a == 2)
                    mm.then_inc(h1_w, 1)
                    pe.wait_ge(hh_w, s + 1 - 2 + HH_0)
                    for a, (f, w) in enumerate(((f1, w12), (f2, w12), (f13, w31))):
                        mm = pe.matmul(H3[i][:], w[:, (NM + m) * P:(NM + m + 1) * P], f[k][:], start=a == 0, stop=a == 2)
                    mm.then_inc(h3_w, 1)

                def experts(g, k, n):
                    q = TB * g + n
                    if n == 0:
                        pe.wait_ge(hh_w, NM * g + NM + HH_0)
                    pe.wait_ge(ow_r, q + 1 - 2 + OW_0)
                    dst = OUT[n % 2]
                    for r in range(NM - NE):
                        w = min(PER, NE - PER * r) * C
                        pe.matmul(dst[:, PER * C * r:PER * C * r + w], hh[k][:, NE + r, n * P:(n + 1) * P], w2_rest[:, r, 0:w],
                                  start=r == 0, stop=False, skip_group_check=True)
                    for e in range(NE):
                        mm = pe.matmul(dst[:, C * e:C * e + C], hh[k][:, e, n * P:(n + 1) * P], w2_main[:, e, :],
                                       start=False, stop=True, skip_group_check=True)
                    mm.then_inc(o_w, 1)

                def period(g, k, first, last):
                    for m in range(NM):
                        hidden(g, k, m)
                        if not first and m in (2, 4, 6, 8):
                            experts(g - 1, 1 - k, (m - 2) // 2)
                        if not last and m == 5:
                            turn(g + 1, 1 - k)
                        if not last and m == 10:
                            route(g + 1, 1 - k)

                turn(0, 0)
                pe.wait_ge(su_dve, 4)
                route(0, 0)
                for j in range(NTI):
                    period(j, j % 2, j == 0, False)
                with pe.Fori(1, B) as b:
                    for j in range(NTI):
                        period(NTI * b + j, j % 2, False, False)
                period(NTI * B, 0, False, False)
                period(NTI * B + 1, 1, False, True)
                for n in range(TB):
                    experts(NTI * B + 1, 1, n)

            @block.scalar
            def _(act):
                def square(g, k, pair):
                    act.wait_ge(x_in[k], 32 * pair + 32)
                    act.wait_ge(f_dve, 2 * g + 1 - 2 + FD_0)
                    act.activation(squares[:], x2[k][:], ACT.Square, scale=C ** -0.5).then_inc(f_act, 1)

                def first_part(g, k):
                    act.wait_ge(tp_w, g + 1 + TP_0)
                    act.activation(f1[k][:], TP[:], ACT.Copy).then_inc(f_act, 1)
                    act.wait_ge(f_act, 4 * g + 2)
                    act.activation(f13[k][0:C], f1[k][0:C], ACT.Copy).then_inc(f_act, 1)

                def second_part(g, k):
                    act.wait_ge(f_dve, 2 * g + 2 + FD_0)
                    act.activation(f2[k][:], left[:], ACT.Copy).then_inc(f_act, 1)

                def exponential(g):
                    act.wait_ge(r_dve, NCH * g + 2 + RD_0)
                    act.activation(ex[:], lg[:], ACT.Exp).then_inc(ex_w, 1)

                def silu(g, k, m):
                    s = NM * g + m
                    i = (k + m) % 2
                    act.wait_ge(h1_w, s + 1)
                    act.wait_ge(hh_w, s + 1 - 2 + HH_0)
                    act.activation(S[i][:], H1[i][:], ACT.Silu).then_inc(s_w, 1)

                def period(g, k, pair, last):
                    for m in range(NM):
                        silu(g, k, m)
                        if m == 0:
                            exponential(g)
                        if not last and m == 1:
                            square(g + 1, 1 - k, pair)
                        if not last and m == 6:
                            first_part(g + 1, 1 - k)
                        if not last and m == 7:
                            second_part(g + 1, 1 - k)

                square(0, 0, 0)
                first_part(0, 0)
                second_part(0, 0)
                act.wait_ge(su_dve, 1)
                act.activation(w12[0:C], wf[0:C], ACT.Copy).then_inc(su_act, 1)
                act.activation(w31[C:P], wf[C:P], ACT.Copy).then_inc(su_act, 1)
                act.wait_ge(su_dve, 3)
                act.activation(w12[C:P], wf[C:P], ACT.Copy).then_inc(su_act, 1)
                act.activation(w_part2[:], wf[0:C], ACT.Copy).then_inc(su_act, 1)
                act.wait_ge(su_dve, 4)
                with act.Fori(0, B) as b:
                    for j in range(NTI):
                        period(NTI * b + j, j % 2, (NTI // 2) * b + (j + 1) // 2, False)
                period(NTI * B, 0, NTI * B // 2, False)
                period(NTI * B + 1, 1, None, True)

            @block.vector
            def _(dve):
                for s_, n_ in ((tp_w, TP_0), (r_dve, RD_0), (f_dve, FD_0), (f_pool, FP_0), (s_w, S_0), (hh_w, HH_0), (o_w, O_0),
                               (ow_r, OW_0), (sum_w, SUM_0), (y_w, Y_0), (stored[0], 16), (stored[1], 16)):
                    dve.sem_inc(s_, n_)
                def sum_squares(g):
                    dve.wait_ge(f_act, 4 * g + 1)
                    dve.wait_ge(f_pool, 5 * g + 1 - 5 + FP_0)
                    dve.tensor_reduce(ssum[:], squares[:], AX.X, ALU.add).then_inc(f_dve, 1)

                def leave(g, k):
                    dve.wait_ge(f_act, 4 * g + 2)
                    dve.wait_ge(f_pool, 5 * g + 4 - 5 + FP_0)
                    dve.tensor_tensor(left[:], TP[:], f1[k][:], ALU.subtract).then_inc(f_dve, 1)

                def routing(g, steps):
                    r = NCH * g + RD_0

                    def wide(a):
                        return a[:].unsqueeze(2).to_broadcast([P, TB, NE])
                    logits = LG[:, 0:TB * NE].rearrange("p (n e) -> p n e", e=NE)
                    rk = rank[:].rearrange("p (n e) -> p n e", e=NE)
                    for i in steps:
                        dve.wait_ge(r_dve, r + i)
                        if i == 0:
                            dve.wait_ge(lg_w, g + 1)
                            op = dve.tensor_reduce(top[:], logits, AX.X, ALU.max)
                        elif i == 1:
                            op = dve.tensor_tensor(lg[:], logits, wide(top), ALU.subtract)
                        elif i == 2:
                            dve.wait_ge(ex_w, g + 1)
                            op = dve.tensor_reduce(top[:], ex[:], AX.X, ALU.add)
                        elif i == 3:
                            op = dve.reciprocal(top[:], top[:])
                        elif i == 4:
                            op = dve.tensor_tensor(pr[:], ex[:], wide(top), ALU.mult)
                        elif i == 5:
                            op = dve.tensor_reduce(top[:], pr[:], AX.X, ALU.max)
                        elif i == 6:
                            op = dve.tensor_tensor(eq[:], pr[:], wide(top), ALU.is_equal)
                        elif i == 7:
                            op = dve.tensor_tensor(eq[:], eq[:], rk, ALU.mult)
                        elif i == 8:
                            op = dve.tensor_reduce(top[:], eq[:], AX.X, ALU.max)
                        elif i == 9:
                            op = dve.tensor_tensor(m1[:], eq[:], wide(top), ALU.is_equal)
                        elif i == 10:
                            op = dve.scalar_tensor_tensor(ex[:], m1[:], -2.0, pr[:], ALU.mult, ALU.add)
                        elif i == 11:
                            op = dve.tensor_reduce(top[:], ex[:], AX.X, ALU.max)
                        elif i == 12:
                            op = dve.tensor_tensor(eq[:], ex[:], wide(top), ALU.is_equal)
                        elif i == 13:
                            op = dve.tensor_tensor(eq[:], eq[:], rk, ALU.mult)
                        elif i == 14:
                            op = dve.tensor_reduce(top[:], eq[:], AX.X, ALU.max)
                        elif i == 15:
                            op = dve.tensor_tensor(m2[:], eq[:], wide(top), ALU.is_equal)
                        elif i == 16:
                            op = dve.tensor_tensor(m1[:], m1[:], m2[:], ALU.add)
                        elif i == 17:
                            op = dve.tensor_tensor(pr[:], pr[:], m1[:], ALU.mult)
                        elif i == 18:
                            op = dve.tensor_reduce(top[:], pr[:], AX.X, ALU.add)
                        elif i == 19:
                            op = dve.tensor_scalar(top[:], top[:], 1e-9, None, ALU.add)
                        elif i == 20:
                            op = dve.reciprocal(top[:], top[:])
                        elif i == 21:
                            dve.wait_ge(ow_r, TB * g + OW_0)
                            op = dve.tensor_tensor(wt[:], pr[:], wide(top), ALU.mult)
                        op.then_inc(r_dve, 1)

                def product(g, k, m):
                    s = NM * g + m
                    i = (k + m) % 2
                    if m == 0:
                        dve.wait_ge(o_w, TB * (g - 1) + O_0)
                    dve.wait_ge(s_w, s + 1 + S_0)
                    dve.wait_ge(h3_w, s + 1)
                    dve.tensor_tensor(hh[k][:, m, :], S[i][:], H3[i][:], ALU.mult).then_inc(hh_w, 1)

                def weigh(g, n):
                    q = TB * g + n
                    dve.wait_ge(o_w, q + 1 + O_0)
                    dve.wait_ge(sum_w, q + SUM_0)
                    if n == 0:
                        dve.wait_ge(r_dve, NCH * g + NCH + RD_0)
                    dve.tensor_tensor(weighted[:], OUT[n % 2][:].rearrange("p (e c) -> p e c", c=C),
                                      wt[:, n, :].unsqueeze(2).to_broadcast([P, NE, C]), ALU.mult).then_inc(ow_r, 1)

                def add_experts(g, n):
                    q = TB * g + n
                    dve.wait_ge(ow_r, q + 1 + OW_0)
                    dve.wait_ge(y_w, q + 1 - 4 + Y_0)
                    dve.tensor_reduce(summed[:, n, :], weighted[:].rearrange("p e c -> p c e"), AX.X, ALU.add).then_inc(sum_w, 1)

                def period(g, k, first, last):
                    for m in range(NM):
                        if m == 0:
                            routing(g, range(0, 2))
                        product(g, k, m)
                        if not first:
                            if m in (3, 5, 7, 9):
                                weigh(g - 1, (m - 3) // 2)
                            if m in (4, 6, 8, 10):
                                add_experts(g - 1, (m - 4) // 2)
                        if m >= 3:
                            routing(g, range(2 + (NCH - 2) * (m - 3) // 8, 2 + (NCH - 2) * (m - 2) // 8))
                        if not last and m == 2:
                            sum_squares(g + 1)
                        if not last and m == 6:
                            leave(g + 1, 1 - k)

                sum_squares(0)
                leave(0, 0)
                dve.wait_ge(loaded, nl)
                dve.tensor_scalar(wf[:], wf[:], ln2[:], None, ALU.mult).then_inc(su_dve, 1)
                dve.wait_ge(su_dve, 1)
                dve.wait_ge(su_act, 2)
                dve.tensor_tensor(wf[0:C], wf[0:C], w12[0:C], ALU.subtract).then_inc(su_dve, 1)
                dve.tensor_tensor(wf[C:P], wf[C:P], w31[C:P], ALU.subtract).then_inc(su_dve, 1)
                dve.wait_ge(su_dve, 3)
                dve.wait_ge(su_act, 4)
                dve.tensor_tensor(w31[0:C], wf[0:C], w_part2[:], ALU.subtract).then_inc(su_dve, 1)
                for j in range(NTI):
                    period(j, j % 2, j == 0, False)
                with dve.Fori(1, B) as b:
                    for j in range(NTI):
                        period(NTI * b + j, j % 2, False, False)
                period(NTI * B, 0, False, False)
                period(NTI * B + 1, 1, False, True)
                for n in range(TB):
                    weigh(NTI * B + 1, n)
                    add_experts(NTI * B + 1, n)

            @block.gpsimd
            def _(pool):
                pool.memset(half_neg[:], -0.5)
                pool.memset(eps[:], EPS)
                pool.drain().then_inc(su_pool, 1)
                pool.wait_ge(su_pool, 1)
                pool.wait_ge(f_pool, FP_0)

                def normed(g, k):
                    r = 5 * g + FP_0
                    pool.wait_ge(f_dve, 2 * g + 1 + FD_0)
                    pool.wait_ge(f_pool, r)
                    pool.tensor_tensor(mean[:], ssum[:], eps[:], ALU.add).then_inc(f_pool, 1)
                    pool.wait_ge(f_pool, r + 1)
                    pool.tensor_tensor(rstd[:], mean[:], half_neg[:], ALU.pow).then_inc(f_pool, 1)
                    pool.wait_ge(f_pool, r + 2)
                    pool.wait_ge(tp_w, g + TP_0)
                    pool.tensor_tensor(fd[:], x2[k][:].unsqueeze(2).to_broadcast([P, TB, 2, C]),
                                       rstd[:].unsqueeze(2).unsqueeze(3).to_broadcast([P, TB, 2, C]), ALU.mult).then_inc(f_pool, 1)

                def third_part(g, k, outputs):
                    pool.wait_ge(f_act, 4 * g + 4)
                    pool.wait_ge(y_w, TB * (g - 2) + outputs + Y_0)
                    pool.tensor_tensor(f13[k][C:P], left[C:P], f2[k][C:P], ALU.subtract).then_inc(f_pool, 1)
                    pool.wait_ge(f_pool, 5 * g + 4 + FP_0)

                def residual(g, k):
                    pool.wait_ge(y_w, TB * (g - 1) + Y_0)
                    pool.tensor_tensor(res[k][:], x2[k][:], h2[k][:], ALU.add).then_inc(f_pool, 1)

                def output(g, k, n, pair):
                    q = TB * g + n
                    pool.wait_ge(sum_w, q + 1 + SUM_0)
                    if n == 0:
                        pool.wait_ge(stored[k], 16 * pair + 16)
                        pool.wait_ge(f_pool, 5 * g + 5 + FP_0)
                    pool.tensor_tensor(y[k][:, n, :], summed[:, n, :], res[k][:, n, :], ALU.add).then_inc(y_w, 1)

                THIRD_OUTPUTS = sum(n < THIRD for n in (5, 7, 9))

                def period(g, k, first, last, pair):
                    for m in range(NM):
                        if not last and m == 2:
                            normed(g + 1, 1 - k)
                        if not last and m == THIRD:
                            third_part(g + 1, 1 - k, 0 if first else THIRD_OUTPUTS)
                        if not first and m in (5, 7, 9):
                            output(g - 1, 1 - k, (m - 5) // 2, pair)
                    if not first:
                        output(g - 1, 1 - k, TB - 1, pair)
                    if not last:
                        residual(g + 1, 1 - k)

                normed(0, 0)
                third_part(0, 0, TB)
                residual(0, 0)
                for j in range(NTI):
                    period(j, j % 2, j == 0, False, (j - 1) // 2)
                with pool.Fori(1, B) as b:
                    for j in range(NTI):
                        period(NTI * b + j, j % 2, False, False, (NTI // 2) * b + (j - 1) // 2)
                period(NTI * B, 0, False, False, NTI * B // 2 - 1)
                period(NTI * B + 1, 1, False, True, NTI * B // 2)
                for n in range(TB):
                    output(NTI * B + 1, 1, n, NTI * B // 2)


def shape_constants():
    import numpy as np
    P, S, D, NE = 128, 16, 16, 8
    bf16 = mybir.dt.np(BF16)
    r = np.arange(P)
    selectors = np.zeros((6 * S, 2 * S, P), np.float32)
    for k in range(6 * S):
        selectors[k, k % (2 * S)] = 1
    part_signs = np.zeros((6 * S, 2), np.float32)
    part_signs[2 * S:, 0] = -1
    part_signs[4 * S:, 1] = -1
    sum_selector = np.zeros((P, P), np.float32)
    sum_selector[32 * (r // 32) + D, r] = 1
    inv_freq = 1.0 / 10000.0 ** (np.arange(0, D, 2, dtype=np.float32) / D)
    freqs = np.outer(np.arange(LT, dtype=np.float32), inv_freq)
    emb = np.concatenate([freqs, freqs], axis=-1).astype(np.float32)
    cos, sin = np.cos(emb).T, np.sin(emb).T.copy()
    sin[:D // 2] *= -1
    return {
        "ident": np.eye(P, dtype=np.float32), "ident_bf16": np.eye(P).astype(bf16), "selectors": selectors.astype(bf16),
        "part_signs": part_signs, "sum_selector": sum_selector,
        "mask_queries": np.where(r[None, :] > r[:, None], -1e30, 0).astype(bf16),
        "mask_keys": np.where(r[:, None] > r[None, :], -1e30, 0).astype(bf16),
        "rope_cos": np.tile(cos, (6, 1)), "rope_sin": np.tile(sin, (6, 1)),
        "expert_rank": np.tile(np.arange(NE, 0, -1, dtype=np.float32), (P, 4)),
    }


def laid_out(inputs):
    import numpy as np
    P = 128
    d = {n: np.asarray(a) for n, a in inputs.items()}
    pairs = [(0, 3), (1, 4), (2, 5), (6, 7), (8, None)]
    w1, w2 = d.pop("L0_tok_W1").reshape(C, 9, C), d.pop("L0_tok_W2").reshape(C, C, 9)
    w3, b2 = d.pop("L0_tok_W3").reshape(C, 9, C), d.pop("L0_tok_b2").reshape(C, 9)
    d["tok_w1_pairs"] = np.zeros((2, C, len(pairs), 2, C), w1.dtype)
    d["tok_w2_pairs"] = np.zeros((2, C, len(pairs), 2, C), w2.dtype)
    d["tok_w3_pairs"] = np.zeros((2, C, len(pairs), C), w3.dtype)
    d["tok_b2_pairs"] = np.zeros((2, C, len(pairs)), b2.dtype)
    for p, taps in enumerate(pairs):
        for part, tap in enumerate(taps):
            if tap is not None:
                d["tok_w1_pairs"][part, :, p] = w1[:, tap, None]
                d["tok_w2_pairs"][:, :, p, part] = w2[None, :, :, tap]
                d["tok_w3_pairs"][part, :, p] = w3[:, tap]
                d["tok_b2_pairs"][part, :, p] = b2[:, tap]
    for n in ("w1", "w2", "w3", "b2"):
        a = d[f"tok_{n}_pairs"]
        d[f"tok_{n}_pairs"] = a.reshape((P, len(pairs)) + ((-1,) if a.ndim > 3 else ()))
    d["L0_attn_b_in_w"] = d["L0_attn_b_in_w"][:, ::-1]
    d["L0_attn_b_out_w"] = d["L0_attn_b_out_w"][::-1]
    for n in ("wq", "wk"):
        w = d["L0_ffn_" + n]
        d[n + "_rotated"] = w.reshape(-1, 2, 8, C)[:, ::-1].reshape(w.shape)
    w1, w2, w3 = (d.pop("L0_ffn_" + n) for n in ("w1", "w2", "w3"))
    ne, hid = w1.shape[:2]
    per = P // (hid - P)
    groups = [range(a, min(a + per, ne)) for a in range(0, ne, per)]
    columns = np.zeros((C, 2, ne + len(groups), P), w1.dtype)
    rest = np.zeros((P, len(groups), per, C), w2.dtype)
    for k, w in enumerate((w1, w3)):
        columns[:, k, :ne] = w[:, :P].transpose(2, 0, 1)
        for r, group in enumerate(groups):
            for a, e in enumerate(group):
                rows = slice(a * (hid - P), (a + 1) * (hid - P))
                columns[:, k, ne + r, rows] = w[e, P:].T
                rest[rows, r, a] = w2[e, :, P:].T
    d["w13_columns"] = columns.reshape(C, -1)
    d["router_columns"] = d.pop("L0_ffn_router_w").T
    d["w2_main"] = w2[:, :, :P].transpose(2, 0, 1)
    d["w2_rest"] = rest.reshape(P, len(groups), per * C)
    return d


def kernel(**inputs):
    import numpy as _np
    import concourse.bacc as _bacc
    from concourse import mybir as _mybir
    from concourse.bass_utils import run_bass_kernel_spmd as _run

    nc = _bacc.Bacc("TRN2", target_bir_lowering=False, num_devices=1)
    arrays, d = {}, {}
    for name, a in {**laid_out(inputs), **shape_constants()}.items():
        a = _np.ascontiguousarray(a)
        arrays[f"in_{name}_dram"] = a
        d[name] = nc.dram_tensor(f"in_{name}_dram", a.shape, _mybir.dt.from_np(a.dtype), kind="ExternalInput").ap()
    for name in ("h1", "h2", "x2"):
        d[name] = nc.dram_tensor(f"scratch_{name}", (B, LT, C), F32, kind="Internal").ap()
    d["out"] = nc.dram_tensor("out_0_dram", (B, L, C), F32, kind="ExternalOutput").ap()
    tok_phase(nc, d)
    mamba_phase(nc, d)
    attn_phase(nc, d)
    moe_phase(nc, d)
    r = _run(nc, [arrays], core_ids=[0])
    return r.results[0]["out_0_dram"]
```
